# Optimizing a Trainium2 kernel written in Bass

```python
import numpy as np
import jax
import jax.numpy as jnp

def _softmax(x, axis=-1):
    return jax.nn.softmax(x, axis=axis)

def _gelu(x):
    return jax.nn.gelu(x, approximate=True)

def _silu(x):
    return jax.nn.silu(x)

def _sigmoid(x):
    return jax.nn.sigmoid(x)

def _layernorm(x, axis=-1, eps=1e-05):
    m = jnp.mean(x, axis=axis, keepdims=True)
    v = jnp.var(x, axis=axis, keepdims=True)
    return (x - m) / jnp.sqrt(v + eps)

def _scatter_add(tgt, idx, src, axis=0):
    return tgt.at[idx].add(src)

def _segment_sum(src, seg, n):
    return jax.ops.segment_sum(src, seg, n)
kernel_name = 'mk_prb_d2_jaxref_r8_3d2618'

def setup_inputs(seed: int=0):
    np.random.seed(seed)
    _w = jnp.asarray

    def _L0_attn_setup():
        import jax, jax.numpy as jnp
        import numpy as np
        B, S, H = (8, 256, 128)
        CHUNK = 64
        INTER = 256
        BASE_LR = 0.01
        MAX_GRAD_NORM = 1.0
        EPS = 1e-06

        def rmsnorm(x, w):
            return x * jax.lax.rsqrt(jnp.mean(x * x, axis=-1, keepdims=True) + EPS) * w

        def mem_fwd(params, x):
            w0, w1, ln = params
            h = jax.nn.silu(x @ w0.T)
            y = h @ w1.T
            return x + rmsnorm(y, ln)

        def forward(x, wq_w, wk_w, wv_w, q_norm_w, k_norm_w, alpha_w, theta_w, eta_w, mem_w0, mem_w1, mem_ln_w):
            Bx, Sx, Hx = x.shape
            NC = Sx // CHUNK
            xc = x.reshape(Bx, NC, CHUNK, Hx)
            xf = xc.reshape(Bx, NC, CHUNK * Hx)
            alpha = jax.nn.sigmoid(jnp.mean(xf @ alpha_w.T, axis=0))
            theta = jax.nn.sigmoid(xf @ theta_w.T) * BASE_LR
            eta = jax.nn.sigmoid(jnp.mean(xf @ eta_w.T, axis=0))
            beta = 1.0 - alpha
            k = rmsnorm(jax.nn.silu(xc @ wk_w.T), k_norm_w)
            v = jax.nn.silu(xc @ wv_w.T)
            mem0 = (mem_w0, mem_w1, mem_ln_w)
            surp0 = jax.tree_util.tree_map(jnp.zeros_like, mem0)

            def step(carry, inp):
                mem, surp = carry
                k_c, v_c, th_c, eta_c, beta_c = inp

                def loss_fn(p):
                    pred = mem_fwd(p, k_c)
                    return jnp.mean((v_c - pred) ** 2 * th_c[:, :, None])
                grads = jax.grad(loss_fn)(mem)
                total = jnp.sqrt(sum((jnp.sum(g * g) for g in grads)))
                clip = jax.lax.stop_gradient(jnp.minimum(MAX_GRAD_NORM / (total + 1e-06), 1.0))
                new_surp = tuple((eta_c * s_ - g * clip for s_, g in zip(surp, grads)))
                new_mem = tuple((beta_c * m + ns for m, ns in zip(mem, new_surp)))
                return ((new_mem, new_surp), None)
            xs = (jnp.swapaxes(k, 0, 1), jnp.swapaxes(v, 0, 1), jnp.swapaxes(theta, 0, 1), eta, beta)
            (mem_f, _), _ = jax.lax.scan(step, (mem0, surp0), xs)
            q = rmsnorm(jax.nn.silu(x @ wq_w.T), q_norm_w)
            return mem_fwd(mem_f, q)
        key = jax.random.key(seed)
        ks = jax.random.split(key, 9)
        s = 0.02
        return {'x': jax.random.normal(ks[0], (B, S, H), jnp.float32), 'wq_w': jax.random.normal(ks[1], (H, H), jnp.float32) * s, 'wk_w': jax.random.normal(ks[2], (H, H), jnp.float32) * s, 'wv_w': jax.random.normal(ks[3], (H, H), jnp.float32) * s, 'q_norm_w': jnp.ones((H,), jnp.float32), 'k_norm_w': jnp.ones((H,), jnp.float32), 'alpha_w': jax.random.normal(ks[4], (1, CHUNK * H), jnp.float32) * s, 'theta_w': jax.random.normal(ks[5], (1, CHUNK * H), jnp.float32) * s, 'eta_w': jax.random.normal(ks[6], (1, CHUNK * H), jnp.float32) * s, 'mem_w0': jax.random.normal(ks[7], (INTER, H), jnp.float32) * s, 'mem_w1': jax.random.normal(ks[8], (H, INTER), jnp.float32) * s, 'mem_ln_w': jnp.ones((H,), jnp.float32)}
    _L0_attn_in = _L0_attn_setup()

    def _L0_ffn_setup():
        import jax, jax.numpy as jnp
        import numpy as np
        DIM, HEADS, EXPERTS, DFF = (128, 16, 8, 512)
        EPS = 1e-05

        def layernorm(x, g, b):
            mu = jnp.mean(x, -1, keepdims=True)
            var = jnp.mean(jnp.square(x - mu), -1, keepdims=True)
            return (x - mu) * jax.lax.rsqrt(var + EPS) * g + b
        key = jax.random.key(seed)
        ks = jax.random.split(key, 12)
        s = lambda d: 1.0 / np.sqrt(d)
        return {'x': jax.random.normal(ks[0], (2, 256, DIM), jnp.float32), 'conv_w': jax.random.normal(ks[1], (DIM, DIM, 3), jnp.float32) * s(DIM * 3), 'conv_b': jnp.zeros((DIM,), jnp.float32), 'wqkv': jax.random.normal(ks[2], (3 * DIM, DIM), jnp.float32) * s(DIM), 'bqkv': jnp.zeros((3 * DIM,), jnp.float32), 'wo': jax.random.normal(ks[3], (DIM, DIM), jnp.float32) * s(DIM), 'bo': jnp.zeros((DIM,), jnp.float32), 'ln1_g': jnp.ones((DIM,), jnp.float32), 'ln1_b': jnp.zeros((DIM,), jnp.float32), 'gate_w': jax.random.normal(ks[4], (DIM, EXPERTS), jnp.float32) * s(DIM), 'gate_b': jnp.zeros((EXPERTS,), jnp.float32), 'w1': jax.random.normal(ks[5], (EXPERTS, DIM, DFF), jnp.float32) * s(DIM), 'b1': jnp.zeros((EXPERTS, DFF), jnp.float32), 'w2': jax.random.normal(ks[6], (EXPERTS, DFF, DIM), jnp.float32) * s(DFF), 'b2': jnp.zeros((EXPERTS, DIM), jnp.float32), 'ln2_g': jnp.ones((DIM,), jnp.float32), 'ln2_b': jnp.zeros((DIM,), jnp.float32)}
    _L0_ffn_in = _L0_ffn_setup()

    def _L1_attn_setup():
        import jax, jax.numpy as jnp
        import numpy as np
        import math
        D_MODEL = 128
        NUM_HEADS = 16
        HEAD_DIM = D_MODEL // NUM_HEADS
        B, S = (2, 256)

        def _causal_attn(q, k, v):
            scale = 1.0 / math.sqrt(q.shape[-1])
            scores = jnp.einsum('bthd,bshd->bhts', q, k) * scale
            t = q.shape[1]
            mask = jnp.tril(jnp.ones((t, t), dtype=bool))
            scores = jnp.where(mask, scores, -jnp.inf)
            attn = jax.nn.softmax(scores, axis=-1)
            return jnp.einsum('bhts,bshd->bthd', attn, v)
        key = jax.random.key(seed)
        ks = jax.random.split(key, 7)
        sc = 0.02
        return {'x': jax.random.normal(ks[0], (B, S, D_MODEL), dtype=jnp.float32), 'Wqkv_w': jax.random.normal(ks[1], (3 * D_MODEL, D_MODEL), dtype=jnp.float32) * sc, 'Wqkv_b': jnp.zeros((3 * D_MODEL,), dtype=jnp.float32), 'conv_w': jax.random.normal(ks[2], (D_MODEL, D_MODEL, 3), dtype=jnp.float32) * sc, 'conv_b': jnp.zeros((D_MODEL,), dtype=jnp.float32), 'out_w': jax.random.normal(ks[3], (D_MODEL, D_MODEL), dtype=jnp.float32) * sc, 'out_b': jnp.zeros((D_MODEL,), dtype=jnp.float32)}
    _L1_attn_in = _L1_attn_setup()

    def _L1_ffn_setup():
        import jax, jax.numpy as jnp
        import numpy as np
        TOP_K = 8
        NUM_EXPERTS = 32
        CAPACITY = 128
        key = jax.random.key(seed)
        k1, k2, k3, k4 = jax.random.split(key, 4)
        B, S, H, E, F = (2, 128, 128, NUM_EXPERTS, 96)
        return {'hidden_states': jax.random.normal(k1, (B, S, H), dtype=jnp.float32), 'gate_weight': jax.random.normal(k2, (E, H), dtype=jnp.float32) * 0.02, 'gate_up_proj': jax.random.normal(k3, (E, 2 * F, H), dtype=jnp.float32) * 0.02, 'down_proj': jax.random.normal(k4, (E, H, F), dtype=jnp.float32) * 0.02}
    _L1_ffn_in = _L1_ffn_setup()
    _d = {'L0_attn_x': _L0_attn_in['x'], 'L0_attn_wq_w': _L0_attn_in['wq_w'], 'L0_attn_wk_w': _L0_attn_in['wk_w'], 'L0_attn_wv_w': _L0_attn_in['wv_w'], 'L0_attn_q_norm_w': _L0_attn_in['q_norm_w'], 'L0_attn_k_norm_w': _L0_attn_in['k_norm_w'], 'L0_attn_alpha_w': _L0_attn_in['alpha_w'], 'L0_attn_theta_w': _L0_attn_in['theta_w'], 'L0_attn_eta_w': _L0_attn_in['eta_w'], 'L0_attn_mem_w0': _L0_attn_in['mem_w0'], 'L0_attn_mem_w1': _L0_attn_in['mem_w1'], 'L0_attn_mem_ln_w': _L0_attn_in['mem_ln_w'], 'L0_ffn_conv_w': _L0_ffn_in['conv_w'], 'L0_ffn_conv_b': _L0_ffn_in['conv_b'], 'L0_ffn_wqkv': _L0_ffn_in['wqkv'], 'L0_ffn_bqkv': _L0_ffn_in['bqkv'], 'L0_ffn_wo': _L0_ffn_in['wo'], 'L0_ffn_bo': _L0_ffn_in['bo'], 'L0_ffn_ln1_g': _L0_ffn_in['ln1_g'], 'L0_ffn_ln1_b': _L0_ffn_in['ln1_b'], 'L0_ffn_gate_w': _L0_ffn_in['gate_w'], 'L0_ffn_gate_b': _L0_ffn_in['gate_b'], 'L0_ffn_w1': _L0_ffn_in['w1'], 'L0_ffn_b1': _L0_ffn_in['b1'], 'L0_ffn_w2': _L0_ffn_in['w2'], 'L0_ffn_b2': _L0_ffn_in['b2'], 'L0_ffn_ln2_g': _L0_ffn_in['ln2_g'], 'L0_ffn_ln2_b': _L0_ffn_in['ln2_b'], 'L1_attn_Wqkv_w': _L1_attn_in['Wqkv_w'], 'L1_attn_Wqkv_b': _L1_attn_in['Wqkv_b'], 'L1_attn_conv_w': _L1_attn_in['conv_w'], 'L1_attn_conv_b': _L1_attn_in['conv_b'], 'L1_attn_out_w': _L1_attn_in['out_w'], 'L1_attn_out_b': _L1_attn_in['out_b'], 'L1_ffn_gate_weight': _L1_ffn_in['gate_weight'], 'L1_ffn_gate_up_proj': _L1_ffn_in['gate_up_proj'], 'L1_ffn_down_proj': _L1_ffn_in['down_proj']}
    _x0 = _d['L0_attn_x']
    _d['L0_attn_x'] = jax.random.normal(jax.random.fold_in(jax.random.key(seed), 1), (16, 512, 128), dtype=_x0.dtype)
    del _x0
    return _d

def reference(L0_attn_x, L0_attn_wq_w, L0_attn_wk_w, L0_attn_wv_w, L0_attn_q_norm_w, L0_attn_k_norm_w, L0_attn_alpha_w, L0_attn_theta_w, L0_attn_eta_w, L0_attn_mem_w0, L0_attn_mem_w1, L0_attn_mem_ln_w, L0_ffn_conv_w, L0_ffn_conv_b, L0_ffn_wqkv, L0_ffn_bqkv, L0_ffn_wo, L0_ffn_bo, L0_ffn_ln1_g, L0_ffn_ln1_b, L0_ffn_gate_w, L0_ffn_gate_b, L0_ffn_w1, L0_ffn_b1, L0_ffn_w2, L0_ffn_b2, L0_ffn_ln2_g, L0_ffn_ln2_b, L1_attn_Wqkv_w, L1_attn_Wqkv_b, L1_attn_conv_w, L1_attn_conv_b, L1_attn_out_w, L1_attn_out_b, L1_ffn_gate_weight, L1_ffn_gate_up_proj, L1_ffn_down_proj):

    def _L0_attn_ref(x, wq_w, wk_w, wv_w, q_norm_w, k_norm_w, alpha_w, theta_w, eta_w, mem_w0, mem_w1, mem_ln_w):
        import jax, jax.numpy as jnp
        import numpy as np
        B, S, H = (8, 256, 128)
        CHUNK = 64
        INTER = 256
        BASE_LR = 0.01
        MAX_GRAD_NORM = 1.0
        EPS = 1e-06

        def rmsnorm(x, w):
            return x * jax.lax.rsqrt(jnp.mean(x * x, axis=-1, keepdims=True) + EPS) * w

        def mem_fwd(params, x):
            w0, w1, ln = params
            h = jax.nn.silu(x @ w0.T)
            y = h @ w1.T
            return x + rmsnorm(y, ln)

        def forward(x, wq_w, wk_w, wv_w, q_norm_w, k_norm_w, alpha_w, theta_w, eta_w, mem_w0, mem_w1, mem_ln_w):
            Bx, Sx, Hx = x.shape
            NC = Sx // CHUNK
            xc = x.reshape(Bx, NC, CHUNK, Hx)
            xf = xc.reshape(Bx, NC, CHUNK * Hx)
            alpha = jax.nn.sigmoid(jnp.mean(xf @ alpha_w.T, axis=0))
            theta = jax.nn.sigmoid(xf @ theta_w.T) * BASE_LR
            eta = jax.nn.sigmoid(jnp.mean(xf @ eta_w.T, axis=0))
            beta = 1.0 - alpha
            k = rmsnorm(jax.nn.silu(xc @ wk_w.T), k_norm_w)
            v = jax.nn.silu(xc @ wv_w.T)
            mem0 = (mem_w0, mem_w1, mem_ln_w)
            surp0 = jax.tree_util.tree_map(jnp.zeros_like, mem0)

            def step(carry, inp):
                mem, surp = carry
                k_c, v_c, th_c, eta_c, beta_c = inp

                def loss_fn(p):
                    pred = mem_fwd(p, k_c)
                    return jnp.mean((v_c - pred) ** 2 * th_c[:, :, None])
                grads = jax.grad(loss_fn)(mem)
                total = jnp.sqrt(sum((jnp.sum(g * g) for g in grads)))
                clip = jax.lax.stop_gradient(jnp.minimum(MAX_GRAD_NORM / (total + 1e-06), 1.0))
                new_surp = tuple((eta_c * s_ - g * clip for s_, g in zip(surp, grads)))
                new_mem = tuple((beta_c * m + ns for m, ns in zip(mem, new_surp)))
                return ((new_mem, new_surp), None)
            xs = (jnp.swapaxes(k, 0, 1), jnp.swapaxes(v, 0, 1), jnp.swapaxes(theta, 0, 1), eta, beta)
            (mem_f, _), _ = jax.lax.scan(step, (mem0, surp0), xs)
            q = rmsnorm(jax.nn.silu(x @ wq_w.T), q_norm_w)
            return mem_fwd(mem_f, q)
        return forward(x, wq_w, wk_w, wv_w, q_norm_w, k_norm_w, alpha_w, theta_w, eta_w, mem_w0, mem_w1, mem_ln_w)

    def _L0_ffn_ref(x, conv_w, conv_b, wqkv, bqkv, wo, bo, ln1_g, ln1_b, gate_w, gate_b, w1, b1, w2, b2, ln2_g, ln2_b):
        import jax, jax.numpy as jnp
        import numpy as np
        DIM, HEADS, EXPERTS, DFF = (128, 16, 8, 512)
        EPS = 1e-05

        def layernorm(x, g, b):
            mu = jnp.mean(x, -1, keepdims=True)
            var = jnp.mean(jnp.square(x - mu), -1, keepdims=True)
            return (x - mu) * jax.lax.rsqrt(var + EPS) * g + b
        B, S, D = x.shape
        H, dh = (HEADS, D // HEADS)
        xt = jnp.transpose(x, (0, 2, 1))
        xt = jax.lax.conv_general_dilated(xt, conv_w, (1,), [(1, 1)], dimension_numbers=('NCH', 'OIH', 'NCH'))
        x = jnp.transpose(xt + conv_b[None, :, None], (0, 2, 1))
        qkv = x @ wqkv.T + bqkv
        q, k, v = jnp.split(qkv, 3, axis=-1)
        q = q.reshape(B, S, H, dh).transpose(0, 2, 1, 3)
        k = k.reshape(B, S, H, dh).transpose(0, 2, 1, 3)
        v = v.reshape(B, S, H, dh).transpose(0, 2, 1, 3)
        scores = jnp.einsum('bhqd,bhkd->bhqk', q, k) / jnp.sqrt(jnp.float32(dh))
        attn = jax.nn.softmax(scores, axis=-1)
        ctx = jnp.einsum('bhqk,bhkd->bhqd', attn, v)
        ctx = ctx.transpose(0, 2, 1, 3).reshape(B, S, D)
        attn_out = ctx @ wo.T + bo
        x = layernorm(x + attn_out, ln1_g, ln1_b)
        probs = jax.nn.softmax(x @ gate_w + gate_b, axis=-1)
        h = jax.nn.relu(jnp.einsum('bsd,edf->bsef', x, w1) + b1)
        y = jnp.einsum('bsef,efd->bsed', h, w2) + b2
        moe_out = jnp.einsum('bse,bsed->bsd', probs, y)
        x = layernorm(x + moe_out, ln2_g, ln2_b)
        return x

    def _L1_attn_ref(x, Wqkv_w, Wqkv_b, conv_w, conv_b, out_w, out_b):
        import jax, jax.numpy as jnp
        import numpy as np
        import math
        D_MODEL = 128
        NUM_HEADS = 16
        HEAD_DIM = D_MODEL // NUM_HEADS
        B, S = (2, 256)

        def _causal_attn(q, k, v):
            scale = 1.0 / math.sqrt(q.shape[-1])
            scores = jnp.einsum('bthd,bshd->bhts', q, k) * scale
            t = q.shape[1]
            mask = jnp.tril(jnp.ones((t, t), dtype=bool))
            scores = jnp.where(mask, scores, -jnp.inf)
            attn = jax.nn.softmax(scores, axis=-1)
            return jnp.einsum('bhts,bshd->bthd', attn, v)
        b, s, d = x.shape
        qkv = x @ Wqkv_w.T + Wqkv_b
        qkv = qkv.reshape(b, s, 3, NUM_HEADS, HEAD_DIM)
        q, k, v = (qkv[:, :, 0], qkv[:, :, 1], qkv[:, :, 2])
        ctx = _causal_attn(q, k, v)
        ctx_c = ctx.reshape(b, s, d).transpose(0, 2, 1)
        conv_out = jax.lax.conv_general_dilated(ctx_c, conv_w, window_strides=(1,), padding=[(1, 1)], dimension_numbers=('NCH', 'OIH', 'NCH')) + conv_b[None, :, None]
        q2 = conv_out.transpose(0, 2, 1).reshape(b, s, NUM_HEADS, HEAD_DIM)
        ctx2 = _causal_attn(q2, k, v)
        out = ctx2.reshape(b, s, d) @ out_w.T + out_b
        return out

    def _L1_ffn_ref(hidden_states, gate_weight, gate_up_proj, down_proj):
        import jax, jax.numpy as jnp
        import numpy as np
        TOP_K = 8
        NUM_EXPERTS = 32
        CAPACITY = 128
        B, S, H = hidden_states.shape
        E = gate_weight.shape[0]
        N = B * S
        x = hidden_states.reshape(N, H)
        logits = x @ gate_weight.T
        probs = jax.nn.softmax(logits.astype(jnp.float32), axis=-1)
        topw, topi = jax.lax.top_k(probs, TOP_K)
        topw = topw / topw.sum(-1, keepdims=True)
        topw = topw.astype(x.dtype)
        flat_e = topi.reshape(-1)
        flat_w = topw.reshape(-1)
        flat_x = jnp.repeat(x, TOP_K, axis=0)
        oh = jax.nn.one_hot(flat_e, E, dtype=jnp.int32)
        pos = (jnp.cumsum(oh, axis=0) * oh).sum(-1) - 1
        buf = jnp.zeros((E, CAPACITY, H), x.dtype).at[flat_e, pos].set(flat_x, mode='drop')
        gu = jnp.einsum('ech,efh->ecf', buf, gate_up_proj)
        gate, up = jnp.split(gu, 2, axis=-1)
        h = jax.nn.silu(gate) * up
        eo = jnp.einsum('ecf,ehf->ech', h, down_proj)
        tok_out = eo.at[flat_e, pos].get(mode='fill', fill_value=0)
        out = (tok_out * flat_w[:, None]).reshape(N, TOP_K, H).sum(1)
        return out.reshape(B, S, H)
    x = L0_attn_x
    xn = _layernorm(x, axis=-1)
    x = x + _L0_attn_ref(xn, L0_attn_wq_w, L0_attn_wk_w, L0_attn_wv_w, L0_attn_q_norm_w, L0_attn_k_norm_w, L0_attn_alpha_w, L0_attn_theta_w, L0_attn_eta_w, L0_attn_mem_w0, L0_attn_mem_w1, L0_attn_mem_ln_w) + _L0_ffn_ref(xn, L0_ffn_conv_w, L0_ffn_conv_b, L0_ffn_wqkv, L0_ffn_bqkv, L0_ffn_wo, L0_ffn_bo, L0_ffn_ln1_g, L0_ffn_ln1_b, L0_ffn_gate_w, L0_ffn_gate_b, L0_ffn_w1, L0_ffn_b1, L0_ffn_w2, L0_ffn_b2, L0_ffn_ln2_g, L0_ffn_ln2_b)
    xn = _layernorm(x, axis=-1)
    x = x + _L1_attn_ref(xn, L1_attn_Wqkv_w, L1_attn_Wqkv_b, L1_attn_conv_w, L1_attn_conv_b, L1_attn_out_w, L1_attn_out_b) + _L1_ffn_ref(xn, L1_ffn_gate_weight, L1_ffn_gate_up_proj, L1_ffn_down_proj)
    return x

_drawn_inputs = setup_inputs


def setup_inputs(seed=0):
    import zlib

    import numpy as np

    out = dict(_drawn_inputs(seed))
    spreads = {'L0_attn_q_norm_w': (1.0, 0.2),
     'L0_attn_k_norm_w': (1.0, 0.6),
     'L0_attn_mem_ln_w': (1.0, 0.6),
     'L0_ffn_conv_b': (0.0, 0.1),
     'L0_ffn_bqkv': (0.0, 0.1),
     'L0_ffn_bo': (0.0, 0.1),
     'L0_ffn_ln1_g': (1.0, 0.2),
     'L0_ffn_ln1_b': (0.0, 0.1),
     'L0_ffn_gate_b': (0.0, 0.53),
     'L0_ffn_b1': (0.0, 0.449),
     'L0_ffn_b2': (0.0, 0.339),
     'L0_ffn_ln2_g': (1.0, 0.2),
     'L0_ffn_ln2_b': (0.0, 0.1),
     'L1_attn_Wqkv_b': (0.0, 0.596),
     'L1_attn_conv_b': (0.0, 0.8),
     'L1_attn_out_b': (0.0, 0.1)}
    factors = {'L0_attn_wk_w': 64.0,
     'L0_attn_wv_w': 64.0,
     'L0_attn_alpha_w': 64.0,
     'L0_attn_theta_w': 64.0,
     'L0_attn_eta_w': 64.0,
     'L0_attn_mem_w0': 64.0,
     'L0_attn_mem_w1': 64.0,
     'L1_attn_Wqkv_w': 8.0,
     'L1_attn_conv_w': 8.0,
     'L1_attn_out_w': 3.894,
     'L1_ffn_gate_weight': 8.0,
     'L1_ffn_gate_up_proj': 8.0,
     'L1_ffn_down_proj': 8.0}
    for name, (base, spread) in spreads.items():
        noise = np.random.default_rng([zlib.crc32(name.encode()), seed]).standard_normal(out[name].shape)
        drawn = base * np.exp(spread * noise) if base else spread * noise
        out[name] = jnp.asarray(drawn.astype(out[name].dtype))
    for name, factor in factors.items():
        out[name] = (out[name] * factor).astype(out[name].dtype)
    return out
```

```python
from contextlib import ExitStack

import concourse.bass as bass
from concourse import mybir

F32 = mybir.dt.float32
BF16 = mybir.dt.bfloat16
I32 = mybir.dt.int32
ACT = mybir.ActivationFunctionType
ALU = mybir.AluOpType
X = mybir.AxisListType.X

P = 128
D = 128
NB = 16
S = 512
T = S // P
NT = NB * T
N = NB * S
CHUNK = 64
NC = S // CHUNK
CT = NB * CHUNK // P
INTER = 256
H = 16
DH = 8
G = 4
HG = H // G
E0 = 8
F0 = 512
FC = F0 // P
E1 = 32
F1 = 96
CAP = 128
ROWS = N + CAP
SCALE = DH ** -0.5
NEG = -1.0e30
MAGIC = 0x5F3759DF

COLUMNS = {
    "shared": [("ident", D), ("ones", D), ("wq", D), ("qnorm", D)],
    "memory": [("gates", 3 * D), ("half", 2 * D), ("wk", D), ("wv", D), ("knorm", D),
               ("mem", 2 * INTER + D), ("memw1", INTER)],
    "layer0": [("conv0", 3 * D), ("q0", D), ("k0", D), ("v0", G * D), ("vbias0", G * D), ("out0", D),
               ("cols0", 5), ("outb0", D), ("gate0", E0), ("gateb0", E0), ("up0", E0 * F0),
               ("upb0", E0 * FC), ("down0", E0 * F0), ("downb0", D), ("ln2g", D), ("ln2b", D),
               ("router", E1)],
    "layer1": [("q1", D), ("k1", D), ("v1", G * D), ("vbias1", G * D), ("conv1", 3 * D), ("cols1", 3),
               ("out1", D), ("outb1", D), ("maskq", D), ("maskk", D), ("upto", D), ("before", NT),
               ("slots", CAP), ("spare", 1), ("slot", 1)],
}
PLACE = {name: (part, sum(w for _, w in columns[:n]), width)
         for part, columns in COLUMNS.items() for n, (name, width) in enumerate(columns)}
WIDTH = {part: sum(w for _, w in columns) for part, columns in COLUMNS.items()}


class Semaphores(ExitStack):

    def __init__(self):
        super().__init__()
        self.made = []

    def enter_context(self, semaphore):
        self.made.append(super().enter_context(semaphore))
        return self.made[-1]

    def clear(self, nc):
        with nc.Block() as block:
            @block.sync
            def _(sp):
                for sem in self.made:
                    sp.sem_clear(sem)


class Signal:

    def __init__(self, ctx, nc, name, per=1, first=0, unit=1):
        self.sem = ctx.enter_context(nc.semaphore(name))
        self.per, self.first, self.unit = per, first, unit

    def at(self, i, k):
        return i * (self.per * self.unit) + (self.first + k) * self.unit


class Own:

    column = None

    def __init__(self, ctx, nc, name, engine, per):
        self.sem = ctx.enter_context(nc.semaphore(name))
        self.engine, self.per, self.k, self.i = engine, per, 0, 0

    def start(self, i):
        self.i, self.k = i, 0

    def done(self, instruction):
        self.k += 1
        instruction.then_inc(self.sem, 1)
        self.engine.wait_ge(self.sem, self.i * self.per + self.k)

    def hold(self, nc):
        nc.vector.memset(self.column, 0.0)

    def end(self):
        assert self.k == self.per, (self.sem, self.k)


def rsqrt(nc, own, y, v, t):
    own.done(nc.vector.tensor_scalar(y.bitcast(I32), v.bitcast(I32), -0.5, float(MAGIC), ALU.mult, ALU.add))
    for _ in range(3):
        own.done(nc.vector.scalar_tensor_tensor(t, y, -0.5, y, ALU.mult, ALU.mult))
        own.done(nc.vector.tensor_tensor(t, t, v, ALU.mult))
        own.done(nc.vector.scalar_tensor_tensor(y, t, 1.5, y, ALU.add, ALU.mult))


RSQRT_STEPS = 10


def normalise(nc, own, out, src, stats, mv, var, rstd, tmp, eps):
    for t in range(T):
        last = nc.vector.bn_stats(stats[:, t, :], src[:, t, :])
    own.done(last)
    own.hold(nc)
    for t in range(T):
        last = nc.vector.bn_aggr(mv[:, t, :], stats[:, t, :])
    own.done(last)
    own.done(nc.vector.tensor_scalar(var, mv[:, :, 1], eps, None, ALU.add))
    rsqrt(nc, own, rstd, var, tmp)
    for t in range(T):
        last = nc.vector.tensor_scalar(out[:, t, :], src[:, t, :], mv[:, t, 0:1], rstd[:, t:t + 1],
                                       ALU.subtract, ALU.mult)
    return last


NORMALISE_STEPS = 3 + RSQRT_STEPS


def over(ap, n):
    return ap.unsqueeze(1).broadcast_to([P, n, ap.shape[-1]])


def along(ap, n):
    return ap.unsqueeze(2).broadcast_to([P, ap.shape[-1], n])


def project(nc, ctx0, K, bank, x, xnt_d, kn_d, vn_d, R):
    with ExitStack() as ctx:
        def sb(name, shape, dt=F32):
            return ctx.enter_context(nc.sbuf_tensor("p_" + name, shape, dt))

        xin = sb("xin", [P, T, D])
        xn = sb("xn", [P, T, D])
        xt = sb("xt", [P, S])
        tk = sb("tk", [P, T, D])
        tv = sb("tv", [P, T, D])
        sk = sb("sk", [P, T, D])
        sq = sb("sq", [P, T, D])
        kn = sb("kn", [P, T, D])
        vn = sb("vn", [P, T, D])
        prod = sb("prod", [P, 3, T, D])
        stats = sb("stats", [P, T, 6])
        mv = sb("mv", [P, T, 2])
        var = sb("var", [P, T])
        rstd = sb("rstd", [P, T])
        tmp = sb("tmp", [P, T])
        ss = sb("ss", [P, T])

        x_loaded = Signal(ctx0, nc, "p_x_loaded", unit=16)
        x_free = Signal(ctx0, nc, "p_x_free", first=1)
        xn_ready = Signal(ctx0, nc, "p_xn_ready")
        t_ready = Signal(ctx0, nc, "p_t_ready")
        xt_ready = Signal(ctx0, nc, "p_xt_ready")
        kv_ready = Signal(ctx0, nc, "p_kv_ready")
        tanh_ready = Signal(ctx0, nc, "p_tanh_ready")
        kv_free = Signal(ctx0, nc, "p_kv_free", first=1)
        kn_ready = Signal(ctx0, nc, "p_kn_ready")
        vs_ready = Signal(ctx0, nc, "p_vs_ready")
        vn_ready = Signal(ctx0, nc, "p_vn_ready")
        prod_ready = Signal(ctx0, nc, "p_prod_ready")
        prod_free = Signal(ctx0, nc, "p_prod_free", first=1)
        xt_stored = Signal(ctx0, nc, "p_xt_stored", first=1, unit=16)
        kn_stored = Signal(ctx0, nc, "p_kn_stored", first=1, per=T, unit=16)
        vn_stored = Signal(ctx0, nc, "p_vn_stored", first=1, per=T, unit=16)

        def rows_of(table, b, t):
            return table[2 * t:2 * t + 2, bass.ds(b * CHUNK, CHUNK), :]

        with nc.Block() as block:
            @block.sync
            def _(sp):
                sp.sem_inc(xt_stored.sem, 16)
                sp.sem_inc(kn_stored.sem, 16)
                sp.sem_inc(vn_stored.sem, 16)
                with sp.Fori(0, NB) as b:
                    sp.wait_ge(x_free.sem, x_free.at(b, 0))
                    sp.dma_start(xin[:, :, :], x[bass.ds(b, 1), :, :].rearrange("o (t p) d -> p (o t) d", p=P)
                                 ).then_inc(x_loaded.sem, 16)
                    sp.wait_ge(xt_ready.sem, xt_ready.at(b, 1))
                    sp.dma_start(xnt_d[bass.ds(b * P, P), :], xt[:, :]).then_inc(xt_stored.sem, 16)
                    sp.wait_ge(kn_ready.sem, kn_ready.at(b, 1))
                    for t in range(T):
                        sp.dma_start(rows_of(kn_d, b, t), kn[:, t, :]).then_inc(kn_stored.sem, 16)
                    sp.wait_ge(vn_ready.sem, vn_ready.at(b, 1))
                    for t in range(T):
                        sp.dma_start(rows_of(vn_d, b, t), vn[:, t, :]).then_inc(vn_stored.sem, 16)
                sp.wait_ge(xt_stored.sem, xt_stored.at(NB, 0))
                sp.wait_ge(kn_stored.sem, kn_stored.at(NB, 0))
                sp.wait_ge(vn_stored.sem, vn_stored.at(NB, 0))

            @block.tensor
            def _(pe):
                with pe.Fori(0, NB) as b:
                    pe.wait_ge(xn_ready.sem, xn_ready.at(b, 1))
                    for t in range(T):
                        last = nc.tensor.transpose(bank[0][:, t * P:(t + 1) * P], xn[:, t, :], K("ident"))
                    last.then_inc(t_ready.sem, 1)
                    pe.wait_ge(xt_ready.sem, xt_ready.at(b, 1))
                    pe.wait_ge(kv_free.sem, kv_free.at(b, 0))
                    for t in range(T):
                        nc.tensor.matmul(bank[1][:, t * P:(t + 1) * P], xt[:, t * P:(t + 1) * P], K("wk"), start=True, stop=True)
                    for t in range(T):
                        last = nc.tensor.matmul(bank[2][:, t * P:(t + 1) * P], xt[:, t * P:(t + 1) * P], K("wv"), start=True, stop=True)
                    last.then_inc(kv_ready.sem, 1)

            @block.scalar
            def _(act):
                with act.Fori(0, NB) as b:
                    act.wait_ge(t_ready.sem, t_ready.at(b, 1))
                    act.wait_ge(xt_stored.sem, xt_stored.at(b, 0))
                    act.wait_ge(kv_free.sem, kv_free.at(b, 0))
                    nc.scalar.activation(xt[:, :], bank[0][:, :], ACT.Copy).then_inc(xt_ready.sem, 1)
                    act.wait_ge(kv_ready.sem, kv_ready.at(b, 1))
                    nc.scalar.activation(tk[:, :, :], bank[1][:, :].rearrange("p (t d) -> p t d", t=T), ACT.Tanh, scale=0.5)
                    nc.scalar.activation(tv[:, :, :], bank[2][:, :].rearrange("p (t d) -> p t d", t=T), ACT.Tanh, scale=0.5
                                         ).then_inc(tanh_ready.sem, 1)
                    act.wait_ge(vs_ready.sem, vs_ready.at(b, 1))
                    act.wait_ge(vn_stored.sem, vn_stored.at(b, 0))
                    nc.scalar.activation(vn[:, :, :], tv[:, :, :], ACT.Copy, scale=0.5).then_inc(vn_ready.sem, 1)

            @block.gpsimd
            def _(pool):
                with pool.Fori(0, NB) as b:
                    pool.wait_ge(xn_ready.sem, xn_ready.at(b, 1))
                    pool.wait_ge(prod_free.sem, prod_free.at(b, 0))
                    for w in range(3):
                        last = nc.gpsimd.tensor_tensor(prod[:, w], xn[:, :, :], over(K("gates", w * D, D), T), ALU.mult)
                    last.then_inc(prod_ready.sem, 1)

            @block.vector
            def _(dve):
                nc.vector.sem_inc(x_free.sem, 1)
                nc.vector.sem_inc(kv_free.sem, 1)
                nc.vector.sem_inc(prod_free.sem, 1)
                own = Own(ctx0, nc, "p_own", dve, NORMALISE_STEPS + 4 + RSQRT_STEPS)
                with dve.Fori(0, NB) as b:
                    own.start(b)
                    dve.wait_ge(x_loaded.sem, x_loaded.at(b, 1))
                    dve.wait_ge(kv_free.sem, kv_free.at(b, 0))
                    dve.wait_ge(prod_free.sem, prod_free.at(b, 0))
                    last = normalise(nc, own, xn, xin, stats, mv, var[:, :], rstd[:, :], tmp[:, :], 1e-5)
                    last.then_inc(xn_ready.sem, 1)
                    dve.wait_ge(xn_ready.sem, xn_ready.at(b, 1))
                    nc.vector.sem_inc(x_free.sem, 1)
                    dve.wait_ge(tanh_ready.sem, tanh_ready.at(b, 1))
                    nc.vector.scalar_tensor_tensor(tv[:, :, :], tv[:, :, :], 1.0, bank[2][:, :].rearrange("p (t d) -> p t d", t=T), ALU.add, ALU.mult
                                                   ).then_inc(vs_ready.sem, 1)
                    own.done(nc.vector.scalar_tensor_tensor(sk[:, :, :], tk[:, :, :], 1.0, bank[1][:, :].rearrange("p (t d) -> p t d", t=T), ALU.add, ALU.mult))
                    own.done(nc.vector.tensor_tensor(sq[:, :, :], sk[:, :, :], sk[:, :, :], ALU.mult))
                    own.done(nc.vector.tensor_reduce(ss[:, :], sq[:, :, :], X, ALU.add))
                    own.done(nc.vector.tensor_scalar(ss[:, :], ss[:, :], 1.0 / D, 4e-6, ALU.mult, ALU.add))
                    rsqrt(nc, own, rstd[:, :], ss[:, :], tmp[:, :])
                    dve.wait_ge(kn_stored.sem, kn_stored.at(b, 0))
                    for t in range(T):
                        last = nc.vector.scalar_tensor_tensor(kn[:, t, :], sk[:, t, :], rstd[:, t:t + 1], K("knorm"), ALU.mult, ALU.mult)
                    last.then_inc(kn_ready.sem, 1)
                    dve.wait_ge(vn_ready.sem, vn_ready.at(b, 1))
                    dve.wait_ge(kn_ready.sem, kn_ready.at(b, 1))
                    nc.vector.sem_inc(kv_free.sem, 1)
                    dve.wait_ge(prod_ready.sem, prod_ready.at(b, 1))
                    own.hold(nc)
                    for w in range(3):
                        last = nc.vector.tensor_reduce(R[:, bass.ds(b * T + w * NT, T)], prod[:, w], X, ALU.add)
                    last.then_inc(prod_free.sem, 1)
                own.end()
                dve.wait_ge(prod_free.sem, prod_free.at(NB, 0))


def learn(nc, ctx0, K, ps, bank, kn_d, vn_d, R, mem, memw1):
    with ExitStack() as ctx:
        def sb(name, shape, dt=F32):
            return ctx.enter_context(nc.sbuf_tensor("m_" + name, shape, dt))

        M = 2 * INTER + D
        kn = [sb(f"kn{i}", [P, CT, D]) for i in range(2)]
        vn = [sb(f"vn{i}", [P, CT, D]) for i in range(2)]
        kv = sb("kv", [P, CT, D])
        kt = sb("kt", [P, CT * P])
        tz = sb("tz", [P, CT, INTER])
        hid = sb("hid", [P, CT, INTER])
        slope = sb("slope", [P, CT, INTER])
        hs = sb("hs", [P, CT, INTER])
        ht = sb("ht", [P, 2, CT * P])
        ys = sb("ys", [P, CT, D])
        nrm = sb("nrm", [P, CT, D])
        e = sb("e", [P, CT, D])
        en = sb("en", [P, CT, D])
        dn = sb("dn", [P, CT, D])
        dy = sb("dy", [P, CT, D])
        dyt = sb("dyt", [P, CT * P])
        dz = sb("dz", [P, CT, INTER])
        keep = sb("keep", [P, M])
        surp = sb("surp", [P, M])
        sqs = sb("sqs", [P, M])
        logits = sb("logits", [P, 2, 3 * NT])
        tgate = sb("tgate", [P, 2, NT])
        decay = sb("decay", [P, 3, 2, T])
        th = sb("th", [P, NC, CT])
        eta_beta = sb("eta_beta", [P, NC, 2])
        eb = sb("eb", [P, 2])
        ths = sb("ths", [P, CT])
        ss = sb("ss", [P, CT])
        r = sb("r", [P, CT])
        tmp = sb("tmp", [P, CT])
        dot = sb("dot", [P, CT])
        gs = sb("gs", [P, 4])
        tot = sb("tot", [P, 1])
        rt = sb("rt", [P, 1])
        t1 = sb("t1", [P, 1])
        clip = sb("clip", [P, 1])

        def S1(name, **kw):
            return Signal(ctx0, nc, "m_" + name, **kw)

        gate_sums = S1("gate_sums")
        gate_copied = S1("gate_copied")
        gate_means = S1("gate_means")
        gate_tanh = S1("gate_tanh")
        kv_loaded = [S1(f"kv_loaded{i}", per=2, unit=16) for i in range(2)]
        step_done = S1("step_done", first=1)
        kt_ready = S1("kt_ready")
        kt_copied = S1("kt_copied")
        z_ready = S1("z_ready")
        tanh_ready = S1("tanh_ready")
        h_ready = S1("h_ready")
        slope_ready = S1("slope_ready", per=3)
        kv_ready = S1("kv_ready")
        ht_ready = S1("ht_ready")
        ht_copied = S1("ht_copied")
        y_ready = S1("y_ready")
        y_copied = S1("y_copied")
        y_squared = S1("y_squared")
        e_ready = S1("e_ready")
        en_ready = S1("en_ready")
        dy_ready = S1("dy_ready")
        dyt_ready = S1("dyt_ready")
        dyt_copied = S1("dyt_copied")
        dh_ready = S1("dh_ready")
        dz_ready = S1("dz_ready")
        grads_ready = S1("grads_ready")
        squares_ready = S1("squares_ready", per=3)
        part_ready = S1("part_ready")
        norm_ready = S1("norm_ready")
        keep_ready = S1("keep_ready")
        mem_ready = S1("mem_ready")
        w1_ready = S1("w1_ready")
        w1_copied = S1("w1_copied")

        w0t = mem[:, 0:INTER]
        w1t = [mem[:, INTER + f * D:INTER + (f + 1) * D] for f in range(2)]
        ln = mem[:, 2 * INTER:M]

        def tiles(ap, w):
            return ap.rearrange("p (t w) -> p t w", w=w)

        z_ps = ps[:, 0:4, :].rearrange("p b (t w) -> p (b t) w", w=INTER)
        y_ps = ps[:, 0:2, :].rearrange("p b (t w) -> p (b t) w", w=D)
        ht_ps = ps[:, 4:8, :].rearrange("p (f b) w -> p f (b w)", f=2)
        kt_ps = ps[:, 4:6, :].rearrange("p b w -> p (b w)")
        dyt_ps = ps[:, 2:4, :].rearrange("p b w -> p (b w)")
        dh_ps = ps[:, 4:8, :].rearrange("p b (t w) -> p (b t) w", w=INTER)
        g_w = ps[:, 0, :]
        g_ln = ps[:, 1, 0:D]
        norm_ps = ps[:, 2, 0:1]
        w1_ps = ps[:, 3, 0:INTER]

        with nc.Block() as block:
            @block.sync
            def _(sp):
                sp.dma_start(kn[0][:, :, :], kn_d[0].rearrange("(t p) d -> p t d", p=P)).then_inc(kv_loaded[0].sem, 16)
                sp.dma_start(vn[0][:, :, :], vn_d[0].rearrange("(t p) d -> p t d", p=P)).then_inc(kv_loaded[0].sem, 16)
                sp.dma_start(kn[1][:, :, :], kn_d[1].rearrange("(t p) d -> p t d", p=P)).then_inc(kv_loaded[1].sem, 16)
                sp.dma_start(vn[1][:, :, :], vn_d[1].rearrange("(t p) d -> p t d", p=P)).then_inc(kv_loaded[1].sem, 16)
                with sp.Fori(0, NC // 2 - 1) as pair:
                    c = pair * 2
                    for u in range(2):
                        sp.wait_ge(grads_ready.sem, grads_ready.at(c, u + 1))
                        sp.dma_start(kn[u][:, :, :], kn_d[bass.ds(c + (u + 2), 1)].rearrange("o (t p) d -> p (o t) d", p=P)
                                     ).then_inc(kv_loaded[u].sem, 16)
                        sp.dma_start(vn[u][:, :, :], vn_d[bass.ds(c + (u + 2), 1)].rearrange("o (t p) d -> p (o t) d", p=P)
                                     ).then_inc(kv_loaded[u].sem, 16)

            @block.tensor
            def _(pe):
                for h in range(2):
                    last = nc.tensor.matmul(bank[6 + h][:, 0:3 * NT], K("half", h * D, D), R[:, :], start=True, stop=True)
                last.then_inc(gate_sums.sem, 1)
                pe.wait_ge(gate_copied.sem, 1)
                with pe.Fori(0, NC // 2) as pair:
                    c = pair * 2
                    for u in range(2):
                        pe.wait_ge(kv_loaded[u].sem, c * 16 + 32)
                        pe.wait_ge(step_done.sem, step_done.at(c, u))
                        for t in range(CT):
                            last = nc.tensor.transpose(kt_ps[:, t * P:(t + 1) * P], kn[u][:, t, :], K("ident"))
                        last.then_inc(kt_ready.sem, 1)
                        pe.wait_ge(kt_copied.sem, kt_copied.at(c, u + 1))
                        for t in range(CT):
                            last = nc.tensor.matmul(z_ps[:, t, :], kt[:, t * P:(t + 1) * P], w0t, start=True, stop=True)
                        last.then_inc(z_ready.sem, 1)
                        pe.wait_ge(h_ready.sem, h_ready.at(c, u + 1))
                        for f in range(2):
                            for t in range(CT):
                                last = nc.tensor.transpose(ht_ps[:, f, t * P:(t + 1) * P], hid[:, t, f * P:(f + 1) * P], K("ident"))
                        last.then_inc(ht_ready.sem, 1)
                        pe.wait_ge(ht_copied.sem, ht_copied.at(c, u + 1))
                        for t in range(CT):
                            for f in range(2):
                                last = nc.tensor.matmul(y_ps[:, t, :], ht[:, f, t * P:(t + 1) * P], w1t[f], start=f == 0, stop=f == 1)
                        last.then_inc(y_ready.sem, 1)
                        pe.wait_ge(dy_ready.sem, dy_ready.at(c, u + 1))
                        for t in range(CT):
                            last = nc.tensor.transpose(dyt_ps[:, t * P:(t + 1) * P], dy[:, t, :], K("ident"))
                        last.then_inc(dyt_ready.sem, 1)
                        for f in range(2):
                            for t in range(CT):
                                nc.tensor.matmul(g_w[:, INTER + f * D:INTER + (f + 1) * D], hid[:, t, f * P:(f + 1) * P], dy[:, t, :],
                                                 start=t == 0, stop=t == CT - 1)
                        pe.wait_ge(dyt_copied.sem, dyt_copied.at(c, u + 1))
                        for t in range(CT):
                            last = nc.tensor.matmul(dh_ps[:, t, :], dyt[:, t * P:(t + 1) * P], memw1[:, :], start=True, stop=True)
                        last.then_inc(dh_ready.sem, 1)
                        pe.wait_ge(en_ready.sem, en_ready.at(c, u + 1))
                        for t in range(CT):
                            nc.tensor.matmul(g_ln, K("ones"), en[:, t, :], start=t == 0, stop=t == CT - 1)
                        pe.wait_ge(dz_ready.sem, dz_ready.at(c, u + 1))
                        for t in range(CT):
                            last = nc.tensor.matmul(g_w[:, 0:INTER], kn[u][:, t, :], dz[:, t, :], start=t == 0, stop=t == CT - 1)
                        last.then_inc(grads_ready.sem, 1)
                        pe.wait_ge(part_ready.sem, part_ready.at(c, u + 1))
                        nc.tensor.matmul(norm_ps, K("ones"), gs[:, 3:4], start=True, stop=True).then_inc(norm_ready.sem, 1)
                        pe.wait_ge(mem_ready.sem, mem_ready.at(c, u + 1))
                        for f in range(2):
                            last = nc.tensor.transpose(w1_ps[:, f * P:(f + 1) * P], w1t[f], K("ident"))
                        last.then_inc(w1_ready.sem, 1)

            @block.scalar
            def _(act):
                act.wait_ge(gate_sums.sem, 1)
                nc.scalar.activation(logits[:, 0, :], bank[6][:, 0:3 * NT], ACT.Copy)
                nc.scalar.activation(logits[:, 1, :], bank[7][:, 0:3 * NT], ACT.Copy).then_inc(gate_copied.sem, 1)
                act.wait_ge(gate_copied.sem, 1)
                nc.scalar.activation(tgate[:, :, :], logits[:, :, NT:2 * NT], ACT.Tanh, scale=0.5)
                act.wait_ge(gate_means.sem, 1)
                nc.scalar.activation(decay[:, :, :, :], decay[:, :, :, :], ACT.Tanh, scale=0.5 / NB).then_inc(gate_tanh.sem, 1)
                with act.Fori(0, NC // 2) as pair:
                    c = pair * 2
                    for u in range(2):
                        act.wait_ge(kt_ready.sem, kt_ready.at(c, u + 1))
                        nc.scalar.activation(kt[:, :], kt_ps, ACT.Copy).then_inc(kt_copied.sem, 1)
                        act.wait_ge(z_ready.sem, z_ready.at(c, u + 1))
                        nc.scalar.activation(tz[:, :, :], z_ps, ACT.Tanh, scale=0.5).then_inc(tanh_ready.sem, 1)
                        act.wait_ge(ht_ready.sem, ht_ready.at(c, u + 1))
                        nc.scalar.activation(ht[:, :, :], ht_ps, ACT.Copy).then_inc(ht_copied.sem, 1)
                        act.wait_ge(y_ready.sem, y_ready.at(c, u + 1))
                        nc.scalar.activation(ys[:, :, :], y_ps, ACT.Copy).then_inc(y_copied.sem, 1)
                        act.wait_ge(y_copied.sem, y_copied.at(c, u + 1))
                        nc.scalar.activation(nrm[:, :, :], ys[:, :, :], ACT.Square).then_inc(y_squared.sem, 1)
                        act.wait_ge(dyt_ready.sem, dyt_ready.at(c, u + 1))
                        nc.scalar.activation(dyt[:, :], dyt_ps, ACT.Copy).then_inc(dyt_copied.sem, 1)
                        act.wait_ge(grads_ready.sem, grads_ready.at(c, u + 1))
                        nc.scalar.activation(sqs[:, 0:INTER], g_w[:, 0:INTER], ACT.Square, accum_out=gs[:, 0:1]).then_inc(squares_ready.sem, 1)
                        nc.scalar.activation(sqs[:, INTER:2 * INTER], g_w[:, INTER:2 * INTER], ACT.Square, accum_out=gs[:, 1:2]).then_inc(squares_ready.sem, 1)
                        nc.scalar.activation(sqs[:, 2 * INTER:M], g_ln, ACT.Square, accum_out=gs[:, 2:3]).then_inc(squares_ready.sem, 1)
                        act.wait_ge(w1_ready.sem, w1_ready.at(c, u + 1))
                        nc.scalar.activation(memw1[:, :], w1_ps, ACT.Copy).then_inc(w1_copied.sem, 1)

            @block.gpsimd
            def _(pool):
                with pool.Fori(0, NC // 2) as pair:
                    c = pair * 2
                    for u in range(2):
                        pool.wait_ge(kv_loaded[u].sem, c * 16 + 32)
                        pool.wait_ge(step_done.sem, step_done.at(c, u))
                        nc.gpsimd.tensor_tensor(kv[:, :, :], kn[u][:, :, :], vn[u][:, :, :], ALU.subtract).then_inc(kv_ready.sem, 1)
                        pool.wait_ge(h_ready.sem, h_ready.at(c, u + 1))
                        nc.gpsimd.tensor_tensor(hs[:, :, :], hid[:, :, :], tz[:, :, :], ALU.mult).then_inc(slope_ready.sem, 1)
                        nc.gpsimd.tensor_tensor(slope[:, :, :], hid[:, :, :], tz[:, :, :], ALU.add).then_inc(slope_ready.sem, 1)
                        pool.wait_ge(slope_ready.sem, slope_ready.at(c, 3 * u + 2))
                        nc.gpsimd.tensor_tensor(slope[:, :, :], slope[:, :, :], hs[:, :, :], ALU.subtract).then_inc(slope_ready.sem, 1)
                        pool.wait_ge(e_ready.sem, e_ready.at(c, u + 1))
                        nc.gpsimd.tensor_tensor(en[:, :, :], e[:, :, :], nrm[:, :, :], ALU.mult).then_inc(en_ready.sem, 1)

            @block.vector
            def _(dve):
                setup = Own(ctx0, nc, "m_setup", dve, 4)
                setup.start(0)
                setup.done(nc.vector.tensor_copy(mem[:, :], K("mem")))
                setup.done(nc.vector.tensor_copy(memw1[:, :], K("memw1")))
                setup.done(nc.vector.memset(surp[:, :], 0.0))
                dve.wait_ge(gate_copied.sem, 1)
                for g in range(3):
                    last = nc.vector.tensor_reduce(decay[:, g], logits[:, :, g * NT:(g + 1) * NT].rearrange("p h (b t) -> p h t b", t=T), X, ALU.add)
                last.then_inc(gate_means.sem, 1)
                dve.wait_ge(gate_tanh.sem, 1)
                k_th = 0.01 * 0.5 * 2.0 / (NB * CHUNK * D)
                for half in range(2):
                    rows = slice(half * CHUNK, (half + 1) * CHUNK)
                    for h in range(2):
                        src = tgate[rows, h, :].rearrange("p (t b q) -> p t b q", b=2, q=T)[:, :, half, :]
                        dst = th[rows, :, :].rearrange("p (q h) t -> p t h q", h=2)[:, :, h, :]
                        nc.vector.tensor_scalar(dst, src, 1.0, k_th, ALU.add, ALU.mult)
                for h in range(2):
                    dst = eta_beta[:, :, :].rearrange("p (q h) x -> p h q x", h=2)[:, h]
                    nc.vector.tensor_scalar(dst[:, :, 0], decay[:, 2, h, :], 0.5, 0.5, ALU.mult, ALU.add)
                    last = nc.vector.tensor_scalar(dst[:, :, 1], decay[:, 0, h, :], -0.5, 0.5, ALU.mult, ALU.add)
                setup.done(last)
                nc.vector.sem_inc(step_done.sem, 1)
                steps = 21 + 2 * RSQRT_STEPS
                own = Own(ctx0, nc, "m_own", dve, steps)
                with dve.Fori(0, NC // 2) as pair:
                    c = pair * 2
                    for u in range(2):
                        own.start(c)
                        own.k = u * steps
                        own.hold(nc)
                        nc.vector.tensor_copy(eb[:, :], eta_beta[:, bass.ds(c + u, 1), :].rearrange("p o x -> p (o x)"))
                        own.done(nc.vector.tensor_copy(ths[:, :], th[:, bass.ds(c + u, 1), :].rearrange("p o x -> p (o x)")))
                        dve.wait_ge(tanh_ready.sem, tanh_ready.at(c, u + 1))
                        own.done(nc.vector.tensor_scalar(tz[:, :, :], tz[:, :, :], 0.5, 0.5, ALU.mult, ALU.add))
                        nc.vector.tensor_tensor(hid[:, :, :], tz[:, :, :], z_ps, ALU.mult).then_inc(h_ready.sem, 1)
                        own.done(nc.vector.tensor_scalar(keep[:, :], surp[:, :], eb[:, 0:1], None, ALU.mult))
                        dve.wait_ge(y_squared.sem, y_squared.at(c, u + 1))
                        own.done(nc.vector.tensor_reduce(ss[:, :], nrm[:, :, :], X, ALU.add))
                        own.done(nc.vector.tensor_scalar(ss[:, :], ss[:, :], 1.0 / D, 1e-6, ALU.mult, ALU.add))
                        rsqrt(nc, own, r[:, :], ss[:, :], tmp[:, :])
                        own.done(nc.vector.tensor_tensor(nrm[:, :, :], ys[:, :, :], along(r[:, :], D), ALU.mult))
                        own.done(nc.vector.tensor_tensor(e[:, :, :], nrm[:, :, :], over(ln, CT), ALU.mult))
                        dve.wait_ge(kv_ready.sem, kv_ready.at(c, u + 1))
                        own.done(nc.vector.tensor_tensor(e[:, :, :], e[:, :, :], kv[:, :, :], ALU.add))
                        nc.vector.tensor_tensor(e[:, :, :], e[:, :, :], along(ths[:, :], D), ALU.mult).then_inc(e_ready.sem, 1)
                        dve.wait_ge(e_ready.sem, e_ready.at(c, u + 1))
                        own.done(nc.vector.tensor_tensor(dn[:, :, :], e[:, :, :], over(ln, CT), ALU.mult))
                        own.done(nc.vector.tensor_tensor(dy[:, :, :], dn[:, :, :], nrm[:, :, :], ALU.mult))
                        own.done(nc.vector.tensor_reduce(dot[:, :], dy[:, :, :], X, ALU.add))
                        own.done(nc.vector.tensor_scalar(dot[:, :], dot[:, :], 1.0 / D, None, ALU.mult))
                        own.done(nc.vector.tensor_tensor(dy[:, :, :], nrm[:, :, :], along(dot[:, :], D), ALU.mult))
                        own.done(nc.vector.tensor_tensor(dy[:, :, :], dn[:, :, :], dy[:, :, :], ALU.subtract))
                        nc.vector.tensor_tensor(dy[:, :, :], dy[:, :, :], along(r[:, :], D), ALU.mult).then_inc(dy_ready.sem, 1)
                        dve.wait_ge(slope_ready.sem, slope_ready.at(c, 3 * u + 3))
                        dve.wait_ge(dh_ready.sem, dh_ready.at(c, u + 1))
                        nc.vector.tensor_tensor(dz[:, :, :], slope[:, :, :], dh_ps, ALU.mult).then_inc(dz_ready.sem, 1)
                        dve.wait_ge(squares_ready.sem, squares_ready.at(c, 3 * u + 3))
                        own.done(nc.vector.scalar_tensor_tensor(gs[:, 3:4], gs[:, 2:3], 1.0 / P, gs[:, 0:1], ALU.mult, ALU.add))
                        nc.vector.tensor_tensor(gs[:, 3:4], gs[:, 3:4], gs[:, 1:2], ALU.add).then_inc(part_ready.sem, 1)
                        dve.wait_ge(norm_ready.sem, norm_ready.at(c, u + 1))
                        own.done(nc.vector.tensor_scalar(tot[:, :], norm_ps, 1e-36, None, ALU.max))
                        rsqrt(nc, own, rt[:, :], tot[:, :], t1[:, :])
                        own.done(nc.vector.tensor_tensor(rt[:, :], rt[:, :], tot[:, :], ALU.mult))
                        own.done(nc.vector.tensor_scalar(rt[:, :], rt[:, :], 1e-6, None, ALU.add))
                        own.done(nc.vector.reciprocal(clip[:, :], rt[:, :]))
                        own.done(nc.vector.tensor_scalar(clip[:, :], clip[:, :], 1.0, -1.0, ALU.min, ALU.mult))
                        nc.vector.scalar_tensor_tensor(surp[:, 0:2 * INTER], g_w, clip[:, 0:1], keep[:, 0:2 * INTER], ALU.mult, ALU.add)
                        own.done(nc.vector.scalar_tensor_tensor(surp[:, 2 * INTER:M], g_ln, clip[:, 0:1], keep[:, 2 * INTER:M], ALU.mult, ALU.add))
                        nc.vector.scalar_tensor_tensor(mem[:, :], mem[:, :], eb[:, 1:2], surp[:, :], ALU.mult, ALU.add).then_inc(mem_ready.sem, 1)
                        dve.wait_ge(mem_ready.sem, mem_ready.at(c, u + 1))
                        dve.wait_ge(w1_copied.sem, w1_copied.at(c, u + 1))
                        nc.vector.sem_inc(step_done.sem, 1)
                        assert own.k == (u + 1) * steps, own.k
                dve.wait_ge(step_done.sem, step_done.at(NC, 0))


PARTS = 6
Q_PARTS = (0, 0, 0, 1, 1, 2)
K_PARTS = (0, 1, 2, 0, 1, 0)
SHIFT = PARTS * DH


class Attention:

    def __init__(self, ctx, csem, nc, K, ps, bank, name, causal, calls):
        def sb(n, shape, dt=F32):
            return ctx.enter_context(nc.sbuf_tensor(f"{name}_{n}", shape, dt))

        def sig(n, per, first=0, unit=1):
            return Signal(csem, nc, f"{name}_{n}", per=per * calls, first=first, unit=unit)

        self.nc, self.K, self.ps, self.bank, self.causal, self.calls = nc, K, ps, bank, causal, calls
        self.qk = sb("qk", [P, 2, S])
        self.part = [sb(f"part{n}", [P, 2, S], BF16) for n in range(3)]
        self.rest = sb("rest", [P, 2, S])
        self.qa = sb("qa", [P, H, S], BF16)
        self.ka = sb("ka", [P, H, S], BF16)
        self.zero = sb("zero", [2, S], BF16)
        self.one = sb("one", [2, S], BF16)
        self.v = sb("v", [P, T, H * 32])
        self.maxima = sb("maxima", [P, 2, HG * T])
        self.shift = sb("shift", [HG * T, 2, P], BF16)
        self.prob = sb("prob", [P, 2, HG, T, S])
        self.c = sb("c", [P, S])
        self.rsum = sb("rsum", [P, T, HG])
        self.ctxn = sb("ctxn", [P, T, D])
        self.ctxt = sb("ctxt", [P, S])
        if causal:
            self.mask = [sb(f"mask{n}", [P, P], BF16) for n in range(2)]
            self.identb = sb("identb", [P, P], BF16)
        self.units = T if causal else T // 2
        self.setup_done = Signal(csem, nc, f"{name}_setup_done")
        self.ones_loaded = Signal(csem, nc, f"{name}_ones_loaded", unit=16)
        self.qk_ready = sig("qk_ready", 1)
        self.hi_ready = sig("hi_ready", 1)
        self.rest_ready = sig("rest_ready", 1, first=1)
        self.mid_ready = sig("mid_ready", 1)
        self.lo_ready = sig("lo_ready", 1)
        loads = [1 + 2 * PARTS, 1 + PARTS]
        self.loads = loads[:calls]
        self.rows_loaded = [Signal(csem, nc, f"{name}_rows_loaded{a}", per=loads[a], first=1, unit=16)
                            for a in range(calls)]
        self.m_ready = sig("m_ready", H * T)
        self.m_free = sig("m_free", H * T, first=2)
        self.misc_free = sig("misc_free", 2 * G + 1, first=1)
        self.maxt_ready = sig("maxt_ready", G)
        self.shift_ready = sig("shift_ready", G)
        self.shift_loaded = sig("shift_loaded", 2 * G, first=2, unit=16)
        self.s_ready = sig("s_ready", H * self.units, first=1)
        self.s_free = sig("s_free", H * self.units, first=4 * self.units // T)
        self.pv_ready = sig("pv_ready", G, first=2)
        self.c_copied = sig("c_copied", G, first=1)
        self.ct_ready = sig("ct_ready", G, first=1)
        self.ctxn_ready = sig("ctxn_ready", 1)
        self.ctxt_ready = sig("ctxt_ready", 1, first=1)
        self.ctxt_copied = sig("ctxt_copied", 1)

    def setup_pool(self, pool):
        nc = self.nc
        nc.gpsimd.memset(self.qa[:, :, :], 0.0)
        nc.gpsimd.memset(self.ka[:, :, :], 0.0)
        nc.gpsimd.memset(self.zero[:, :], 0.0)
        last = nc.gpsimd.memset(self.one[:, :], 1.0)
        if self.causal:
            nc.gpsimd.tensor_copy(self.mask[0][:, :], self.K("maskq"))
            nc.gpsimd.tensor_copy(self.mask[1][:, :], self.K("maskk"))
            last = nc.gpsimd.tensor_copy(self.identb[:, :], self.K("ident"))
        last.then_inc(self.setup_done.sem, 1)

    def setup_sync(self, sp):
        sp.wait_ge(self.setup_done.sem, 1)
        sp.dma_start(self.ka[SHIFT:SHIFT + 2, :, :], self.one[0:2, :].unsqueeze(1).broadcast_to([2, H, S])
                     ).then_inc(self.ones_loaded.sem, 16)
        for a in range(self.calls):
            sp.sem_inc(self.rows_loaded[a].sem, 16)
        sp.sem_inc(self.shift_loaded.sem, 32)

    def setup_tensor(self, pe):
        pe.sem_inc(self.s_ready.sem, 1)
        pe.sem_inc(self.pv_ready.sem, 2)
        pe.sem_inc(self.ct_ready.sem, 1)
        pe.sem_inc(self.ctxt_ready.sem, 1)
        pe.wait_ge(self.ones_loaded.sem, 16)

    def setup_scalar(self, act):
        act.sem_inc(self.s_free.sem, self.s_free.first)
        act.sem_inc(self.c_copied.sem, 1)

    def setup_vector(self, dve):
        dve.sem_inc(self.rest_ready.sem, 1)
        dve.sem_inc(self.m_free.sem, 2)
        dve.sem_inc(self.misc_free.sem, 1)

    def before_qk(self, act, i, a):
        act.wait_ge(self.rest_ready.sem, self.rest_ready.at(i, a))

    def split_scalar(self, act, i, a, n):
        nc = self.nc
        act.wait_ge(self.qk_ready.sem, self.qk_ready.at(i, a + 1))
        if a:
            act.wait_ge(self.rows_loaded[0].sem, self.rows_loaded[0].at(i, self.loads[0]))
        else:
            act.wait_ge(self.rows_loaded[-1].sem, self.rows_loaded[-1].at(i, 0))
        nc.scalar.activation(self.part[0][:, 0:n, :], self.qk[:, 0:n, :], ACT.Copy).then_inc(self.hi_ready.sem, 1)
        act.wait_ge(self.rest_ready.sem, self.rest_ready.at(i, a + 1))
        nc.scalar.activation(self.part[1][:, 0:n, :], self.rest[:, 0:n, :], ACT.Copy).then_inc(self.mid_ready.sem, 1)

    def split_vector(self, dve, i, a, n):
        nc = self.nc
        dve.wait_ge(self.hi_ready.sem, self.hi_ready.at(i, a + 1))
        nc.vector.tensor_tensor(self.rest[:, 0:n, :], self.qk[:, 0:n, :], self.part[0][:, 0:n, :], ALU.subtract
                                ).then_inc(self.rest_ready.sem, 1)
        dve.wait_ge(self.mid_ready.sem, self.mid_ready.at(i, a + 1))
        nc.vector.tensor_tensor(self.part[2][:, 0:n, :], self.rest[:, 0:n, :], self.part[1][:, 0:n, :], ALU.subtract
                                ).then_inc(self.lo_ready.sem, 1)

    def sync(self, sp, i, a, n):
        nc = self.nc
        if a == 0:
            sp.wait_ge(self.s_ready.sem, self.s_ready.at(i, 0))
        sp.wait_ge(self.lo_ready.sem, self.lo_ready.at(i, a + 1))
        sem = self.rows_loaded[a].sem
        sp.dma_start(self.qa[SHIFT:SHIFT + 2, :, :], self.zero[0:2, :].unsqueeze(1).broadcast_to([2, H, S])).then_inc(sem, 16)
        for r in range(PARTS):
            rows = slice(r * DH, (r + 1) * DH)
            sp.dma_start(self.qa[rows, :, :], self.part[Q_PARTS[r]][:, 0, :]).then_inc(sem, 16)
            if n == 2:
                sp.dma_start(self.ka[rows, :, :], self.part[K_PARTS[r]][:, 1, :]).then_inc(sem, 16)
        for g in range(G):
            k = a * G + g
            sp.wait_ge(self.shift_ready.sem, self.shift_ready.at(i, k + 1))
            for w in range(2):
                sp.dma_start(self.qa[SHIFT + w:SHIFT + w + 1, g * HG:(g + 1) * HG, :], self.shift[:, w, :]
                             ).then_inc(self.shift_loaded.sem, 16)

    def tensor(self, pe, i, a, v_ready, v_value):
        nc, bank, K = self.nc, self.bank, self.K
        pe.wait_ge(self.rows_loaded[a].sem, self.rows_loaded[a].at(i, self.loads[a]))

        def max_scores(g, j):
            h = g * HG + j
            for t in range(T):
                k = (a * H + h) * T + t
                out = bank[k % 2]
                w = (t + 1) * P if self.causal else S
                pe.wait_ge(self.m_free.sem, self.m_free.at(i, k - 1))
                last = nc.tensor.matmul(out[:, 0:w], self.qa[:, h, t * P:(t + 1) * P], self.ka[:, h, 0:w], start=True, stop=not self.causal)
                if self.causal:
                    last = nc.tensor.matmul(out[:, t * P:w], self.identb[:, :], self.mask[0][:, :], start=False, stop=True)
                last.then_inc(self.m_ready.sem, 1)

        def max_turn(g):
            pe.wait_ge(self.m_free.sem, self.m_free.at(i, (a * G + g + 1) * HG * T))
            pe.wait_ge(self.misc_free.sem, self.misc_free.at(i, a * (2 * G + 1) + misc[0]))
            misc[0] += 1
            nc.tensor.transpose(bank[7][0:HG * T, 0:P], self.maxima[:, g % 2, :], K("ident")).then_inc(self.maxt_ready.sem, 1)

        def scores(g, j):
            h = g * HG + j
            if j == 0:
                pe.wait_ge(self.shift_loaded.sem, self.shift_loaded.at(i, 2 * (a * G + g + 1)))
            for t in range(T):
                unit = (a * H + h) * self.units + t * self.units // T
                if t % (T // self.units) == 0:
                    pe.wait_ge(self.s_free.sem, self.s_free.at(i, unit + 1 - self.s_free.first))
                q0 = t * P if self.causal else 0
                out = bank[2 + t]
                if not self.causal:
                    out = bank[2 + 2 * (unit % 2) + t % 2]
                last = nc.tensor.matmul(out[:, q0:S], self.ka[:, h, t * P:(t + 1) * P], self.qa[:, h, q0:S], start=True, stop=not self.causal)
                if self.causal:
                    last = nc.tensor.matmul(out[:, q0:q0 + P], self.identb[:, :], self.mask[1][:, :], start=False, stop=True)
                if (t + 1) % (T // self.units) == 0:
                    last.then_inc(self.s_ready.sem, 1)

        def values(g):
            if g == 0:
                pe.wait_ge(v_ready, v_value)
            pe.wait_ge(self.s_free.sem, self.s_free.at(i, (a * G + g + 1) * HG * self.units))
            pe.wait_ge(self.c_copied.sem, self.c_copied.at(i, a * G + g))
            for t in range(T):
                q0 = t * P if self.causal else 0
                for j in range(HG):
                    h = g * HG + j
                    last = nc.tensor.matmul(bank[6][32 * j:32 * (j + 1), q0:S], self.v[:, t, h * 32:(h + 1) * 32],
                                            self.prob[:, g % 2, j, t, q0:S], start=t == 0, stop=t == T - 1)
            last.then_inc(self.pv_ready.sem, 1)
            pe.wait_ge(self.c_copied.sem, self.c_copied.at(i, a * G + g + 1))
            pe.wait_ge(self.misc_free.sem, self.misc_free.at(i, a * (2 * G + 1) + misc[0]))
            misc[0] += 1
            for t in range(T):
                last = nc.tensor.transpose(bank[7][:, t * P:(t + 1) * P], self.c[:, t * P:(t + 1) * P], K("ident"))
            last.then_inc(self.ct_ready.sem, 1)

        misc = [0]
        for g in range(2):
            for j in range(HG):
                max_scores(g, j)
            max_turn(g)
        for g in range(G):
            for j in range(HG):
                if g + 2 < G:
                    max_scores(g + 2, j)
                scores(g, j)
            if g + 2 < G:
                max_turn(g + 2)
            if g:
                values(g - 1)
        values(G - 1)
        pe.wait_ge(self.ctxn_ready.sem, self.ctxn_ready.at(i, a + 1))
        pe.wait_ge(self.misc_free.sem, self.misc_free.at(i, a * (2 * G + 1) + misc[0]))
        for t in range(T):
            last = nc.tensor.transpose(bank[7][:, t * P:(t + 1) * P], self.ctxn[:, t, :], K("ident"))
        last.then_inc(self.ctxt_ready.sem, 1)

    def scalar(self, act, i, a):
        nc = self.nc

        def copy_out(g):
            act.wait_ge(self.pv_ready.sem, self.pv_ready.at(i, a * G + g + 1))
            act.wait_ge(self.ct_ready.sem, self.ct_ready.at(i, a * G + g))
            nc.scalar.activation(self.c[:, :], self.bank[6], ACT.Copy).then_inc(self.c_copied.sem, 1)

        for g in range(G):
            act.wait_ge(self.pv_ready.sem, self.pv_ready.at(i, a * G + g - 1))
            for j in range(HG):
                h = g * HG + j
                for u in range(self.units):
                    unit = (a * H + h) * self.units + u
                    act.wait_ge(self.s_ready.sem, self.s_ready.at(i, unit + 1))
                    if self.causal:
                        out = self.prob[:, g % 2, j, u, u * P:S]
                        src = self.ps[:, 2 + u, u * P:S]
                    else:
                        out = self.prob[:, g % 2, j, 2 * u:2 * u + 2, :]
                        src = self.ps[:, 2 + 2 * (unit % 2):4 + 2 * (unit % 2), :]
                    nc.scalar.activation(out, src, ACT.Exp, scale=SCALE).then_inc(self.s_free.sem, 1)
            if g:
                copy_out(g - 1)
        copy_out(G - 1)
        act.wait_ge(self.ctxt_ready.sem, self.ctxt_ready.at(i, a + 1))

    def copy_ctxt(self, act, out):
        self.nc.scalar.activation(out, self.bank[7], ACT.Copy).then_inc(self.ctxt_copied.sem, 1)

    def free_misc(self, act, i, a):
        act.wait_ge(self.ctxt_copied.sem, self.ctxt_copied.at(i, a + 1))
        act.sem_inc(self.misc_free.sem, 1)

    def vector(self, dve, i, a, own):
        nc = self.nc

        def maxima(g):
            for j in range(HG):
                for t in range(T):
                    k = (a * H + g * HG + j) * T + t
                    w = (t + 1) * P if self.causal else S
                    dve.wait_ge(self.m_ready.sem, self.m_ready.at(i, k + 1))
                    nc.vector.reduce_max(self.maxima[:, g % 2, j * T + t:j * T + t + 1], self.bank[k % 2][:, 0:w], X
                                         ).then_inc(self.m_free.sem, 1)
            dve.wait_ge(self.maxt_ready.sem, self.maxt_ready.at(i, a * G + g + 1))
            dve.wait_ge(self.shift_loaded.sem, self.shift_loaded.at(i, 2 * (a * G + g)))
            own.done(nc.vector.tensor_scalar(self.shift[:, 0, :], self.bank[7][0:HG * T, 0:P], -1.0, None, ALU.mult))
            nc.vector.scalar_tensor_tensor(self.shift[:, 1, :], self.bank[7][0:HG * T, 0:P], -1.0, self.shift[:, 0, :], ALU.mult, ALU.subtract
                                           ).then_inc(self.shift_ready.sem, 1)
            dve.wait_ge(self.shift_ready.sem, self.shift_ready.at(i, a * G + g + 1))
            nc.vector.sem_inc(self.misc_free.sem, 1)

        def normed(g):
            dve.wait_ge(self.ct_ready.sem, self.ct_ready.at(i, a * G + g + 1))
            if g == 0:
                dve.wait_ge(self.ctxt_ready.sem, self.ctxt_ready.at(i, a))
            src = self.bank[7].rearrange("p (t j x) -> p t j x", t=T, x=32)
            own.done(nc.vector.reciprocal(self.rsum[:, :, :], src[:, :, :, DH]))
            out = self.ctxn[:, :, g * HG * DH:(g + 1) * HG * DH].rearrange("p t (j d) -> p t j d", d=DH)
            own.done(nc.vector.tensor_tensor(out, src[:, :, :, 0:DH], self.rsum[:, :, :].unsqueeze(3).broadcast_to([P, T, HG, DH]), ALU.mult))
            nc.vector.sem_inc(self.misc_free.sem, 1)

        for g in range(G):
            maxima(g)
        for g in range(G):
            normed(g)
        nc.vector.sem_inc(self.ctxn_ready.sem, 1)


ATTENTION_STEPS = G + 2 * G


def layer0(nc, ctx0, K, ps, bank, x, xnt_d, mem, chosen, xnt2_d, table_d, sum_d):
    with ExitStack() as ctx:
        def sb(name, shape, dt=F32):
            return ctx.enter_context(nc.sbuf_tensor("a_" + name, shape, dt))

        def sig(name, **kw):
            return Signal(ctx0, nc, "a_" + name, **kw)

        xt = sb("xt", [P, S + 2])
        xc = sb("xc", [P, S])
        att = Attention(ctx, ctx0, nc, K, ps, bank, "a", False, 1)

        def row(j, t):
            return att.prob[:, 0, j, t, :]

        def slot(j, t):
            return row(j, t).rearrange("p (t d) -> p t d", t=T)

        x1h = slot(0, 1)
        x1t = row(1, 1)
        gsm = sb("gsm", [P, T, E0])
        pexp = sb("pexp", [P, T, E0])
        gprob = sb("gprob", [P, T, E0])
        gmax = sb("gmax", [P, T])
        gpt = sb("gpt", [P, S])
        acc = sb("acc", [P, T, D])
        hid = att.prob[:, :, :, 0, :]
        stats = sb("stats", [P, T, 6])
        mv = sb("mv", [P, T, 2])
        var = sb("var", [P, T])
        rstd = sb("rstd", [P, T])
        tmp = sb("tmp", [P, T])
        q2 = slot(1, 2)
        qt = row(0, 3)
        ht = att.prob[:, 0, 2, 1:3, :]
        yy = slot(1, 3)
        ss = sb("ss", [P, T])
        xin = sb("xin", [P, T, D])
        xn2 = sb("xn2", [P, T, D])
        xt2 = sb("xt2", [P, S])
        rl = sb("rl", [P, T, E1])
        top = sb("top", [P, T, 8])
        left = sb("left", [P, T, E1])
        wts = sb("wts", [P, T, E1])
        spare_rows = att.prob[:, 0, 0, 0, 0:D + E1]

        zero_ready = sig("zero_ready")
        zero_stored = sig("zero_stored", unit=16)
        edges_ready = sig("edges_ready")
        x_loaded = sig("x_loaded", unit=16)
        conv_ready = sig("conv_ready", first=1)
        xc_ready = sig("xc_ready")
        qkp_ready = sig("qkp_ready")
        vp_ready = sig("vp_ready")
        v_ready = sig("v_ready")
        z_ready = sig("z_ready")
        x1h_ready = sig("x1h_ready")
        x1p_ready = sig("x1p_ready")
        x1t_ready = sig("x1t_ready")
        gate_ready = sig("gate_ready")
        gsm_ready = sig("gsm_ready")
        gexp_ready = sig("gexp_ready")
        gprob_ready = sig("gprob_ready")
        gpp_ready = sig("gpp_ready")
        gpt_ready = sig("gpt_ready")
        base_ready = sig("base_ready")
        acc_ready = sig("acc_ready")
        up_ready = sig("up_ready", per=E0 * FC)
        hid_ready = sig("hid_ready", per=E0 * FC)
        down_ready = sig("down_ready", per=E0)
        down_used = sig("down_used", per=E0)
        mq_ready = sig("mq_ready", first=1)
        mqt_ready = sig("mqt_ready")
        mq2_ready = sig("mq2_ready")
        mqp_ready = sig("mqp_ready")
        mqtt_ready = sig("mqtt_ready")
        mz_ready = sig("mz_ready")
        mtanh_ready = sig("mtanh_ready")
        mh_ready = sig("mh_ready")
        my_ready = sig("my_ready")
        my_copied = sig("my_copied")
        my_squared = sig("my_squared")
        xin_loaded = sig("xin_loaded", unit=16)
        sum_ready = sig("sum_ready")
        xn2_ready = sig("xn2_ready")
        xn2p_ready = sig("xn2p_ready")
        xt2_ready = sig("xt2_ready")
        route_ready = sig("route_ready")
        rl_ready = sig("rl_ready")
        rexp_ready = sig("rexp_ready")
        wts_ready = sig("wts_ready")
        stored = sig("stored", per=4, first=4, unit=16)
        item_done = sig("item_done", first=1)

        def tiled(b):
            return bank[b].rearrange("p (t d) -> p t d", t=T)

        with nc.Block() as block:
            @block.sync
            def _(sp):
                att.setup_sync(sp)
                sp.wait_ge(zero_ready.sem, 1)
                sp.dma_start(table_d[N:ROWS, :], spare_rows).then_inc(zero_stored.sem, 16)
                sp.dma_start(sum_d[N:ROWS, :], spare_rows[:, 0:D]).then_inc(zero_stored.sem, 16)
                sp.wait_ge(zero_stored.sem, 32)
                sp.sem_inc(stored.sem, 64)
                with sp.Fori(0, NB) as b:
                    sp.wait_ge(conv_ready.sem, conv_ready.at(b, 0))
                    sp.wait_ge(mq_ready.sem, mq_ready.at(b, 0))
                    sp.dma_start(xt[:, 1:S + 1], xnt_d[bass.ds(b * P, P), :]).then_inc(x_loaded.sem, 16)
                    sp.wait_ge(item_done.sem, item_done.at(b, 0))
                    sp.dma_start(xin[:, :, :], x[bass.ds(b, 1), :, :].rearrange("o (t p) d -> p (o t) d", p=P)
                                 ).then_inc(xin_loaded.sem, 16)
                    att.sync(sp, b, 0, 2)
                    sp.wait_ge(sum_ready.sem, sum_ready.at(b, 1))
                    sp.dma_start(sum_d[bass.ds(b * S, S), :].rearrange("(t p) d -> p t d", p=P), acc[:, :, :]).then_inc(stored.sem, 16)
                    sp.wait_ge(xn2_ready.sem, xn2_ready.at(b, 1))
                    sp.dma_start(table_d[bass.ds(b * S, S), 0:D].rearrange("(t p) d -> p t d", p=P), xn2[:, :, :]).then_inc(stored.sem, 16)
                    sp.wait_ge(xt2_ready.sem, xt2_ready.at(b, 1))
                    sp.dma_start(xnt2_d[bass.ds(b * P, P), :], xt2[:, :]).then_inc(stored.sem, 16)
                    sp.wait_ge(wts_ready.sem, wts_ready.at(b, 1))
                    sp.dma_start(table_d[bass.ds(b * S, S), D:D + E1].rearrange("(t p) d -> p t d", p=P), wts[:, :, :]).then_inc(stored.sem, 16)
                sp.wait_ge(stored.sem, stored.at(NB, 0))

            @block.tensor
            def _(pe):
                att.setup_tensor(pe)
                pe.sem_inc(conv_ready.sem, 1)
                pe.sem_inc(mq_ready.sem, 1)
                pe.wait_ge(edges_ready.sem, 1)
                with pe.Fori(0, NB) as b:
                    pe.wait_ge(x_loaded.sem, x_loaded.at(b, 1))
                    pe.wait_ge(item_done.sem, item_done.at(b, 0))
                    for tap in range(3):
                        last = nc.tensor.matmul(bank[0], K("conv0", tap * D, D), xt[:, tap:tap + S], start=tap == 0, stop=tap == 2)
                    last.then_inc(conv_ready.sem, 1)
                    pe.wait_ge(xc_ready.sem, xc_ready.at(b, 1))
                    nc.tensor.matmul(bank[1], K("q0"), xc[:, :], start=True, stop=True)
                    nc.tensor.matmul(bank[2], K("k0"), xc[:, :], start=True, stop=True).then_inc(qkp_ready.sem, 1)
                    for t in range(T):
                        last = nc.tensor.matmul(bank[3 + t], xc[:, t * P:(t + 1) * P], K("v0"), start=True, stop=True)
                    last.then_inc(vp_ready.sem, 1)
                    att.tensor(pe, b, 0, v_ready.sem, v_ready.at(b, 1))
                    for t in range(T):
                        last = nc.tensor.matmul(tiled(1)[:, t, :], xt[:, 1 + t * P:1 + (t + 1) * P], K("wq"), start=True, stop=True)
                    last.then_inc(mq_ready.sem, 1)
                    pe.wait_ge(att.ctxt_copied.sem, att.ctxt_copied.at(b, 1))
                    for t in range(T):
                        cols = slice(t * P, (t + 1) * P)
                        nc.tensor.matmul(tiled(0)[:, t, :], att.ctxt[:, cols], K("out0"), start=True, stop=False)
                        nc.tensor.matmul(tiled(0)[:, t, :], xc[:, cols], K("ident"), start=False, stop=False)
                        last = nc.tensor.matmul(tiled(0)[:, t, :], K("ones")[0:1, :], K("outb0")[0:1, :], start=False, stop=True)
                    last.then_inc(z_ready.sem, 1)
                    pe.wait_ge(mq2_ready.sem, mq2_ready.at(b, 1))
                    for t in range(T):
                        last = nc.tensor.transpose(tiled(3)[:, t, :], q2[:, t, :], K("ident"))
                    last.then_inc(mqp_ready.sem, 1)
                    pe.wait_ge(x1h_ready.sem, x1h_ready.at(b, 1))
                    for t in range(T):
                        last = nc.tensor.transpose(tiled(2)[:, t, :], x1h[:, t, :], K("ident"))
                    last.then_inc(x1p_ready.sem, 1)
                    pe.wait_ge(mqtt_ready.sem, mqtt_ready.at(b, 1))
                    for f in range(2):
                        last = nc.tensor.matmul(bank[5 + f], mem[:, f * P:(f + 1) * P], qt[:, :], start=True, stop=True)
                    last.then_inc(mz_ready.sem, 1)
                    pe.wait_ge(x1t_ready.sem, x1t_ready.at(b, 1))
                    for t in range(T):
                        nc.tensor.matmul(bank[4][:, t * E0:(t + 1) * E0], x1t[:, t * P:(t + 1) * P], K("gate0"), start=True, stop=False)
                        last = nc.tensor.matmul(bank[4][:, t * E0:(t + 1) * E0], K("ones")[0:1, :], K("gateb0")[0:1, :], start=False, stop=True)
                    last.then_inc(gate_ready.sem, 1)
                    pe.wait_ge(mh_ready.sem, mh_ready.at(b, 1))
                    for t in range(T):
                        for f in range(2):
                            last = nc.tensor.matmul(tiled(1)[:, t, :], ht[:, f, t * P:(t + 1) * P], mem[:, INTER + f * D:INTER + (f + 1) * D],
                                                    start=f == 0, stop=f == 1)
                    last.then_inc(my_ready.sem, 1)
                    pe.wait_ge(gprob_ready.sem, gprob_ready.at(b, 1))
                    for t in range(T):
                        last = nc.tensor.transpose(bank[7][0:E0, t * P:(t + 1) * P], gprob[:, t, :], K("ident"))
                    last.then_inc(gpp_ready.sem, 1)

                    def up(e):
                        for f in range(FC):
                            u = e * FC + f
                            if u >= 4:
                                pe.wait_ge(hid_ready.sem, hid_ready.at(b, u - 3))
                            nc.tensor.matmul(bank[4 + u % 4], K("up0", e * F0 + f * P, P), x1t[:, :], start=True, stop=True
                                             ).then_inc(up_ready.sem, 1)

                    def down(e):
                        pe.wait_ge(hid_ready.sem, hid_ready.at(b, (e + 1) * FC))
                        if e >= 2:
                            pe.wait_ge(down_used.sem, down_used.at(b, e - 1))
                        for t in range(T):
                            for f in range(FC):
                                last = nc.tensor.matmul(tiled(2 + e % 2)[:, t, :], hid[:, e % 2, f, t * P:(t + 1) * P],
                                                        K("down0", (e * FC + f) * D, D), start=f == 0, stop=f == FC - 1)
                        last.then_inc(down_ready.sem, 1)

                    pe.wait_ge(gpt_ready.sem, gpt_ready.at(b, 1))
                    for t in range(T):
                        nc.tensor.matmul(tiled(0)[:, t, :], x1t[:, t * P:(t + 1) * P], K("ident"), start=True, stop=False)
                        last = nc.tensor.matmul(tiled(0)[:, t, :], gpt[0:E0, t * P:(t + 1) * P], K("downb0")[0:E0, :], start=False, stop=True)
                    last.then_inc(base_ready.sem, 1)
                    up(0)
                    for e in range(E0):
                        if e + 1 < E0:
                            up(e + 1)
                        down(e)
                    pe.wait_ge(xn2_ready.sem, xn2_ready.at(b, 1))
                    for t in range(T):
                        last = nc.tensor.transpose(tiled(0)[:, t, :], xn2[:, t, :], K("ident"))
                    last.then_inc(xn2p_ready.sem, 1)
                    pe.wait_ge(xt2_ready.sem, xt2_ready.at(b, 1))
                    for t in range(T):
                        last = nc.tensor.matmul(bank[1][:, t * E1:(t + 1) * E1], xt2[:, t * P:(t + 1) * P], K("router"), start=True, stop=True)
                    last.then_inc(route_ready.sem, 1)

            @block.scalar
            def _(act):
                att.setup_scalar(act)
                act.wait_ge(zero_stored.sem, 32)
                cols = K("cols0")
                with act.Fori(0, NB) as b:
                    act.wait_ge(conv_ready.sem, conv_ready.at(b, 1))
                    act.wait_ge(item_done.sem, item_done.at(b, 0))
                    nc.scalar.activation(xc[:, :], bank[0], ACT.Identity, bias=cols[:, 0:1]).then_inc(xc_ready.sem, 1)
                    act.wait_ge(qkp_ready.sem, qkp_ready.at(b, 1))
                    att.before_qk(act, b, 0)
                    nc.scalar.activation(att.qk[:, 0, :], bank[1], ACT.Identity, bias=cols[:, 1:2])
                    nc.scalar.activation(att.qk[:, 1, :], bank[2], ACT.Identity, bias=cols[:, 2:3]).then_inc(att.qk_ready.sem, 1)
                    att.split_scalar(act, b, 0, 2)
                    att.scalar(act, b, 0)
                    att.copy_ctxt(act, att.ctxt[:, :])
                    att.free_misc(act, b, 0)
                    act.wait_ge(mq_ready.sem, mq_ready.at(b, 1))
                    nc.scalar.activation(q2[:, :, :], tiled(1), ACT.Tanh, scale=0.5).then_inc(mqt_ready.sem, 1)
                    act.wait_ge(mqp_ready.sem, mqp_ready.at(b, 1))
                    nc.scalar.activation(qt[:, :], bank[3], ACT.Copy).then_inc(mqtt_ready.sem, 1)
                    act.wait_ge(x1p_ready.sem, x1p_ready.at(b, 1))
                    nc.scalar.activation(x1t[:, :], bank[2], ACT.Identity, bias=cols[:, 4:5], scale=cols[:, 3:4]).then_inc(x1t_ready.sem, 1)
                    act.wait_ge(mz_ready.sem, mz_ready.at(b, 1))
                    nc.scalar.activation(ht[:, :, :], ps[:, 5:7, :], ACT.Tanh, scale=0.5).then_inc(mtanh_ready.sem, 1)
                    act.wait_ge(gsm_ready.sem, gsm_ready.at(b, 1))
                    nc.scalar.activation(pexp[:, :, :], gsm[:, :, :], ACT.Exp).then_inc(gexp_ready.sem, 1)
                    act.wait_ge(gpp_ready.sem, gpp_ready.at(b, 1))
                    nc.scalar.activation(gpt[0:E0, :], bank[7][0:E0, :], ACT.Copy).then_inc(gpt_ready.sem, 1)
                    act.wait_ge(my_ready.sem, my_ready.at(b, 1))
                    nc.scalar.activation(yy[:, :, :], tiled(1), ACT.Copy).then_inc(my_copied.sem, 1)
                    act.wait_ge(my_copied.sem, my_copied.at(b, 1))
                    act.wait_ge(stored.sem, stored.at(b, 0))
                    nc.scalar.activation(xn2[:, :, :], yy[:, :, :], ACT.Square).then_inc(my_squared.sem, 1)
                    for e in range(E0):
                        if e >= 2:
                            act.wait_ge(down_ready.sem, down_ready.at(b, e - 1))
                        for f in range(FC):
                            u = e * FC + f
                            act.wait_ge(up_ready.sem, up_ready.at(b, u + 1))
                            nc.scalar.activation(hid[:, e % 2, f, :], bank[4 + u % 4], ACT.Relu, bias=K("upb0", u, 1)).then_inc(hid_ready.sem, 1)
                    act.wait_ge(xn2p_ready.sem, xn2p_ready.at(b, 1))
                    nc.scalar.activation(xt2[:, :], bank[0], ACT.Copy).then_inc(xt2_ready.sem, 1)
                    act.wait_ge(rl_ready.sem, rl_ready.at(b, 1))
                    nc.scalar.activation(rl[:, :, :], rl[:, :, :], ACT.Exp).then_inc(rexp_ready.sem, 1)

            @block.gpsimd
            def _(pool):
                nc.gpsimd.memset(spare_rows, 0.0).then_inc(zero_ready.sem, 1)
                nc.gpsimd.memset(xt[:, 0:1], 0.0)
                nc.gpsimd.memset(xt[:, S + 1:S + 2], 0.0).then_inc(edges_ready.sem, 1)
                att.setup_pool(pool)

            @block.vector
            def _(dve):
                att.setup_vector(dve)
                dve.sem_inc(item_done.sem, 1)
                steps = ATTENTION_STEPS + 3 * NORMALISE_STEPS + 2 * RSQRT_STEPS + 4 + 3 + 5 + 1 + E0 + 3 + 8
                own = Own(ctx0, nc, "a_own", dve, steps)
                with dve.Fori(0, NB) as b:
                    own.start(b)
                    att.split_vector(dve, b, 0, 2)
                    dve.wait_ge(vp_ready.sem, vp_ready.at(b, 1))
                    for t in range(T):
                        last = nc.vector.tensor_tensor(att.v[:, t, :], bank[3 + t], K("vbias0"), ALU.add)
                    last.then_inc(v_ready.sem, 1)
                    att.vector(dve, b, 0, own)

                    dve.wait_ge(mqt_ready.sem, mqt_ready.at(b, 1))
                    own.done(nc.vector.scalar_tensor_tensor(q2[:, :, :], q2[:, :, :], 1.0, tiled(1), ALU.add, ALU.mult))
                    own.done(nc.vector.tensor_tensor(yy[:, :, :], q2[:, :, :], q2[:, :, :], ALU.mult))
                    own.done(nc.vector.tensor_reduce(ss[:, :], yy[:, :, :], X, ALU.add))
                    own.done(nc.vector.tensor_scalar(ss[:, :], ss[:, :], 1.0 / D, 4e-6, ALU.mult, ALU.add))
                    rsqrt(nc, own, rstd[:, :], ss[:, :], tmp[:, :])
                    for t in range(T):
                        last = nc.vector.scalar_tensor_tensor(q2[:, t, :], q2[:, t, :], rstd[:, t:t + 1], K("qnorm"), ALU.mult, ALU.mult)
                    last.then_inc(mq2_ready.sem, 1)

                    dve.wait_ge(z_ready.sem, z_ready.at(b, 1))
                    last = normalise(nc, own, x1h, tiled(0), stats, mv, var[:, :], rstd[:, :], tmp[:, :], 1e-5)
                    last.then_inc(x1h_ready.sem, 1)

                    dve.wait_ge(mtanh_ready.sem, mtanh_ready.at(b, 1))
                    nc.vector.scalar_tensor_tensor(ht[:, :, :], ht[:, :, :], 1.0, ps[:, 5:7, :], ALU.add, ALU.mult).then_inc(mh_ready.sem, 1)

                    dve.wait_ge(gate_ready.sem, gate_ready.at(b, 1))
                    gl = bank[4][:, 0:T * E0].rearrange("p (t e) -> p t e", t=T)
                    own.done(nc.vector.reduce_max(gmax[:, :], gl, X))
                    nc.vector.tensor_tensor(gsm[:, :, :], gl, along(gmax[:, :], E0), ALU.subtract).then_inc(gsm_ready.sem, 1)
                    dve.wait_ge(gexp_ready.sem, gexp_ready.at(b, 1))
                    own.done(nc.vector.tensor_reduce(gmax[:, :], pexp[:, :, :], X, ALU.add))
                    own.done(nc.vector.reciprocal(gmax[:, :], gmax[:, :]))
                    nc.vector.tensor_tensor(gprob[:, :, :], pexp[:, :, :], along(gmax[:, :], E0), ALU.mult).then_inc(gprob_ready.sem, 1)

                    dve.wait_ge(my_squared.sem, my_squared.at(b, 1))
                    own.done(nc.vector.tensor_reduce(ss[:, :], xn2[:, :, :], X, ALU.add))
                    own.done(nc.vector.tensor_scalar(ss[:, :], ss[:, :], 1.0 / D, 4e-6, ALU.mult, ALU.add))
                    rsqrt(nc, own, rstd[:, :], ss[:, :], tmp[:, :])
                    for t in range(T):
                        last = nc.vector.scalar_tensor_tensor(yy[:, t, :], yy[:, t, :], rstd[:, t:t + 1], mem[:, 2 * INTER:2 * INTER + D], ALU.mult, ALU.mult)
                    own.done(last)
                    own.done(nc.vector.tensor_tensor(q2[:, :, :], q2[:, :, :], yy[:, :, :], ALU.add))
                    dve.wait_ge(xin_loaded.sem, xin_loaded.at(b, 1))
                    own.done(nc.vector.tensor_tensor(q2[:, :, :], q2[:, :, :], xin[:, :, :], ALU.add))

                    dve.wait_ge(base_ready.sem, base_ready.at(b, 1))
                    dve.wait_ge(stored.sem, stored.at(b, 0))
                    own.done(nc.vector.tensor_copy(acc[:, :, :], tiled(0)))
                    for e in range(E0):
                        dve.wait_ge(down_ready.sem, down_ready.at(b, e + 1))
                        for t in range(T):
                            last = nc.vector.scalar_tensor_tensor(acc[:, t, :], tiled(2 + e % 2)[:, t, :], gprob[:, t, e:e + 1], acc[:, t, :], ALU.mult, ALU.add)
                        own.done(last)
                        nc.vector.sem_inc(down_used.sem, 1)

                    own.done(normalise(nc, own, x1h, acc, stats, mv, var[:, :], rstd[:, :], tmp[:, :], 1e-5))
                    own.done(nc.vector.tensor_tensor(x1h[:, :, :], x1h[:, :, :], over(K("ln2g"), T), ALU.mult))
                    own.done(nc.vector.tensor_tensor(x1h[:, :, :], x1h[:, :, :], over(K("ln2b"), T), ALU.add))
                    nc.vector.tensor_tensor(acc[:, :, :], x1h[:, :, :], q2[:, :, :], ALU.add).then_inc(sum_ready.sem, 1)
                    dve.wait_ge(sum_ready.sem, sum_ready.at(b, 1))

                    last = normalise(nc, own, xn2, acc, stats, mv, var[:, :], rstd[:, :], tmp[:, :], 1e-5)
                    last.then_inc(xn2_ready.sem, 1)

                    dve.wait_ge(route_ready.sem, route_ready.at(b, 1))
                    lg = bank[1][:, 0:T * E1].rearrange("p (t e) -> p t e", t=T)
                    own.done(nc.vector.reduce_max(gmax[:, :], lg, X))
                    nc.vector.tensor_tensor(rl[:, :, :], lg, along(gmax[:, :], E1), ALU.subtract).then_inc(rl_ready.sem, 1)
                    dve.wait_ge(rexp_ready.sem, rexp_ready.at(b, 1))
                    own.hold(nc)
                    for t in range(T):
                        last = nc.vector.max(top[:, t, :], rl[:, t, :])
                    own.done(last)
                    own.hold(nc)
                    for t in range(T):
                        last = nc.vector.match_replace(left[:, t, :], top[:, t, :], rl[:, t, :], -1.0)
                    own.done(last)
                    own.done(nc.vector.tensor_scalar(left[:, :, :], left[:, :, :], 0.0, None, ALU.is_lt))
                    own.done(nc.vector.tensor_reduce(gmax[:, :], top[:, :, :], X, ALU.add))
                    own.done(nc.vector.reciprocal(gmax[:, :], gmax[:, :]))
                    own.done(nc.vector.tensor_tensor(wts[:, :, :], rl[:, :, :], left[:, :, :], ALU.mult))
                    own.hold(nc)
                    own.done(nc.vector.tensor_copy(chosen[:, bass.ds(b * T * E1, T * E1)], left[:, :, :].rearrange("p t e -> p (t e)")))
                    nc.vector.tensor_tensor(wts[:, :, :], wts[:, :, :], along(gmax[:, :], E1), ALU.mult).then_inc(wts_ready.sem, 1)
                    dve.wait_ge(wts_ready.sem, wts_ready.at(b, 1))
                    nc.vector.sem_inc(item_done.sem, 1)
                    own.end()


Q = 4


def routed(nc, ctx0, K, ps, bank, chosen, gate_up, down, table_d, sum_d):
    with ExitStack() as ctx:
        def sb(name, shape, dt=F32):
            return ctx.enter_context(nc.sbuf_tensor("r_" + name, shape, dt))

        def sig(name, **kw):
            return Signal(ctx0, nc, "r_" + name, **kw)

        upto = sb("upto", [P, P], BF16)
        pick = sb("pick", [P, Q, NT], BF16)
        total = sb("total", [P, Q])
        excl = sb("excl", [NT, Q])
        incl = sb("incl", [NT, Q])
        count = sb("count", [NT, Q, P], BF16)
        onehot = sb("onehot", [NT, Q, CAP], BF16)
        passed = sb("passed", [NT, Q, CAP], BF16)
        onesb = sb("onesb", [NT, 1], BF16)
        below = sb("below", [P, Q, P])
        slot = sb("slot", [P, Q])
        token = sb("token", [P, Q])
        tiles_before = sb("tiles_before", [P, Q])
        index = sb("index", [P, Q], I32)
        row = sb("row", [P, Q, D + E1])
        rt = sb("rt", [P, Q, P])
        wgu = [sb(f"wgu{u}", [P, Q, 2 * F1]) for u in range(2)]
        wdn = [sb(f"wdn{u}", [F1, Q, D]) for u in range(2)]
        th = sb("th", [P, Q, F1])
        h = sb("h", [P, Q, F1])
        ht = sb("ht", [F1, Q, P])
        share = sb("share", [P, Q, 1])
        out = sb("out", [P, Q, D])
        still = sb("still", [P, 2])

        held = sig("held", per=Q + 1, first=1)
        zeroed = sig("zeroed")
        upto_ready = sig("upto_ready")
        loaded = [sig(f"loaded{u}", per=2, unit=16) for u in range(2)]
        pick_ready = sig("pick_ready")
        local_ready = sig("local_ready")
        total_ready = sig("total_ready")
        excl_ready = sig("excl_ready")
        hot_ready = sig("hot_ready")
        sel_ready = sig("sel_ready")
        index_ready = sig("index_ready")
        gathered = sig("gathered", per=Q, unit=16)
        rt_ready = sig("rt_ready")
        rt_copied = sig("rt_copied")
        gu_ready = sig("gu_ready")
        tanh_ready = sig("tanh_ready")
        h_ready = sig("h_ready")
        ht_ready = sig("ht_ready")
        ht_copied = sig("ht_copied")
        eo_ready = sig("eo_ready", first=1)
        out_ready = sig("out_ready")
        added = sig("added", per=Q, unit=16)
        round_done = sig("round_done", first=1)

        local_ps = bank[0].rearrange("p (q s) -> p q s", q=Q)
        excl_ps = bank[1][0:NT, 0:Q]
        sel_ps = bank[2].rearrange("p (q s) -> p q s", q=Q)
        tiles_ps = bank[3][:, 0:Q]
        rt_ps = bank[4].rearrange("p (q s) -> p q s", q=Q)
        gu_ps = ps[:, 5:7, :].rearrange("p b (q s) -> p (b q) s", q=2)[:, :, 0:2 * F1]
        ht_ps = bank[7][0:F1, :].rearrange("p (q s) -> p q s", q=Q)
        eo_ps = bank[0].rearrange("p (q s) -> p q s", q=Q)
        LOOPS = E1 // Q

        with nc.Block() as block:
            @block.sync
            def _(sp):
                for u in range(2):
                    sp.dma_start(wgu[u][:, :, :], gate_up[:, u * Q:(u + 1) * Q, :]).then_inc(loaded[u].sem, 16)
                    sp.dma_start(wdn[u][:, :, :], down[:, u * Q:(u + 1) * Q, :]).then_inc(loaded[u].sem, 16)
                with sp.Fori(0, LOOPS // 2 - 1) as pair:
                    for u in range(2):
                        sp.wait_ge(eo_ready.sem, eo_ready.at(pair * 2, u + 1))
                        sp.dma_start(wgu[u][:, :, :], gate_up[:, bass.ds(pair * (2 * Q) + (2 + u) * Q, Q), :]).then_inc(loaded[u].sem, 16)
                        sp.dma_start(wdn[u][:, :, :], down[:, bass.ds(pair * (2 * Q) + (2 + u) * Q, Q), :]).then_inc(loaded[u].sem, 16)

            @block.tensor
            def _(pe):
                pe.wait_ge(upto_ready.sem, 1)
                pe.sem_inc(eo_ready.sem, 1)
                with pe.Fori(0, LOOPS // 2) as pair:
                    g = pair * 2
                    for u in range(2):
                        pe.wait_ge(pick_ready.sem, pick_ready.at(g, u + 1))
                        for q in range(Q):
                            last = nc.tensor.matmul(local_ps[0:NT, q, :], pick[:, q, :], upto[:, :], start=True, stop=True)
                        last.then_inc(local_ready.sem, 1)
                        pe.wait_ge(total_ready.sem, total_ready.at(g, u + 1))
                        nc.tensor.matmul(excl_ps, K("before"), total[:, :], start=True, stop=True).then_inc(excl_ready.sem, 1)
                        pe.wait_ge(hot_ready.sem, hot_ready.at(g, u + 1))
                        for q in range(Q):
                            nc.tensor.matmul(sel_ps[:, q, :], onehot[:, q, :], count[:, q, :], start=True, stop=True)
                        for q in range(Q):
                            last = nc.tensor.matmul(tiles_ps[:, q:q + 1], passed[:, q, :], onesb[:, :], start=True, stop=True)
                        last.then_inc(sel_ready.sem, 1)
                        pe.wait_ge(gathered.sem, gathered.at(g, (u + 1) * Q))
                        for q in range(Q):
                            last = nc.tensor.transpose(rt_ps[:, q, :], row[:, q, 0:D], K("ident"))
                        last.then_inc(rt_ready.sem, 1)
                        pe.wait_ge(rt_copied.sem, rt_copied.at(g, u + 1))
                        pe.wait_ge(loaded[u].sem, pair * 32 + 32)
                        for q in range(Q):
                            last = nc.tensor.matmul(gu_ps[:, q, :], rt[:, q, :], wgu[u][:, q, :], start=True, stop=True)
                        last.then_inc(gu_ready.sem, 1)
                        pe.wait_ge(h_ready.sem, h_ready.at(g, u + 1))
                        for q in range(Q):
                            last = nc.tensor.transpose(ht_ps[:, q, :], h[:, q, :], K("ident"))
                        last.then_inc(ht_ready.sem, 1)
                        pe.wait_ge(ht_copied.sem, ht_copied.at(g, u + 1))
                        for q in range(Q):
                            last = nc.tensor.matmul(eo_ps[:, q, :], ht[:, q, :], wdn[u][:, q, :], start=True, stop=True)
                        last.then_inc(eo_ready.sem, 1)

            @block.scalar
            def _(act):
                with act.Fori(0, LOOPS) as g:
                    act.wait_ge(rt_ready.sem, rt_ready.at(g, 1))
                    nc.scalar.activation(rt[:, :, :], rt_ps, ACT.Copy).then_inc(rt_copied.sem, 1)
                    act.wait_ge(gu_ready.sem, gu_ready.at(g, 1))
                    nc.scalar.activation(th[:, :, :], gu_ps[:, :, 0:F1], ACT.Tanh, scale=0.5).then_inc(tanh_ready.sem, 1)
                    act.wait_ge(ht_ready.sem, ht_ready.at(g, 1))
                    nc.scalar.activation(ht[:, :, :], ht_ps, ACT.Copy).then_inc(ht_copied.sem, 1)

            @block.gpsimd
            def _(pool):
                nc.gpsimd.tensor_copy(upto[:, :], K("upto"))
                nc.gpsimd.memset(still[:, :], 0.0)
                nc.gpsimd.memset(onesb[:, :], 1.0).then_inc(upto_ready.sem, 1)
                pool.wait_ge(upto_ready.sem, 1)
                pool.sem_inc(round_done.sem, 1)

                pool.sem_inc(held.sem, 1)

                def hold(g, k):
                    pool.wait_ge(held.sem, held.at(g, k))
                    nc.gpsimd.tensor_tensor(still[:, 0:1], still[:, 1:2], still[:, 1:2], ALU.add).then_inc(held.sem, 1)

                with pool.Fori(0, LOOPS) as g:
                    pool.wait_ge(index_ready.sem, index_ready.at(g, 1))
                    hold(g, 0)
                    for q in range(Q):
                        nc.gpsimd.indirect_dma_start(out=row[:, q, :], out_offset=None, in_=table_d,
                                                     in_offset=bass.IndirectOffsetOnAxis(ap=index[:, q:q + 1], axis=0)
                                                     ).then_inc(gathered.sem, 16)
                    pool.wait_ge(out_ready.sem, out_ready.at(g, 1))
                    hold(g, 1)
                    for q in range(Q):
                        if q:
                            pool.wait_ge(added.sem, added.at(g, q))
                            hold(g, q + 1)
                        nc.gpsimd.indirect_dma_start(out=sum_d, out_offset=bass.IndirectOffsetOnAxis(ap=index[:, q:q + 1], axis=0),
                                                     in_=out[:, q, :], in_offset=None, compute_op=ALU.add
                                                     ).then_inc(added.sem, 16)
                    pool.wait_ge(added.sem, added.at(g, Q))
                    pool.sem_inc(round_done.sem, 1)

            @block.vector
            def _(dve):
                own = Own(ctx0, nc, "r_own", dve, 14)
                nc.vector.memset(total[:, :], 0.0).then_inc(zeroed.sem, 1)
                dve.wait_ge(zeroed.sem, 1)
                with dve.Fori(0, LOOPS) as g:
                    own.start(g)
                    own.hold(nc)
                    nc.vector.tensor_copy(pick[:, :, :], chosen[:, :].rearrange("p (t e) -> p e t", e=E1)[:, bass.ds(g * Q, Q), :]
                                          ).then_inc(pick_ready.sem, 1)
                    dve.wait_ge(local_ready.sem, local_ready.at(g, 1))
                    nc.vector.tensor_copy(total[0:NT, :], local_ps[0:NT, :, P - 1]).then_inc(total_ready.sem, 1)
                    dve.wait_ge(excl_ready.sem, excl_ready.at(g, 1))
                    own.done(nc.vector.tensor_copy(excl[:, :], excl_ps))
                    own.done(nc.vector.tensor_tensor(incl[:, :], excl[:, :], total[0:NT, :], ALU.add))
                    for q in range(Q):
                        nc.vector.tensor_scalar(count[:, q, :], local_ps[0:NT, q, :], excl[:, q:q + 1], float(CAP + 1), ALU.add, ALU.min)
                        last = nc.vector.tensor_scalar(passed[:, q, :], K("slots")[0:NT, :], incl[:, q:q + 1], None, ALU.is_ge)
                    own.done(last)
                    for q in range(Q):
                        last = nc.vector.tensor_scalar(onehot[:, q, :], K("slots")[0:NT, :], excl[:, q:q + 1], None, ALU.is_ge)
                    own.done(last)
                    nc.vector.tensor_tensor(onehot[:, :, :], onehot[:, :, :], passed[:, :, :], ALU.subtract).then_inc(hot_ready.sem, 1)
                    dve.wait_ge(sel_ready.sem, sel_ready.at(g, 1))
                    own.done(nc.vector.tensor_scalar(tiles_before[:, :], tiles_ps, float(P), None, ALU.mult))
                    own.done(nc.vector.tensor_scalar(below[:, :, :], sel_ps, K("slot"), None, ALU.is_le))
                    own.done(nc.vector.tensor_reduce(slot[:, :], below[:, :, :], X, ALU.add))
                    own.done(nc.vector.tensor_tensor(token[:, :], tiles_before[:, :], slot[:, :], ALU.add))
                    own.done(nc.vector.tensor_scalar(token[:, :], token[:, :], K("spare"), None, ALU.min))
                    dve.wait_ge(round_done.sem, round_done.at(g, 0))
                    nc.vector.tensor_copy(index[:, :], token[:, :]).then_inc(index_ready.sem, 1)
                    dve.wait_ge(tanh_ready.sem, tanh_ready.at(g, 1))
                    own.done(nc.vector.scalar_tensor_tensor(th[:, :, :], th[:, :, :], 1.0, gu_ps[:, :, 0:F1], ALU.add, ALU.mult))
                    own.done(nc.vector.tensor_tensor(h[:, :, :], th[:, :, :], gu_ps[:, :, F1:2 * F1], ALU.mult))
                    nc.vector.sem_inc(h_ready.sem, 1)
                    own.hold(nc)
                    for q in range(Q):
                        last = nc.vector.tensor_copy(share[:, q, :], row[:, q, bass.ds(g * Q + (D + q), 1)])
                    own.done(last)
                    own.done(nc.vector.tensor_scalar(share[:, :, :], share[:, :, :], 0.5, None, ALU.mult))
                    dve.wait_ge(eo_ready.sem, eo_ready.at(g, 1))
                    for q in range(Q):
                        last = nc.vector.tensor_scalar(out[:, q, :], eo_ps[:, q, :], share[:, q, :], None, ALU.mult)
                    own.done(last)
                    nc.vector.sem_inc(out_ready.sem, 1)
                    assert own.k == own.per, own.k


def layer1(nc, ctx0, K, ps, bank, xnt2_d, sum_d, result):
    with ExitStack() as ctx:
        def sb(name, shape, dt=F32):
            return ctx.enter_context(nc.sbuf_tensor("b_" + name, shape, dt))

        def sig(name, **kw):
            return Signal(ctx0, nc, "b_" + name, **kw)

        xt = sb("xt", [P, S])
        cpad = sb("cpad", [P, S + 2])
        before = sb("before", [P, T, D])
        res = sb("res", [P, T, D])
        att = Attention(ctx, ctx0, nc, K, ps, bank, "b", True, 2)

        x_loaded = sig("x_loaded", unit=16)
        before_loaded = sig("before_loaded", unit=16)
        edges_ready = sig("edges_ready")
        proj_ready = sig("proj_ready", first=1)
        vp_ready = sig("vp_ready")
        v_ready = sig("v_ready")
        conv_ready = sig("conv_ready")
        out_ready = sig("out_ready")
        res_ready = sig("res_ready", first=1)
        res_stored = sig("res_stored", first=1, unit=16)

        def tiled(b):
            return bank[b].rearrange("p (t d) -> p t d", t=T)

        with nc.Block() as block:
            @block.sync
            def _(sp):
                att.setup_sync(sp)
                sp.sem_inc(res_stored.sem, 16)
                with sp.Fori(0, NB) as b:
                    sp.wait_ge(proj_ready.sem, proj_ready.at(b, 0))
                    sp.dma_start(xt[:, :], xnt2_d[bass.ds(b * P, P), :]).then_inc(x_loaded.sem, 16)
                    sp.wait_ge(res_ready.sem, res_ready.at(b, 0))
                    sp.dma_start(before[:, :, :], sum_d[bass.ds(b * S, S), :].rearrange("(t p) d -> p t d", p=P)
                                 ).then_inc(before_loaded.sem, 16)
                    att.sync(sp, b, 0, 2)
                    att.sync(sp, b, 1, 1)
                    sp.wait_ge(res_ready.sem, res_ready.at(b, 1))
                    sp.dma_start(result[bass.ds(b, 1), :, :].rearrange("o (t p) d -> p (o t) d", p=P), res[:, :, :]
                                 ).then_inc(res_stored.sem, 16)
                sp.wait_ge(res_stored.sem, res_stored.at(NB, 0))

            @block.gpsimd
            def _(pool):
                nc.gpsimd.memset(cpad[:, 0:1], 0.0)
                nc.gpsimd.memset(cpad[:, S + 1:S + 2], 0.0).then_inc(edges_ready.sem, 1)
                att.setup_pool(pool)

            @block.tensor
            def _(pe):
                att.setup_tensor(pe)
                pe.sem_inc(proj_ready.sem, 1)
                pe.wait_ge(edges_ready.sem, 1)
                with pe.Fori(0, NB) as b:
                    pe.wait_ge(x_loaded.sem, x_loaded.at(b, 1))
                    pe.wait_ge(res_ready.sem, res_ready.at(b, 0))
                    nc.tensor.matmul(bank[0], K("q1"), xt[:, :], start=True, stop=True)
                    nc.tensor.matmul(bank[1], K("k1"), xt[:, :], start=True, stop=True).then_inc(proj_ready.sem, 1)
                    for t in range(T):
                        last = nc.tensor.matmul(bank[2 + t], xt[:, t * P:(t + 1) * P], K("v1"), start=True, stop=True)
                    last.then_inc(vp_ready.sem, 1)
                    att.tensor(pe, b, 0, v_ready.sem, v_ready.at(b, 1))
                    pe.wait_ge(att.ctxt_copied.sem, att.ctxt_copied.at(b, 1))
                    for tap in range(3):
                        last = nc.tensor.matmul(bank[0], K("conv1", tap * D, D), cpad[:, tap:tap + S], start=tap == 0, stop=tap == 2)
                    last.then_inc(conv_ready.sem, 1)
                    att.tensor(pe, b, 1, v_ready.sem, v_ready.at(b, 1))
                    pe.wait_ge(att.ctxt_copied.sem, att.ctxt_copied.at(b, 2))
                    for t in range(T):
                        nc.tensor.matmul(tiled(0)[:, t, :], att.ctxt[:, t * P:(t + 1) * P], K("out1"), start=True, stop=False)
                        last = nc.tensor.matmul(tiled(0)[:, t, :], K("ones")[0:1, :], K("outb1")[0:1, :], start=False, stop=True)
                    last.then_inc(out_ready.sem, 1)

            @block.scalar
            def _(act):
                att.setup_scalar(act)
                cols = K("cols1")
                with act.Fori(0, NB) as b:
                    act.wait_ge(proj_ready.sem, proj_ready.at(b, 1))
                    att.before_qk(act, b, 0)
                    nc.scalar.activation(att.qk[:, 0, :], bank[0], ACT.Identity, bias=cols[:, 0:1])
                    nc.scalar.activation(att.qk[:, 1, :], bank[1], ACT.Identity, bias=cols[:, 1:2]).then_inc(att.qk_ready.sem, 1)
                    att.split_scalar(act, b, 0, 2)
                    att.scalar(act, b, 0)
                    att.copy_ctxt(act, cpad[:, 1:S + 1])
                    att.free_misc(act, b, 0)
                    act.wait_ge(conv_ready.sem, conv_ready.at(b, 1))
                    att.before_qk(act, b, 1)
                    nc.scalar.activation(att.qk[:, 0, :], bank[0], ACT.Identity, bias=cols[:, 2:3]).then_inc(att.qk_ready.sem, 1)
                    att.split_scalar(act, b, 1, 1)
                    att.scalar(act, b, 1)
                    act.wait_ge(res_ready.sem, res_ready.at(b, 0))
                    att.copy_ctxt(act, att.ctxt[:, :])
                    att.free_misc(act, b, 1)

            @block.vector
            def _(dve):
                att.setup_vector(dve)
                dve.sem_inc(res_ready.sem, 1)
                own = Own(ctx0, nc, "b_own", dve, 2 * ATTENTION_STEPS)
                with dve.Fori(0, NB) as b:
                    own.start(b)
                    att.split_vector(dve, b, 0, 2)
                    dve.wait_ge(vp_ready.sem, vp_ready.at(b, 1))
                    for t in range(T):
                        last = nc.vector.tensor_tensor(att.v[:, t, :], bank[2 + t], K("vbias1"), ALU.add)
                    last.then_inc(v_ready.sem, 1)
                    att.vector(dve, b, 0, own)
                    att.split_vector(dve, b, 1, 1)
                    att.vector(dve, b, 1, own)
                    own.end()
                    dve.wait_ge(before_loaded.sem, before_loaded.at(b, 1))
                    dve.wait_ge(res_stored.sem, res_stored.at(b, 0))
                    dve.wait_ge(out_ready.sem, out_ready.at(b, 1))
                    nc.vector.tensor_tensor(res[:, :, :], tiled(0), before[:, :, :], ALU.add).then_inc(res_ready.sem, 1)


def fused(nc, x, shared, memory, layer0_in, layer1_in, gate_up, down, result):
    given = {"shared": shared, "memory": memory, "layer0": layer0_in, "layer1": layer1_in}
    with ExitStack() as ctx:
        consts = {}
        loaded = ctx.enter_context(nc.semaphore("consts_loaded"))
        loaded0 = ctx.enter_context(nc.semaphore("consts0_loaded"))

        def hold(stack, part):
            consts[part] = stack.enter_context(nc.sbuf_tensor("consts_" + part, [P, WIDTH[part]], F32))

        def K(name, offset=0, width=None):
            part, start, w = PLACE[name]
            return consts[part][:, start + offset:start + offset + (w if width is None else width)]

        hold(ctx, "shared")
        mem = ctx.enter_context(nc.sbuf_tensor("mem", [P, 2 * INTER + D], F32))
        chosen = ctx.enter_context(nc.sbuf_tensor("chosen", [P, NT * E1], BF16))
        spare = ctx.enter_context(nc.sbuf_tensor("spare_column", [P, 1], F32))
        Own.column = spare[:, :]
        psum = ctx.enter_context(nc.psum_tensor("psum", [P, 8, 512], F32))
        ps = psum[:, :, :]
        bank = [psum[:, i, :] for i in range(8)]

        xnt_d = nc.dram_tensor("xnt", [NB * P, S], F32, kind="Internal").ap()
        kn_d = nc.dram_tensor("kn", [NC, NB * CHUNK, D], F32, kind="Internal").ap()
        vn_d = nc.dram_tensor("vn", [NC, NB * CHUNK, D], F32, kind="Internal").ap()
        xnt2_d = nc.dram_tensor("xnt2", [NB * P, S], F32, kind="Internal").ap()
        table_d = nc.dram_tensor("table", [ROWS, D + E1], F32, kind="Internal").ap()
        sum_d = nc.dram_tensor("sum", [ROWS, D], F32, kind="Internal").ap()

        with ExitStack() as first:
            hold(first, "layer0")
            with ExitStack() as start:
                hold(start, "memory")
                memw1 = start.enter_context(nc.sbuf_tensor("memw1", [P, INTER], F32))
                R = start.enter_context(nc.sbuf_tensor("gate_parts", [P, 3 * NT], F32))
                with nc.Block() as block:
                    @block.sync
                    def _(sp):
                        for part in ("shared", "memory"):
                            sp.dma_start(consts[part][:, :], given[part]).then_inc(loaded, 16)
                        sp.dma_start(consts["layer0"][:, :], given["layer0"]).then_inc(loaded0, 16)
                        sp.wait_ge(loaded, 32)
                with Semaphores() as sems:
                    project(nc, sems, K, bank, x, xnt_d, kn_d, vn_d, R)
                    sems.clear(nc)
                with Semaphores() as sems:
                    learn(nc, sems, K, ps, bank, kn_d, vn_d, R, mem, memw1)
                    sems.clear(nc)
            with nc.Block() as block:
                @block.sync
                def _(sp):
                    sp.wait_ge(loaded0, 16)
            with Semaphores() as sems:
                layer0(nc, sems, K, ps, bank, x, xnt_d, mem, chosen, xnt2_d, table_d, sum_d)
                sems.clear(nc)
        with ExitStack() as second:
            hold(second, "layer1")
            with nc.Block() as block:
                @block.sync
                def _(sp):
                    sp.dma_start(consts["layer1"][:, :], given["layer1"]).then_inc(loaded, 16)
                    sp.wait_ge(loaded, 48)
            with Semaphores() as sems:
                routed(nc, sems, K, ps, bank, chosen, gate_up, down, table_d, sum_d)
                sems.clear(nc)
            with Semaphores() as sems:
                layer1(nc, sems, K, ps, bank, xnt2_d, sum_d, result)


def pack(inputs):
    import numpy as np

    a = {k: np.asarray(v) for k, v in inputs.items()}
    out = {part: np.zeros((P, width), np.float32) for part, width in WIDTH.items()}

    def put(name, m, offset=0):
        part, start, _ = PLACE[name]
        out[part][:m.shape[0], start + offset:start + offset + m.shape[1]] = m

    def rows(v):
        return np.broadcast_to(v.reshape(1, -1), (P, v.size))

    p = np.arange(P)
    put("ident", np.eye(P, dtype=np.float32))
    put("ones", np.ones((P, P), np.float32))
    for w, name in enumerate(("alpha", "theta", "eta")):
        put("gates", np.concatenate([a[f"L0_attn_{name}_w"].reshape(CHUNK, D)] * 2), w * D)
    for h in range(2):
        put("half", np.broadcast_to(((p // CHUNK) == h).astype(np.float32)[:, None], (P, P)), h * D)
    put("wk", a["L0_attn_wk_w"].T)
    put("wv", a["L0_attn_wv_w"].T)
    put("wq", a["L0_attn_wq_w"].T)
    put("knorm", rows(a["L0_attn_k_norm_w"]))
    put("qnorm", rows(a["L0_attn_q_norm_w"]))
    w1 = a["L0_attn_mem_w1"]
    put("mem", a["L0_attn_mem_w0"].T)
    put("mem", w1.T[0:P], INTER)
    put("mem", w1.T[P:2 * P], INTER + D)
    put("mem", rows(a["L0_attn_mem_ln_w"]), 2 * INTER)
    put("memw1", w1)

    order = np.arange(D).reshape(H, DH).T.reshape(-1)
    for layer, wqkv, bqkv in ((0, a["L0_ffn_wqkv"], a["L0_ffn_bqkv"]), (1, a["L1_attn_Wqkv_w"], a["L1_attn_Wqkv_b"])):
        put(f"q{layer}", wqkv[0:D][order].T)
        put(f"k{layer}", wqkv[D:2 * D][order].T)
        wv = np.zeros((D, H, 32), np.float32)
        bv = np.zeros((H, 32), np.float32)
        wv[:, :, 0:DH] = wqkv[2 * D:].T.reshape(D, H, DH)
        bv[:, 0:DH] = bqkv[2 * D:].reshape(H, DH)
        bv[:, DH] = 1.0
        put(f"v{layer}", wv.reshape(D, -1))
        put(f"vbias{layer}", rows(bv))
    b0, b1 = a["L0_ffn_bqkv"], a["L1_attn_Wqkv_b"]
    conv = a["L0_ffn_conv_w"]
    for tap in range(3):
        put("conv0", conv[:, :, tap].T, tap * D)
        put("conv1", a["L1_attn_conv_w"][order, :, tap].T, tap * D)
    put("cols0", np.stack([a["L0_ffn_conv_b"], b0[0:D][order], b0[D:2 * D][order], a["L0_ffn_ln1_g"], a["L0_ffn_ln1_b"]], 1))
    put("cols1", np.stack([b1[0:D][order], b1[D:2 * D][order], a["L1_attn_conv_b"][order]], 1))
    put("out0", a["L0_ffn_wo"].T)
    put("outb0", a["L0_ffn_bo"].reshape(1, -1))
    put("gate0", a["L0_ffn_gate_w"])
    put("gateb0", a["L0_ffn_gate_b"].reshape(1, -1))
    put("up0", a["L0_ffn_w1"].transpose(1, 0, 2).reshape(D, -1))
    put("upb0", a["L0_ffn_b1"].reshape(E0 * FC, P).T)
    put("down0", a["L0_ffn_w2"].reshape(E0 * FC, P, D).transpose(1, 0, 2).reshape(P, -1))
    put("downb0", a["L0_ffn_b2"])
    put("ln2g", rows(a["L0_ffn_ln2_g"]))
    put("ln2b", rows(a["L0_ffn_ln2_b"]))
    put("out1", a["L1_attn_out_w"].T)
    put("outb1", a["L1_attn_out_b"].reshape(1, -1))
    put("router", a["L1_ffn_gate_weight"].T)
    put("maskq", np.where(p[None, :] > p[:, None], np.float32(NEG), np.float32(0)))
    put("maskk", np.where(p[:, None] > p[None, :], np.float32(NEG), np.float32(0)))
    put("upto", (p[:, None] <= p[None, :]).astype(np.float32))
    q = np.arange(NT)
    put("before", (q[:, None] < q[None, :]).astype(np.float32))
    put("slots", rows(np.arange(CAP, dtype=np.float32)))
    put("slot", p.astype(np.float32)[:, None])
    put("spare", (N + p).astype(np.float32)[:, None])
    return out


def kernel(**inputs):
    import numpy as np
    import concourse.bacc as bacc
    from concourse.bass_utils import run_bass_kernel_spmd

    nc = bacc.Bacc("TRN2", target_bir_lowering=False, num_devices=1)
    arrays = {
        "x": np.ascontiguousarray(inputs["L0_attn_x"]),
        **{f"{part}_in": a for part, a in pack(inputs).items()},
        "gate_up": np.ascontiguousarray(np.asarray(inputs["L1_ffn_gate_up_proj"]).transpose(2, 0, 1)),
        "down": np.ascontiguousarray(np.asarray(inputs["L1_ffn_down_proj"]).transpose(2, 0, 1)),
    }
    args = [nc.dram_tensor(n, a.shape, mybir.dt.from_np(a.dtype), kind="ExternalInput").ap() for n, a in arrays.items()]
    result = nc.dram_tensor("result", (NB, S, D), F32, kind="ExternalOutput").ap()
    fused(nc, *args, result)
    r = run_bass_kernel_spmd(nc, [arrays], core_ids=[0])
    return r.results[0]["result"]
```

```python
from contextlib import ExitStack

import concourse.bass as bass
from concourse import mybir

F32 = mybir.dt.float32
BF16 = mybir.dt.bfloat16
I32 = mybir.dt.int32
ACT = mybir.ActivationFunctionType
ALU = mybir.AluOpType
X = mybir.AxisListType.X

P = 128
D = 128
NB = 16
S = 512
T = S // P
NT = NB * T
N = NB * S
CHUNK = 64
NC = S // CHUNK
CT = NB * CHUNK // P
INTER = 256
H = 16
DH = 8
G = 4
HG = H // G
E0 = 8
F0 = 512
FC = F0 // P
E1 = 32
F1 = 96
CAP = 128
ROWS = N + CAP
SCALE = DH ** -0.5
NEG = -1.0e30
MAGIC = 0x5F3759DF

COLUMNS = {
    "shared": [("ident", D), ("ones", D), ("wq", D), ("qnorm", D)],
    "memory": [("gates", 3 * D), ("half", 2 * D), ("wk", D), ("wv", D), ("knorm", D),
               ("mem", 2 * INTER + D), ("memw1", INTER)],
    "layer0": [("conv0", 3 * D), ("q0", D), ("k0", D), ("v0", G * D), ("vbias0", G * D), ("out0", D),
               ("cols0", 5), ("outb0", D), ("gate0", E0), ("gateb0", E0), ("up0", E0 * F0),
               ("upb0", E0 * FC), ("down0", E0 * F0), ("downb0", D), ("ln2g", D), ("ln2b", D),
               ("router", E1)],
    "layer1": [("q1", D), ("k1", D), ("v1", G * D), ("vbias1", G * D), ("conv1", 3 * D), ("cols1", 3),
               ("out1", D), ("outb1", D), ("maskq", D), ("maskk", D), ("upto", D), ("before", NT),
               ("slots", CAP), ("spare", 1), ("slot", 1)],
}
PLACE = {name: (part, sum(w for _, w in columns[:n]), width)
         for part, columns in COLUMNS.items() for n, (name, width) in enumerate(columns)}
WIDTH = {part: sum(w for _, w in columns) for part, columns in COLUMNS.items()}


class Semaphores(ExitStack):

    def __init__(self):
        super().__init__()
        self.made = []

    def enter_context(self, semaphore):
        self.made.append(super().enter_context(semaphore))
        return self.made[-1]

    def clear(self, nc):
        with nc.Block() as block:
            @block.sync
            def _(sp):
                for sem in self.made:
                    sp.sem_clear(sem)


class Signal:

    def __init__(self, ctx, nc, name, per=1, first=0, unit=1):
        self.sem = ctx.enter_context(nc.semaphore(name))
        self.per, self.first, self.unit = per, first, unit

    def at(self, i, k):
        return i * (self.per * self.unit) + (self.first + k) * self.unit


class Own:

    column = None

    def __init__(self, ctx, nc, name, engine, per, first=0):
        self.sem = ctx.enter_context(nc.semaphore(name))
        self.engine, self.per, self.first, self.k, self.i = engine, per, first, 0, 0

    def start(self, i, k=0):
        self.i, self.k = i, k

    def done(self, instruction):
        self.k += 1
        instruction.then_inc(self.sem, 1)
        self.engine.wait_ge(self.sem, self.i * self.per + (self.first + self.k))

    def hold(self, nc):
        nc.vector.memset(self.column, 0.0)

    def end(self):
        assert self.k == self.per, (self.sem, self.k)


def rsqrt(nc, own, y, v, t):
    own.done(nc.vector.tensor_scalar(y.bitcast(I32), v.bitcast(I32), -0.5, float(MAGIC), ALU.mult, ALU.add))
    for _ in range(3):
        own.done(nc.vector.scalar_tensor_tensor(t, y, -0.5, y, ALU.mult, ALU.mult))
        own.done(nc.vector.tensor_tensor(t, t, v, ALU.mult))
        own.done(nc.vector.scalar_tensor_tensor(y, t, 1.5, y, ALU.add, ALU.mult))


RSQRT_STEPS = 10


def normalise(nc, own, out, src, stats, mv, var, rstd, tmp, eps):
    for t in range(T):
        last = nc.vector.bn_stats(stats[:, t, :], src[:, t, :])
    own.done(last)
    own.hold(nc)
    for t in range(T):
        last = nc.vector.bn_aggr(mv[:, t, :], stats[:, t, :])
    own.done(last)
    own.done(nc.vector.tensor_scalar(var, mv[:, :, 1], eps, None, ALU.add))
    rsqrt(nc, own, rstd, var, tmp)
    for t in range(T):
        last = nc.vector.tensor_scalar(out[:, t, :], src[:, t, :], mv[:, t, 0:1], rstd[:, t:t + 1],
                                       ALU.subtract, ALU.mult)
    return last


NORMALISE_STEPS = 3 + RSQRT_STEPS


def over(ap, n):
    return ap.unsqueeze(1).broadcast_to([P, n, ap.shape[-1]])


def along(ap, n):
    return ap.unsqueeze(2).broadcast_to([P, ap.shape[-1], n])


def project(nc, ctx0, K, bank, x, xnt_d, kn_d, vn_d, R):
    with ExitStack() as ctx:
        def sb(name, shape, dt=F32):
            return ctx.enter_context(nc.sbuf_tensor("p_" + name, shape, dt))

        xin = sb("xin", [P, T, D])
        xn = sb("xn", [P, T, D])
        xt = sb("xt", [P, S])
        tk = sb("tk", [P, T, D])
        tv = sb("tv", [P, T, D])
        sk = sb("sk", [P, T, D])
        sq = sb("sq", [P, T, D])
        kn = sb("kn", [P, T, D])
        vn = sb("vn", [P, T, D])
        prod = sb("prod", [P, 3, T, D])
        stats = sb("stats", [P, T, 6])
        mv = sb("mv", [P, T, 2])
        var = sb("var", [P, T])
        rstd = sb("rstd", [P, T])
        tmp = sb("tmp", [P, T])
        ss = sb("ss", [P, T])

        x_loaded = Signal(ctx0, nc, "p_x_loaded", unit=16)
        x_free = Signal(ctx0, nc, "p_x_free", first=1)
        xn_ready = Signal(ctx0, nc, "p_xn_ready")
        t_ready = Signal(ctx0, nc, "p_t_ready")
        xt_ready = Signal(ctx0, nc, "p_xt_ready")
        kv_ready = Signal(ctx0, nc, "p_kv_ready")
        tanh_ready = Signal(ctx0, nc, "p_tanh_ready")
        kv_free = Signal(ctx0, nc, "p_kv_free", first=1)
        kn_ready = Signal(ctx0, nc, "p_kn_ready")
        vs_ready = Signal(ctx0, nc, "p_vs_ready")
        vn_ready = Signal(ctx0, nc, "p_vn_ready")
        prod_ready = Signal(ctx0, nc, "p_prod_ready")
        prod_free = Signal(ctx0, nc, "p_prod_free", first=1)
        xt_stored = Signal(ctx0, nc, "p_xt_stored", first=1, unit=16)
        kn_stored = Signal(ctx0, nc, "p_kn_stored", first=1, per=T, unit=16)
        vn_stored = Signal(ctx0, nc, "p_vn_stored", first=1, per=T, unit=16)

        def rows_of(table, b, t):
            return table[2 * t:2 * t + 2, bass.ds(b * CHUNK, CHUNK), :]

        with nc.Block() as block:
            @block.sync
            def _(sp):
                sp.sem_inc(xt_stored.sem, 16)
                sp.sem_inc(kn_stored.sem, 16)
                sp.sem_inc(vn_stored.sem, 16)
                with sp.Fori(0, NB) as b:
                    sp.wait_ge(x_free.sem, x_free.at(b, 0))
                    sp.dma_start(xin[:, :, :], x[bass.ds(b, 1), :, :].rearrange("o (t p) d -> p (o t) d", p=P)
                                 ).then_inc(x_loaded.sem, 16)
                    sp.wait_ge(xt_ready.sem, xt_ready.at(b, 1))
                    sp.dma_start(xnt_d[bass.ds(b * P, P), :], xt[:, :]).then_inc(xt_stored.sem, 16)
                    sp.wait_ge(kn_ready.sem, kn_ready.at(b, 1))
                    for t in range(T):
                        sp.dma_start(rows_of(kn_d, b, t), kn[:, t, :]).then_inc(kn_stored.sem, 16)
                    sp.wait_ge(vn_ready.sem, vn_ready.at(b, 1))
                    for t in range(T):
                        sp.dma_start(rows_of(vn_d, b, t), vn[:, t, :]).then_inc(vn_stored.sem, 16)
                sp.wait_ge(xt_stored.sem, xt_stored.at(NB, 0))
                sp.wait_ge(kn_stored.sem, kn_stored.at(NB, 0))
                sp.wait_ge(vn_stored.sem, vn_stored.at(NB, 0))

            @block.tensor
            def _(pe):
                with pe.Fori(0, NB) as b:
                    pe.wait_ge(xn_ready.sem, xn_ready.at(b, 1))
                    for t in range(T):
                        last = nc.tensor.transpose(bank[0][:, t * P:(t + 1) * P], xn[:, t, :], K("ident"))
                    last.then_inc(t_ready.sem, 1)
                    pe.wait_ge(xt_ready.sem, xt_ready.at(b, 1))
                    pe.wait_ge(kv_free.sem, kv_free.at(b, 0))
                    for t in range(T):
                        nc.tensor.matmul(bank[1][:, t * P:(t + 1) * P], xt[:, t * P:(t + 1) * P], K("wk"), start=True, stop=True)
                    for t in range(T):
                        last = nc.tensor.matmul(bank[2][:, t * P:(t + 1) * P], xt[:, t * P:(t + 1) * P], K("wv"), start=True, stop=True)
                    last.then_inc(kv_ready.sem, 1)

            @block.scalar
            def _(act):
                with act.Fori(0, NB) as b:
                    act.wait_ge(t_ready.sem, t_ready.at(b, 1))
                    act.wait_ge(xt_stored.sem, xt_stored.at(b, 0))
                    act.wait_ge(kv_free.sem, kv_free.at(b, 0))
                    nc.scalar.activation(xt[:, :], bank[0][:, :], ACT.Copy).then_inc(xt_ready.sem, 1)
                    act.wait_ge(kv_ready.sem, kv_ready.at(b, 1))
                    nc.scalar.activation(tk[:, :, :], bank[1][:, :].rearrange("p (t d) -> p t d", t=T), ACT.Tanh, scale=0.5)
                    nc.scalar.activation(tv[:, :, :], bank[2][:, :].rearrange("p (t d) -> p t d", t=T), ACT.Tanh, scale=0.5
                                         ).then_inc(tanh_ready.sem, 1)
                    act.wait_ge(vs_ready.sem, vs_ready.at(b, 1))
                    act.wait_ge(vn_stored.sem, vn_stored.at(b, 0))
                    nc.scalar.activation(vn[:, :, :], tv[:, :, :], ACT.Copy, scale=0.5).then_inc(vn_ready.sem, 1)

            @block.gpsimd
            def _(pool):
                with pool.Fori(0, NB) as b:
                    pool.wait_ge(xn_ready.sem, xn_ready.at(b, 1))
                    pool.wait_ge(prod_free.sem, prod_free.at(b, 0))
                    for w in range(3):
                        last = nc.gpsimd.tensor_tensor(prod[:, w], xn[:, :, :], over(K("gates", w * D, D), T), ALU.mult)
                    last.then_inc(prod_ready.sem, 1)

            @block.vector
            def _(dve):
                nc.vector.sem_inc(x_free.sem, 1)
                nc.vector.sem_inc(kv_free.sem, 1)
                nc.vector.sem_inc(prod_free.sem, 1)
                own = Own(ctx0, nc, "p_own", dve, NORMALISE_STEPS + 4 + RSQRT_STEPS)
                with dve.Fori(0, NB) as b:
                    own.start(b)
                    dve.wait_ge(x_loaded.sem, x_loaded.at(b, 1))
                    dve.wait_ge(kv_free.sem, kv_free.at(b, 0))
                    dve.wait_ge(prod_free.sem, prod_free.at(b, 0))
                    last = normalise(nc, own, xn, xin, stats, mv, var[:, :], rstd[:, :], tmp[:, :], 1e-5)
                    last.then_inc(xn_ready.sem, 1)
                    dve.wait_ge(xn_ready.sem, xn_ready.at(b, 1))
                    nc.vector.sem_inc(x_free.sem, 1)
                    dve.wait_ge(tanh_ready.sem, tanh_ready.at(b, 1))
                    nc.vector.scalar_tensor_tensor(tv[:, :, :], tv[:, :, :], 1.0, bank[2][:, :].rearrange("p (t d) -> p t d", t=T), ALU.add, ALU.mult
                                                   ).then_inc(vs_ready.sem, 1)
                    own.done(nc.vector.scalar_tensor_tensor(sk[:, :, :], tk[:, :, :], 1.0, bank[1][:, :].rearrange("p (t d) -> p t d", t=T), ALU.add, ALU.mult))
                    own.done(nc.vector.tensor_tensor(sq[:, :, :], sk[:, :, :], sk[:, :, :], ALU.mult))
                    own.done(nc.vector.tensor_reduce(ss[:, :], sq[:, :, :], X, ALU.add))
                    own.done(nc.vector.tensor_scalar(ss[:, :], ss[:, :], 1.0 / D, 4e-6, ALU.mult, ALU.add))
                    rsqrt(nc, own, rstd[:, :], ss[:, :], tmp[:, :])
                    dve.wait_ge(kn_stored.sem, kn_stored.at(b, 0))
                    for t in range(T):
                        last = nc.vector.scalar_tensor_tensor(kn[:, t, :], sk[:, t, :], rstd[:, t:t + 1], K("knorm"), ALU.mult, ALU.mult)
                    last.then_inc(kn_ready.sem, 1)
                    dve.wait_ge(vn_ready.sem, vn_ready.at(b, 1))
                    dve.wait_ge(kn_ready.sem, kn_ready.at(b, 1))
                    nc.vector.sem_inc(kv_free.sem, 1)
                    dve.wait_ge(prod_ready.sem, prod_ready.at(b, 1))
                    own.hold(nc)
                    for w in range(3):
                        last = nc.vector.tensor_reduce(R[:, bass.ds(b * T + w * NT, T)], prod[:, w], X, ALU.add)
                    last.then_inc(prod_free.sem, 1)
                own.end()
                dve.wait_ge(prod_free.sem, prod_free.at(NB, 0))


def learn(nc, ctx0, K, ps, bank, kn_d, vn_d, R, mem, memw1):
    with ExitStack() as ctx:
        def sb(name, shape, dt=F32):
            return ctx.enter_context(nc.sbuf_tensor("m_" + name, shape, dt))

        M = 2 * INTER + D
        kn = [sb(f"kn{i}", [P, CT, D]) for i in range(2)]
        vn = [sb(f"vn{i}", [P, CT, D]) for i in range(2)]
        kv = sb("kv", [P, CT, D])
        kt = sb("kt", [P, CT * P])
        tz = sb("tz", [P, CT, INTER])
        hid = sb("hid", [P, CT, INTER])
        slope = sb("slope", [P, CT, INTER])
        hs = sb("hs", [P, CT, INTER])
        ht = sb("ht", [P, 2, CT * P])
        ys = sb("ys", [P, CT, D])
        nrm = sb("nrm", [P, CT, D])
        e = sb("e", [P, CT, D])
        en = sb("en", [P, CT, D])
        dn = sb("dn", [P, CT, D])
        dy = sb("dy", [P, CT, D])
        dyt = sb("dyt", [P, CT * P])
        dz = sb("dz", [P, CT, INTER])
        keep = sb("keep", [P, M])
        surp = sb("surp", [P, M])
        sqs = sb("sqs", [P, M])
        logits = sb("logits", [P, 2, 3 * NT])
        tgate = sb("tgate", [P, 2, NT])
        decay = sb("decay", [P, 3, 2, T])
        th = sb("th", [P, NC, CT])
        eta_beta = sb("eta_beta", [P, NC, 2])
        eb = sb("eb", [P, 2])
        ths = sb("ths", [P, CT])
        ss = sb("ss", [P, CT])
        r = sb("r", [P, CT])
        tmp = sb("tmp", [P, CT])
        dot = sb("dot", [P, CT])
        gs = sb("gs", [P, 4])
        tot = sb("tot", [P, 1])
        rt = sb("rt", [P, 1])
        t1 = sb("t1", [P, 1])
        clip = sb("clip", [P, 1])

        def S1(name, **kw):
            return Signal(ctx0, nc, "m_" + name, **kw)

        gate_sums = S1("gate_sums")
        gate_copied = S1("gate_copied")
        gate_means = S1("gate_means")
        gate_tanh = S1("gate_tanh")
        kv_loaded = [S1(f"kv_loaded{i}", per=2, unit=16) for i in range(2)]
        step_done = S1("step_done", first=1)
        kt_ready = S1("kt_ready")
        kt_copied = S1("kt_copied")
        z_ready = S1("z_ready")
        tanh_ready = S1("tanh_ready")
        h_ready = S1("h_ready")
        slope_ready = S1("slope_ready", per=3)
        kv_ready = S1("kv_ready")
        ht_ready = S1("ht_ready")
        ht_copied = S1("ht_copied")
        y_ready = S1("y_ready")
        y_copied = S1("y_copied")
        y_squared = S1("y_squared")
        e_ready = S1("e_ready")
        en_ready = S1("en_ready")
        dy_ready = S1("dy_ready")
        dyt_ready = S1("dyt_ready")
        dyt_copied = S1("dyt_copied")
        dh_ready = S1("dh_ready")
        dz_ready = S1("dz_ready")
        grads_ready = S1("grads_ready")
        squares_ready = S1("squares_ready", per=3)
        part_ready = S1("part_ready")
        norm_ready = S1("norm_ready")
        keep_ready = S1("keep_ready")
        mem_ready = S1("mem_ready")
        w1_ready = S1("w1_ready")
        w1_copied = S1("w1_copied")

        w0t = mem[:, 0:INTER]
        w1t = [mem[:, INTER + f * D:INTER + (f + 1) * D] for f in range(2)]
        ln = mem[:, 2 * INTER:M]

        def tiles(ap, w):
            return ap.rearrange("p (t w) -> p t w", w=w)

        z_ps = ps[:, 0:4, :].rearrange("p b (t w) -> p (b t) w", w=INTER)
        y_ps = ps[:, 0:2, :].rearrange("p b (t w) -> p (b t) w", w=D)
        ht_ps = ps[:, 4:8, :].rearrange("p (f b) w -> p f (b w)", f=2)
        kt_ps = ps[:, 4:6, :].rearrange("p b w -> p (b w)")
        dyt_ps = ps[:, 2:4, :].rearrange("p b w -> p (b w)")
        dh_ps = ps[:, 4:8, :].rearrange("p b (t w) -> p (b t) w", w=INTER)
        g_w = ps[:, 0, :]
        g_ln = ps[:, 1, 0:D]
        norm_ps = ps[:, 2, 0:1]
        w1_ps = ps[:, 3, 0:INTER]

        with nc.Block() as block:
            @block.sync
            def _(sp):
                sp.dma_start(kn[0][:, :, :], kn_d[0].rearrange("(t p) d -> p t d", p=P)).then_inc(kv_loaded[0].sem, 16)
                sp.dma_start(vn[0][:, :, :], vn_d[0].rearrange("(t p) d -> p t d", p=P)).then_inc(kv_loaded[0].sem, 16)
                sp.dma_start(kn[1][:, :, :], kn_d[1].rearrange("(t p) d -> p t d", p=P)).then_inc(kv_loaded[1].sem, 16)
                sp.dma_start(vn[1][:, :, :], vn_d[1].rearrange("(t p) d -> p t d", p=P)).then_inc(kv_loaded[1].sem, 16)
                with sp.Fori(0, NC // 2 - 1) as pair:
                    c = pair * 2
                    for u in range(2):
                        sp.wait_ge(grads_ready.sem, grads_ready.at(c, u + 1))
                        sp.dma_start(kn[u][:, :, :], kn_d[bass.ds(c + (u + 2), 1)].rearrange("o (t p) d -> p (o t) d", p=P)
                                     ).then_inc(kv_loaded[u].sem, 16)
                        sp.dma_start(vn[u][:, :, :], vn_d[bass.ds(c + (u + 2), 1)].rearrange("o (t p) d -> p (o t) d", p=P)
                                     ).then_inc(kv_loaded[u].sem, 16)

            @block.tensor
            def _(pe):
                for h in range(2):
                    last = nc.tensor.matmul(bank[6 + h][:, 0:3 * NT], K("half", h * D, D), R[:, :], start=True, stop=True)
                last.then_inc(gate_sums.sem, 1)
                pe.wait_ge(gate_copied.sem, 1)
                with pe.Fori(0, NC // 2) as pair:
                    c = pair * 2
                    for u in range(2):
                        pe.wait_ge(kv_loaded[u].sem, c * 16 + 32)
                        pe.wait_ge(step_done.sem, step_done.at(c, u))
                        for t in range(CT):
                            last = nc.tensor.transpose(kt_ps[:, t * P:(t + 1) * P], kn[u][:, t, :], K("ident"))
                        last.then_inc(kt_ready.sem, 1)
                        pe.wait_ge(kt_copied.sem, kt_copied.at(c, u + 1))
                        for t in range(CT):
                            last = nc.tensor.matmul(z_ps[:, t, :], kt[:, t * P:(t + 1) * P], w0t, start=True, stop=True)
                        last.then_inc(z_ready.sem, 1)
                        pe.wait_ge(h_ready.sem, h_ready.at(c, u + 1))
                        for f in range(2):
                            for t in range(CT):
                                last = nc.tensor.transpose(ht_ps[:, f, t * P:(t + 1) * P], hid[:, t, f * P:(f + 1) * P], K("ident"))
                        last.then_inc(ht_ready.sem, 1)
                        pe.wait_ge(ht_copied.sem, ht_copied.at(c, u + 1))
                        for t in range(CT):
                            for f in range(2):
                                last = nc.tensor.matmul(y_ps[:, t, :], ht[:, f, t * P:(t + 1) * P], w1t[f], start=f == 0, stop=f == 1)
                        last.then_inc(y_ready.sem, 1)
                        pe.wait_ge(dy_ready.sem, dy_ready.at(c, u + 1))
                        for t in range(CT):
                            last = nc.tensor.transpose(dyt_ps[:, t * P:(t + 1) * P], dy[:, t, :], K("ident"))
                        last.then_inc(dyt_ready.sem, 1)
                        for f in range(2):
                            for t in range(CT):
                                nc.tensor.matmul(g_w[:, INTER + f * D:INTER + (f + 1) * D], hid[:, t, f * P:(f + 1) * P], dy[:, t, :],
                                                 start=t == 0, stop=t == CT - 1)
                        pe.wait_ge(dyt_copied.sem, dyt_copied.at(c, u + 1))
                        for t in range(CT):
                            last = nc.tensor.matmul(dh_ps[:, t, :], dyt[:, t * P:(t + 1) * P], memw1[:, :], start=True, stop=True)
                        last.then_inc(dh_ready.sem, 1)
                        pe.wait_ge(en_ready.sem, en_ready.at(c, u + 1))
                        for t in range(CT):
                            nc.tensor.matmul(g_ln, K("ones"), en[:, t, :], start=t == 0, stop=t == CT - 1)
                        pe.wait_ge(dz_ready.sem, dz_ready.at(c, u + 1))
                        for t in range(CT):
                            last = nc.tensor.matmul(g_w[:, 0:INTER], kn[u][:, t, :], dz[:, t, :], start=t == 0, stop=t == CT - 1)
                        last.then_inc(grads_ready.sem, 1)
                        pe.wait_ge(part_ready.sem, part_ready.at(c, u + 1))
                        nc.tensor.matmul(norm_ps, K("ones"), gs[:, 3:4], start=True, stop=True).then_inc(norm_ready.sem, 1)
                        pe.wait_ge(mem_ready.sem, mem_ready.at(c, u + 1))
                        for f in range(2):
                            last = nc.tensor.transpose(w1_ps[:, f * P:(f + 1) * P], w1t[f], K("ident"))
                        last.then_inc(w1_ready.sem, 1)

            @block.scalar
            def _(act):
                act.wait_ge(gate_sums.sem, 1)
                nc.scalar.activation(logits[:, 0, :], bank[6][:, 0:3 * NT], ACT.Copy)
                nc.scalar.activation(logits[:, 1, :], bank[7][:, 0:3 * NT], ACT.Copy).then_inc(gate_copied.sem, 1)
                act.wait_ge(gate_copied.sem, 1)
                nc.scalar.activation(tgate[:, :, :], logits[:, :, NT:2 * NT], ACT.Tanh, scale=0.5)
                act.wait_ge(gate_means.sem, 1)
                nc.scalar.activation(decay[:, :, :, :], decay[:, :, :, :], ACT.Tanh, scale=0.5 / NB).then_inc(gate_tanh.sem, 1)
                with act.Fori(0, NC // 2) as pair:
                    c = pair * 2
                    for u in range(2):
                        act.wait_ge(kt_ready.sem, kt_ready.at(c, u + 1))
                        nc.scalar.activation(kt[:, :], kt_ps, ACT.Copy).then_inc(kt_copied.sem, 1)
                        act.wait_ge(z_ready.sem, z_ready.at(c, u + 1))
                        nc.scalar.activation(tz[:, :, :], z_ps, ACT.Tanh, scale=0.5).then_inc(tanh_ready.sem, 1)
                        act.wait_ge(ht_ready.sem, ht_ready.at(c, u + 1))
                        nc.scalar.activation(ht[:, :, :], ht_ps, ACT.Copy).then_inc(ht_copied.sem, 1)
                        act.wait_ge(y_ready.sem, y_ready.at(c, u + 1))
                        nc.scalar.activation(ys[:, :, :], y_ps, ACT.Copy).then_inc(y_copied.sem, 1)
                        act.wait_ge(y_copied.sem, y_copied.at(c, u + 1))
                        nc.scalar.activation(nrm[:, :, :], ys[:, :, :], ACT.Square).then_inc(y_squared.sem, 1)
                        act.wait_ge(dyt_ready.sem, dyt_ready.at(c, u + 1))
                        nc.scalar.activation(dyt[:, :], dyt_ps, ACT.Copy).then_inc(dyt_copied.sem, 1)
                        act.wait_ge(grads_ready.sem, grads_ready.at(c, u + 1))
                        nc.scalar.activation(sqs[:, 0:INTER], g_w[:, 0:INTER], ACT.Square, accum_out=gs[:, 0:1]).then_inc(squares_ready.sem, 1)
                        nc.scalar.activation(sqs[:, INTER:2 * INTER], g_w[:, INTER:2 * INTER], ACT.Square, accum_out=gs[:, 1:2]).then_inc(squares_ready.sem, 1)
                        nc.scalar.activation(sqs[:, 2 * INTER:M], g_ln, ACT.Square, accum_out=gs[:, 2:3]).then_inc(squares_ready.sem, 1)
                        act.wait_ge(w1_ready.sem, w1_ready.at(c, u + 1))
                        nc.scalar.activation(memw1[:, :], w1_ps, ACT.Copy).then_inc(w1_copied.sem, 1)

            @block.gpsimd
            def _(pool):
                with pool.Fori(0, NC // 2) as pair:
                    c = pair * 2
                    for u in range(2):
                        pool.wait_ge(kv_loaded[u].sem, c * 16 + 32)
                        pool.wait_ge(step_done.sem, step_done.at(c, u))
                        nc.gpsimd.tensor_tensor(kv[:, :, :], kn[u][:, :, :], vn[u][:, :, :], ALU.subtract).then_inc(kv_ready.sem, 1)
                        pool.wait_ge(h_ready.sem, h_ready.at(c, u + 1))
                        nc.gpsimd.tensor_tensor(hs[:, :, :], hid[:, :, :], tz[:, :, :], ALU.mult).then_inc(slope_ready.sem, 1)
                        nc.gpsimd.tensor_tensor(slope[:, :, :], hid[:, :, :], tz[:, :, :], ALU.add).then_inc(slope_ready.sem, 1)
                        pool.wait_ge(slope_ready.sem, slope_ready.at(c, 3 * u + 2))
                        nc.gpsimd.tensor_tensor(slope[:, :, :], slope[:, :, :], hs[:, :, :], ALU.subtract).then_inc(slope_ready.sem, 1)
                        pool.wait_ge(e_ready.sem, e_ready.at(c, u + 1))
                        nc.gpsimd.tensor_tensor(en[:, :, :], e[:, :, :], nrm[:, :, :], ALU.mult).then_inc(en_ready.sem, 1)

            @block.vector
            def _(dve):
                setup = Own(ctx0, nc, "m_setup", dve, 4)
                setup.start(0)
                setup.done(nc.vector.tensor_copy(mem[:, :], K("mem")))
                setup.done(nc.vector.tensor_copy(memw1[:, :], K("memw1")))
                setup.done(nc.vector.memset(surp[:, :], 0.0))
                dve.wait_ge(gate_copied.sem, 1)
                for g in range(3):
                    last = nc.vector.tensor_reduce(decay[:, g], logits[:, :, g * NT:(g + 1) * NT].rearrange("p h (b t) -> p h t b", t=T), X, ALU.add)
                last.then_inc(gate_means.sem, 1)
                dve.wait_ge(gate_tanh.sem, 1)
                k_th = 0.01 * 0.5 * 2.0 / (NB * CHUNK * D)
                for half in range(2):
                    rows = slice(half * CHUNK, (half + 1) * CHUNK)
                    for h in range(2):
                        src = tgate[rows, h, :].rearrange("p (t b q) -> p t b q", b=2, q=T)[:, :, half, :]
                        dst = th[rows, :, :].rearrange("p (q h) t -> p t h q", h=2)[:, :, h, :]
                        nc.vector.tensor_scalar(dst, src, 1.0, k_th, ALU.add, ALU.mult)
                for h in range(2):
                    dst = eta_beta[:, :, :].rearrange("p (q h) x -> p h q x", h=2)[:, h]
                    nc.vector.tensor_scalar(dst[:, :, 0], decay[:, 2, h, :], 0.5, 0.5, ALU.mult, ALU.add)
                    last = nc.vector.tensor_scalar(dst[:, :, 1], decay[:, 0, h, :], -0.5, 0.5, ALU.mult, ALU.add)
                setup.done(last)
                nc.vector.sem_inc(step_done.sem, 1)
                steps = 21 + 2 * RSQRT_STEPS
                own = Own(ctx0, nc, "m_own", dve, steps)
                with dve.Fori(0, NC // 2) as pair:
                    c = pair * 2
                    for u in range(2):
                        own.start(c)
                        own.k = u * steps
                        own.hold(nc)
                        nc.vector.tensor_copy(eb[:, :], eta_beta[:, bass.ds(c + u, 1), :].rearrange("p o x -> p (o x)"))
                        own.done(nc.vector.tensor_copy(ths[:, :], th[:, bass.ds(c + u, 1), :].rearrange("p o x -> p (o x)")))
                        dve.wait_ge(tanh_ready.sem, tanh_ready.at(c, u + 1))
                        own.done(nc.vector.tensor_scalar(tz[:, :, :], tz[:, :, :], 0.5, 0.5, ALU.mult, ALU.add))
                        nc.vector.tensor_tensor(hid[:, :, :], tz[:, :, :], z_ps, ALU.mult).then_inc(h_ready.sem, 1)
                        own.done(nc.vector.tensor_scalar(keep[:, :], surp[:, :], eb[:, 0:1], None, ALU.mult))
                        dve.wait_ge(y_squared.sem, y_squared.at(c, u + 1))
                        own.done(nc.vector.tensor_reduce(ss[:, :], nrm[:, :, :], X, ALU.add))
                        own.done(nc.vector.tensor_scalar(ss[:, :], ss[:, :], 1.0 / D, 1e-6, ALU.mult, ALU.add))
                        rsqrt(nc, own, r[:, :], ss[:, :], tmp[:, :])
                        own.done(nc.vector.tensor_tensor(nrm[:, :, :], ys[:, :, :], along(r[:, :], D), ALU.mult))
                        own.done(nc.vector.tensor_tensor(e[:, :, :], nrm[:, :, :], over(ln, CT), ALU.mult))
                        dve.wait_ge(kv_ready.sem, kv_ready.at(c, u + 1))
                        own.done(nc.vector.tensor_tensor(e[:, :, :], e[:, :, :], kv[:, :, :], ALU.add))
                        nc.vector.tensor_tensor(e[:, :, :], e[:, :, :], along(ths[:, :], D), ALU.mult).then_inc(e_ready.sem, 1)
                        dve.wait_ge(e_ready.sem, e_ready.at(c, u + 1))
                        own.done(nc.vector.tensor_tensor(dn[:, :, :], e[:, :, :], over(ln, CT), ALU.mult))
                        own.done(nc.vector.tensor_tensor(dy[:, :, :], dn[:, :, :], nrm[:, :, :], ALU.mult))
                        own.done(nc.vector.tensor_reduce(dot[:, :], dy[:, :, :], X, ALU.add))
                        own.done(nc.vector.tensor_scalar(dot[:, :], dot[:, :], 1.0 / D, None, ALU.mult))
                        own.done(nc.vector.tensor_tensor(dy[:, :, :], nrm[:, :, :], along(dot[:, :], D), ALU.mult))
                        own.done(nc.vector.tensor_tensor(dy[:, :, :], dn[:, :, :], dy[:, :, :], ALU.subtract))
                        nc.vector.tensor_tensor(dy[:, :, :], dy[:, :, :], along(r[:, :], D), ALU.mult).then_inc(dy_ready.sem, 1)
                        dve.wait_ge(slope_ready.sem, slope_ready.at(c, 3 * u + 3))
                        dve.wait_ge(dh_ready.sem, dh_ready.at(c, u + 1))
                        nc.vector.tensor_tensor(dz[:, :, :], slope[:, :, :], dh_ps, ALU.mult).then_inc(dz_ready.sem, 1)
                        dve.wait_ge(squares_ready.sem, squares_ready.at(c, 3 * u + 3))
                        own.done(nc.vector.scalar_tensor_tensor(gs[:, 3:4], gs[:, 2:3], 1.0 / P, gs[:, 0:1], ALU.mult, ALU.add))
                        nc.vector.tensor_tensor(gs[:, 3:4], gs[:, 3:4], gs[:, 1:2], ALU.add).then_inc(part_ready.sem, 1)
                        dve.wait_ge(norm_ready.sem, norm_ready.at(c, u + 1))
                        own.done(nc.vector.tensor_scalar(tot[:, :], norm_ps, 1e-36, None, ALU.max))
                        rsqrt(nc, own, rt[:, :], tot[:, :], t1[:, :])
                        own.done(nc.vector.tensor_tensor(rt[:, :], rt[:, :], tot[:, :], ALU.mult))
                        own.done(nc.vector.tensor_scalar(rt[:, :], rt[:, :], 1e-6, None, ALU.add))
                        own.done(nc.vector.reciprocal(clip[:, :], rt[:, :]))
                        own.done(nc.vector.tensor_scalar(clip[:, :], clip[:, :], 1.0, -1.0, ALU.min, ALU.mult))
                        nc.vector.scalar_tensor_tensor(surp[:, 0:2 * INTER], g_w, clip[:, 0:1], keep[:, 0:2 * INTER], ALU.mult, ALU.add)
                        own.done(nc.vector.scalar_tensor_tensor(surp[:, 2 * INTER:M], g_ln, clip[:, 0:1], keep[:, 2 * INTER:M], ALU.mult, ALU.add))
                        nc.vector.scalar_tensor_tensor(mem[:, :], mem[:, :], eb[:, 1:2], surp[:, :], ALU.mult, ALU.add).then_inc(mem_ready.sem, 1)
                        dve.wait_ge(mem_ready.sem, mem_ready.at(c, u + 1))
                        dve.wait_ge(w1_copied.sem, w1_copied.at(c, u + 1))
                        nc.vector.sem_inc(step_done.sem, 1)
                        assert own.k == (u + 1) * steps, own.k
                dve.wait_ge(step_done.sem, step_done.at(NC, 0))


PARTS = 6
Q_PARTS = (0, 0, 0, 1, 1, 2)
K_PARTS = (0, 1, 2, 0, 1, 0)
SHIFT = PARTS * DH


class Attention:

    def __init__(self, ctx, csem, nc, K, ps, bank, name, causal, calls):
        def sb(n, shape, dt=F32):
            return ctx.enter_context(nc.sbuf_tensor(f"{name}_{n}", shape, dt))

        def sig(n, per, first=0, unit=1):
            return Signal(csem, nc, f"{name}_{n}", per=per * calls, first=first, unit=unit)

        self.nc, self.K, self.ps, self.bank, self.causal, self.calls = nc, K, ps, bank, causal, calls
        self.qk = sb("qk", [P, 2, S])
        self.part = [sb(f"part{n}", [P, 2, S], BF16) for n in range(3)]
        self.rest = sb("rest", [P, 2, S])
        self.qa = sb("qa", [P, H, S], BF16)
        self.ka = sb("ka", [P, H, S], BF16)
        self.zero = sb("zero", [2, S], BF16)
        self.one = sb("one", [2, S], BF16)
        self.v = sb("v", [P, T, H * 32])
        self.maxima = sb("maxima", [P, 2, HG * T])
        self.shift = sb("shift", [HG * T, 2, P], BF16)
        self.prob = sb("prob", [P, 2, HG, T, S])
        self.c = sb("c", [P, S])
        self.rsum = sb("rsum", [P, T, HG])
        self.ctxn = sb("ctxn", [P, T, D])
        self.ctxt = sb("ctxt", [P, S])
        if causal:
            self.mask = [sb(f"mask{n}", [P, P], BF16) for n in range(2)]
            self.identb = sb("identb", [P, P], BF16)
        self.units = T if causal else T // 2
        self.setup_done = Signal(csem, nc, f"{name}_setup_done")
        self.ones_loaded = Signal(csem, nc, f"{name}_ones_loaded", unit=16)
        self.qk_ready = sig("qk_ready", 1)
        self.hi_ready = sig("hi_ready", 1)
        self.rest_ready = sig("rest_ready", 1, first=1)
        self.mid_ready = sig("mid_ready", 1)
        self.lo_ready = sig("lo_ready", 1)
        loads = [1 + 2 * PARTS, 1 + PARTS]
        self.loads = loads[:calls]
        self.rows_loaded = [Signal(csem, nc, f"{name}_rows_loaded{a}", per=loads[a], first=1, unit=16)
                            for a in range(calls)]
        self.m_ready = sig("m_ready", H * T)
        self.m_free = sig("m_free", H * T, first=2)
        self.misc_free = sig("misc_free", 2 * G + 1, first=1)
        self.maxt_ready = sig("maxt_ready", G)
        self.shift_ready = sig("shift_ready", G)
        self.shift_loaded = sig("shift_loaded", 2 * G, first=2, unit=16)
        self.s_ready = sig("s_ready", H * self.units, first=1)
        self.s_free = sig("s_free", H * self.units, first=4 * self.units // T)
        self.pv_ready = sig("pv_ready", G, first=2)
        self.c_copied = sig("c_copied", G, first=1)
        self.ct_ready = sig("ct_ready", G, first=1)
        self.ctxn_ready = sig("ctxn_ready", 1)
        self.ctxt_ready = sig("ctxt_ready", 1, first=1)
        self.ctxt_copied = sig("ctxt_copied", 1)

    def setup_pool(self, pool):
        nc = self.nc
        nc.gpsimd.memset(self.qa[:, :, :], 0.0)
        nc.gpsimd.memset(self.ka[:, :, :], 0.0)
        nc.gpsimd.memset(self.zero[:, :], 0.0)
        last = nc.gpsimd.memset(self.one[:, :], 1.0)
        if self.causal:
            nc.gpsimd.tensor_copy(self.mask[0][:, :], self.K("maskq"))
            nc.gpsimd.tensor_copy(self.mask[1][:, :], self.K("maskk"))
            last = nc.gpsimd.tensor_copy(self.identb[:, :], self.K("ident"))
        last.then_inc(self.setup_done.sem, 1)

    def setup_sync(self, sp):
        sp.wait_ge(self.setup_done.sem, 1)
        sp.dma_start(self.ka[SHIFT:SHIFT + 2, :, :], self.one[0:2, :].unsqueeze(1).broadcast_to([2, H, S])
                     ).then_inc(self.ones_loaded.sem, 16)
        for a in range(self.calls):
            sp.sem_inc(self.rows_loaded[a].sem, 16)
        sp.sem_inc(self.shift_loaded.sem, 32)

    def setup_tensor(self, pe):
        pe.sem_inc(self.s_ready.sem, 1)
        pe.sem_inc(self.pv_ready.sem, 2)
        pe.sem_inc(self.ct_ready.sem, 1)
        pe.sem_inc(self.ctxt_ready.sem, 1)
        pe.wait_ge(self.ones_loaded.sem, 16)

    def setup_scalar(self, act):
        act.sem_inc(self.s_free.sem, self.s_free.first)
        act.sem_inc(self.c_copied.sem, 1)

    def setup_vector(self, dve):
        dve.sem_inc(self.rest_ready.sem, 1)
        dve.sem_inc(self.m_free.sem, 2)
        dve.sem_inc(self.misc_free.sem, 1)

    def before_qk(self, act, i, a):
        act.wait_ge(self.rest_ready.sem, self.rest_ready.at(i, a))

    def split_scalar(self, act, i, a, n):
        nc = self.nc
        act.wait_ge(self.qk_ready.sem, self.qk_ready.at(i, a + 1))
        if a:
            act.wait_ge(self.rows_loaded[0].sem, self.rows_loaded[0].at(i, self.loads[0]))
        else:
            act.wait_ge(self.rows_loaded[-1].sem, self.rows_loaded[-1].at(i, 0))
        nc.scalar.activation(self.part[0][:, 0:n, :], self.qk[:, 0:n, :], ACT.Copy).then_inc(self.hi_ready.sem, 1)
        act.wait_ge(self.rest_ready.sem, self.rest_ready.at(i, a + 1))
        nc.scalar.activation(self.part[1][:, 0:n, :], self.rest[:, 0:n, :], ACT.Copy).then_inc(self.mid_ready.sem, 1)

    def split_vector(self, dve, i, a, n):
        nc = self.nc
        dve.wait_ge(self.hi_ready.sem, self.hi_ready.at(i, a + 1))
        nc.vector.tensor_tensor(self.rest[:, 0:n, :], self.qk[:, 0:n, :], self.part[0][:, 0:n, :], ALU.subtract
                                ).then_inc(self.rest_ready.sem, 1)
        dve.wait_ge(self.mid_ready.sem, self.mid_ready.at(i, a + 1))
        nc.vector.tensor_tensor(self.part[2][:, 0:n, :], self.rest[:, 0:n, :], self.part[1][:, 0:n, :], ALU.subtract
                                ).then_inc(self.lo_ready.sem, 1)

    def sync(self, sp, i, a, n):
        nc = self.nc
        if a == 0:
            sp.wait_ge(self.s_ready.sem, self.s_ready.at(i, 0))
        sp.wait_ge(self.lo_ready.sem, self.lo_ready.at(i, a + 1))
        sem = self.rows_loaded[a].sem
        sp.dma_start(self.qa[SHIFT:SHIFT + 2, :, :], self.zero[0:2, :].unsqueeze(1).broadcast_to([2, H, S])).then_inc(sem, 16)
        for r in range(PARTS):
            rows = slice(r * DH, (r + 1) * DH)
            sp.dma_start(self.qa[rows, :, :], self.part[Q_PARTS[r]][:, 0, :]).then_inc(sem, 16)
            if n == 2:
                sp.dma_start(self.ka[rows, :, :], self.part[K_PARTS[r]][:, 1, :]).then_inc(sem, 16)
        for g in range(G):
            k = a * G + g
            sp.wait_ge(self.shift_ready.sem, self.shift_ready.at(i, k + 1))
            for w in range(2):
                sp.dma_start(self.qa[SHIFT + w:SHIFT + w + 1, g * HG:(g + 1) * HG, :], self.shift[:, w, :]
                             ).then_inc(self.shift_loaded.sem, 16)

    def tensor(self, pe, i, a, v_ready, v_value):
        nc, bank, K = self.nc, self.bank, self.K
        pe.wait_ge(self.rows_loaded[a].sem, self.rows_loaded[a].at(i, self.loads[a]))

        def max_scores(g, j):
            h = g * HG + j
            for t in range(T):
                k = (a * H + h) * T + t
                out = bank[k % 2]
                w = (t + 1) * P if self.causal else S
                pe.wait_ge(self.m_free.sem, self.m_free.at(i, k - 1))
                last = nc.tensor.matmul(out[:, 0:w], self.qa[:, h, t * P:(t + 1) * P], self.ka[:, h, 0:w], start=True, stop=not self.causal)
                if self.causal:
                    last = nc.tensor.matmul(out[:, t * P:w], self.identb[:, :], self.mask[0][:, :], start=False, stop=True)
                last.then_inc(self.m_ready.sem, 1)

        def max_turn(g):
            pe.wait_ge(self.m_free.sem, self.m_free.at(i, (a * G + g + 1) * HG * T))
            pe.wait_ge(self.misc_free.sem, self.misc_free.at(i, a * (2 * G + 1) + misc[0]))
            misc[0] += 1
            nc.tensor.transpose(bank[7][0:HG * T, 0:P], self.maxima[:, g % 2, :], K("ident")).then_inc(self.maxt_ready.sem, 1)

        def scores(g, j):
            h = g * HG + j
            if j == 0:
                pe.wait_ge(self.shift_loaded.sem, self.shift_loaded.at(i, 2 * (a * G + g + 1)))
            for t in range(T):
                unit = (a * H + h) * self.units + t * self.units // T
                if t % (T // self.units) == 0:
                    pe.wait_ge(self.s_free.sem, self.s_free.at(i, unit + 1 - self.s_free.first))
                q0 = t * P if self.causal else 0
                out = bank[2 + t]
                if not self.causal:
                    out = bank[2 + 2 * (unit % 2) + t % 2]
                last = nc.tensor.matmul(out[:, q0:S], self.ka[:, h, t * P:(t + 1) * P], self.qa[:, h, q0:S], start=True, stop=not self.causal)
                if self.causal:
                    last = nc.tensor.matmul(out[:, q0:q0 + P], self.identb[:, :], self.mask[1][:, :], start=False, stop=True)
                if (t + 1) % (T // self.units) == 0:
                    last.then_inc(self.s_ready.sem, 1)

        def values(g):
            if g == 0:
                pe.wait_ge(v_ready, v_value)
            pe.wait_ge(self.s_free.sem, self.s_free.at(i, (a * G + g + 1) * HG * self.units))
            pe.wait_ge(self.c_copied.sem, self.c_copied.at(i, a * G + g))
            for t in range(T):
                q0 = t * P if self.causal else 0
                for j in range(HG):
                    h = g * HG + j
                    last = nc.tensor.matmul(bank[6][32 * j:32 * (j + 1), q0:S], self.v[:, t, h * 32:(h + 1) * 32],
                                            self.prob[:, g % 2, j, t, q0:S], start=t == 0, stop=t == T - 1)
            last.then_inc(self.pv_ready.sem, 1)
            pe.wait_ge(self.c_copied.sem, self.c_copied.at(i, a * G + g + 1))
            pe.wait_ge(self.misc_free.sem, self.misc_free.at(i, a * (2 * G + 1) + misc[0]))
            misc[0] += 1
            for t in range(T):
                last = nc.tensor.transpose(bank[7][:, t * P:(t + 1) * P], self.c[:, t * P:(t + 1) * P], K("ident"))
            last.then_inc(self.ct_ready.sem, 1)

        misc = [0]
        for g in range(2):
            for j in range(HG):
                max_scores(g, j)
            max_turn(g)
        for g in range(G):
            for j in range(HG):
                if g + 2 < G:
                    max_scores(g + 2, j)
                scores(g, j)
            if g + 2 < G:
                max_turn(g + 2)
            if g:
                values(g - 1)
        values(G - 1)
        pe.wait_ge(self.ctxn_ready.sem, self.ctxn_ready.at(i, a + 1))
        pe.wait_ge(self.misc_free.sem, self.misc_free.at(i, a * (2 * G + 1) + misc[0]))
        for t in range(T):
            last = nc.tensor.transpose(bank[7][:, t * P:(t + 1) * P], self.ctxn[:, t, :], K("ident"))
        last.then_inc(self.ctxt_ready.sem, 1)

    def scalar(self, act, i, a):
        nc = self.nc

        def copy_out(g):
            act.wait_ge(self.pv_ready.sem, self.pv_ready.at(i, a * G + g + 1))
            act.wait_ge(self.ct_ready.sem, self.ct_ready.at(i, a * G + g))
            nc.scalar.activation(self.c[:, :], self.bank[6], ACT.Copy).then_inc(self.c_copied.sem, 1)

        for g in range(G):
            act.wait_ge(self.pv_ready.sem, self.pv_ready.at(i, a * G + g - 1))
            for j in range(HG):
                h = g * HG + j
                for u in range(self.units):
                    unit = (a * H + h) * self.units + u
                    act.wait_ge(self.s_ready.sem, self.s_ready.at(i, unit + 1))
                    if self.causal:
                        out = self.prob[:, g % 2, j, u, u * P:S]
                        src = self.ps[:, 2 + u, u * P:S]
                    else:
                        out = self.prob[:, g % 2, j, 2 * u:2 * u + 2, :]
                        src = self.ps[:, 2 + 2 * (unit % 2):4 + 2 * (unit % 2), :]
                    nc.scalar.activation(out, src, ACT.Exp, scale=SCALE).then_inc(self.s_free.sem, 1)
            if g:
                copy_out(g - 1)
        copy_out(G - 1)
        act.wait_ge(self.ctxt_ready.sem, self.ctxt_ready.at(i, a + 1))

    def copy_ctxt(self, act, out):
        self.nc.scalar.activation(out, self.bank[7], ACT.Copy).then_inc(self.ctxt_copied.sem, 1)

    def free_misc(self, act, i, a):
        act.wait_ge(self.ctxt_copied.sem, self.ctxt_copied.at(i, a + 1))
        act.sem_inc(self.misc_free.sem, 1)

    def vector(self, dve, i, a, own):
        nc = self.nc

        def maxima(g):
            for j in range(HG):
                for t in range(T):
                    k = (a * H + g * HG + j) * T + t
                    w = (t + 1) * P if self.causal else S
                    dve.wait_ge(self.m_ready.sem, self.m_ready.at(i, k + 1))
                    nc.vector.reduce_max(self.maxima[:, g % 2, j * T + t:j * T + t + 1], self.bank[k % 2][:, 0:w], X
                                         ).then_inc(self.m_free.sem, 1)
            dve.wait_ge(self.maxt_ready.sem, self.maxt_ready.at(i, a * G + g + 1))
            dve.wait_ge(self.shift_loaded.sem, self.shift_loaded.at(i, 2 * (a * G + g)))
            own.done(nc.vector.tensor_scalar(self.shift[:, 0, :], self.bank[7][0:HG * T, 0:P], -1.0, None, ALU.mult))
            nc.vector.scalar_tensor_tensor(self.shift[:, 1, :], self.bank[7][0:HG * T, 0:P], -1.0, self.shift[:, 0, :], ALU.mult, ALU.subtract
                                           ).then_inc(self.shift_ready.sem, 1)
            dve.wait_ge(self.shift_ready.sem, self.shift_ready.at(i, a * G + g + 1))
            nc.vector.sem_inc(self.misc_free.sem, 1)

        def normed(g):
            dve.wait_ge(self.ct_ready.sem, self.ct_ready.at(i, a * G + g + 1))
            if g == 0:
                dve.wait_ge(self.ctxt_ready.sem, self.ctxt_ready.at(i, a))
            src = self.bank[7].rearrange("p (t j x) -> p t j x", t=T, x=32)
            own.done(nc.vector.reciprocal(self.rsum[:, :, :], src[:, :, :, DH]))
            out = self.ctxn[:, :, g * HG * DH:(g + 1) * HG * DH].rearrange("p t (j d) -> p t j d", d=DH)
            own.done(nc.vector.tensor_tensor(out, src[:, :, :, 0:DH], self.rsum[:, :, :].unsqueeze(3).broadcast_to([P, T, HG, DH]), ALU.mult))
            nc.vector.sem_inc(self.misc_free.sem, 1)

        for g in range(G):
            maxima(g)
        for g in range(G):
            normed(g)
        nc.vector.sem_inc(self.ctxn_ready.sem, 1)


ATTENTION_STEPS = G + 2 * G


SLOTS = G * T
UNITS = H * T


def copied(engine, i, name):
    register = engine.alloc_register(name)
    engine.reg_mov(register, i)
    return engine.snap(register, min_val=0, max_val=NB)


class TurnAttention:

    def __init__(self, ctx, csem, nc, K, ps, bank, name, causal, turns, s_banks, m_banks, m_slots, loads):
        def sb(n, shape, dt=F32):
            return ctx.enter_context(nc.sbuf_tensor(f"{name}_{n}", shape, dt))

        def sig(n, per, first=0, unit=1):
            return Signal(csem, nc, f"{name}_{n}", per=per * turns, first=first, unit=unit)

        self.name = name
        self.nc, self.K, self.ps, self.bank, self.causal, self.turns = nc, K, ps, bank, causal, turns
        self.s_banks, self.m_banks, self.m_slots, self.loads = s_banks, m_banks, m_slots, loads
        self.qk = sb("qk", [P, 2, S])
        self.part = [sb(f"part{n}", [P, 2, S], BF16) for n in range(3)]
        self.rest = sb("rest", [P, 2, S])
        self.qa = [sb(f"qa{n}", [P, H, S], BF16) for n in range(2)]
        self.ka = [sb(f"ka{n}", [P, H, S], BF16) for n in range(2)]
        self.zero = sb("zero", [2, S], BF16)
        self.one = sb("one", [2, S], BF16)
        self.v = [sb(f"v{n}", [P, T, H * 32]) for n in range(2)]
        self.maxima = sb("maxima", [P, 2, HG * T])
        self.shift = sb("shift", [HG * T, 2, P], BF16)
        self.prob = sb("prob", [P, 2, HG, S])
        self.c = sb("c", [P, S])
        self.rsum = sb("rsum", [P, T, HG])
        self.ctxn = sb("ctxn", [P, T, D])
        if causal:
            self.mask = [sb(f"mask{n}", [P, P], BF16) for n in range(2)]
            self.identb = sb("identb", [P, P], BF16)
        self.setup_done = Signal(csem, nc, f"{name}_setup_done")
        self.ones_loaded = Signal(csem, nc, f"{name}_ones_loaded", unit=16)
        self.qk_ready = sig("qk_ready", 1, first=1)
        self.hi_ready = sig("hi_ready", 1, first=1)
        self.rest_ready = sig("rest_ready", 1, first=2)
        self.mid_ready = sig("mid_ready", 1, first=1)
        self.lo_ready = sig("lo_ready", 1, first=1)
        self.rows_loaded = Signal(csem, nc, f"{name}_rows_loaded", per=sum(loads), first=loads[-1] + 1, unit=16)
        self.m_ready = sig("m_ready", UNITS, first=UNITS)
        self.m_free = sig("m_free", UNITS, first=UNITS + 3)
        self.maxt_ready = sig("maxt_ready", G, first=G)
        self.shift_ready = sig("shift_ready", G, first=G)
        self.shift_loaded = sig("shift_loaded", 2 * G, first=2 * G + 2, unit=16)
        self.s_ready = sig("s_ready", UNITS, first=1)
        self.s_free = sig("s_free", UNITS, first=3)
        self.pv_ready = sig("pv_ready", SLOTS, first=2)
        self.c_copied = sig("c_copied", G, first=1)
        self.ct_ready = sig("ct_ready", G, first=1)
        self.ctxn_ready = sig("ctxn_ready", 1)
        self.ctxt_ready = sig("ctxt_ready", 1, first=1)
        self.misc_free = None
        self.misc_used = 0

    def setup_pool(self, pool):
        nc = self.nc
        for n in range(2):
            nc.gpsimd.memset(self.qa[n][:, :, :], 0.0)
            nc.gpsimd.memset(self.ka[n][:, :, :], 0.0)
        nc.gpsimd.memset(self.zero[:, :], 0.0)
        last = nc.gpsimd.memset(self.one[:, :], 1.0)
        if self.causal:
            nc.gpsimd.tensor_copy(self.mask[0][:, :], self.K("maskq"))
            nc.gpsimd.tensor_copy(self.mask[1][:, :], self.K("maskk"))
            last = nc.gpsimd.tensor_copy(self.identb[:, :], self.K("ident"))
        last.then_inc(self.setup_done.sem, 1)

    def setup_sync(self, sp):
        sp.wait_ge(self.setup_done.sem, 1)
        for n in range(2):
            sp.dma_start(self.ka[n][SHIFT:SHIFT + 2, :, :], self.one[0:2, :].unsqueeze(1).broadcast_to([2, H, S])
                         ).then_inc(self.ones_loaded.sem, 16)
        sp.sem_inc(self.rows_loaded.sem, 16)
        sp.sem_inc(self.shift_loaded.sem, 32)

    def setup_tensor(self, pe):
        pe.sem_inc(self.s_ready.sem, 1)
        pe.sem_inc(self.pv_ready.sem, 2)
        pe.sem_inc(self.ct_ready.sem, 1)
        pe.sem_inc(self.ctxt_ready.sem, 1)
        pe.wait_ge(self.ones_loaded.sem, 32)
        pe.wait_ge(self.setup_done.sem, 1)

    def setup_scalar(self, act):
        act.sem_inc(self.s_free.sem, 3)
        act.sem_inc(self.c_copied.sem, 1)
        act.wait_ge(self.setup_done.sem, 1)

    def setup_vector(self, dve):
        dve.sem_inc(self.rest_ready.sem, 1)
        dve.sem_inc(self.m_free.sem, 3)
        dve.sem_inc(self.misc_free.sem, 1)
        dve.wait_ge(self.setup_done.sem, 1)

    def before_qk(self, act, i, a):
        act.wait_ge(self.rest_ready.sem, self.rest_ready.at(i, a))

    def loaded_before(self, a):
        return sum(self.loads[:a])

    def split_hi(self, act, i, a, n):
        act.wait_ge(self.qk_ready.sem, self.qk_ready.at(i, a + 1))
        act.wait_ge(self.rows_loaded.sem, self.rows_loaded.at(i, self.loaded_before(a)))
        self.nc.scalar.activation(self.part[0][:, 0:n, :], self.qk[:, 0:n, :], ACT.Copy).then_inc(self.hi_ready.sem, 1)

    def split_rest(self, dve, i, a, n):
        dve.wait_ge(self.hi_ready.sem, self.hi_ready.at(i, a + 1))
        self.nc.vector.tensor_tensor(self.rest[:, 0:n, :], self.qk[:, 0:n, :], self.part[0][:, 0:n, :], ALU.subtract
                                     ).then_inc(self.rest_ready.sem, 1)

    def split_mid(self, act, i, a, n):
        act.wait_ge(self.rest_ready.sem, self.rest_ready.at(i, a + 1))
        self.nc.scalar.activation(self.part[1][:, 0:n, :], self.rest[:, 0:n, :], ACT.Copy).then_inc(self.mid_ready.sem, 1)

    def split_lo(self, dve, i, a, n):
        dve.wait_ge(self.mid_ready.sem, self.mid_ready.at(i, a + 1))
        self.nc.vector.tensor_tensor(self.part[2][:, 0:n, :], self.rest[:, 0:n, :], self.part[1][:, 0:n, :], ALU.subtract
                                     ).then_inc(self.lo_ready.sem, 1)

    def load_rows(self, sp, i, a, n):
        b = (a + 1) % 2
        sp.wait_ge(self.lo_ready.sem, self.lo_ready.at(i, a + 1))
        sem = self.rows_loaded.sem
        sp.dma_start(self.qa[b][SHIFT:SHIFT + 2, :, :], self.zero[0:2, :].unsqueeze(1).broadcast_to([2, H, S])).then_inc(sem, 16)
        for r in range(PARTS):
            rows = slice(r * DH, (r + 1) * DH)
            sp.dma_start(self.qa[b][rows, :, :], self.part[Q_PARTS[r]][:, 0, :]).then_inc(sem, 16)
            if n == 2:
                sp.dma_start(self.ka[b][rows, :, :], self.part[K_PARTS[r]][:, 1, :]).then_inc(sem, 16)

    def load_shifts(self, sp, i, a):
        b = (a + 1) % 2
        for g in range(G):
            sp.wait_ge(self.shift_ready.sem, self.shift_ready.at(i, a * G + g + 1))
            for w in range(2):
                sp.dma_start(self.qa[b][SHIFT + w:SHIFT + w + 1, g * HG:(g + 1) * HG, :], self.shift[:, w, :]
                             ).then_inc(self.shift_loaded.sem, 16)

    def wait_misc(self, pe, i):
        pe.wait_ge(self.misc_free.sem, self.misc_free.at(i, self.misc_used))
        self.misc_used += 1

    @staticmethod
    def last_use(k, banks):
        if k >= banks:
            return k - banks
        return max(u for u in range(UNITS) if u % banks == k) - UNITS

    def max_units(self, a, slot):
        return range(*self.m_slots[a][slot])

    def tensor_maxima(self, pe, i, a, k):
        nc, b = self.nc, (a + 1) % 2
        if k == 0:
            pe.wait_ge(self.rows_loaded.sem, self.rows_loaded.at(i, self.loaded_before(a + 1)))
        h, t = divmod(k, T)
        out = self.m_banks[k % len(self.m_banks)]
        w = (t + 1) * P if self.causal else S
        pe.wait_ge(self.m_free.sem, self.m_free.at(i, a * UNITS + self.last_use(k, len(self.m_banks)) + 1))
        last = nc.tensor.matmul(out[:, 0:w], self.qa[b][:, h, t * P:(t + 1) * P], self.ka[b][:, h, 0:w], start=True, stop=not self.causal)
        if self.causal:
            last = nc.tensor.matmul(out[:, t * P:w], self.identb[:, :], self.mask[0][:, :], start=False, stop=True)
        last.then_inc(self.m_ready.sem, 1)

    def tensor_turn_maxima(self, pe, i, a, g):
        pe.wait_ge(self.m_free.sem, self.m_free.at(i, a * UNITS + (g + 1) * HG * T))
        self.wait_misc(pe, i)
        self.nc.tensor.transpose(self.bank[7][0:HG * T, 0:P], self.maxima[:, g % 2, :], self.K("ident")).then_inc(self.maxt_ready.sem, 1)

    def tensor_scores(self, pe, i, a, s, j):
        nc, b = self.nc, a % 2
        g, t = divmod(s, T)
        h, k = g * HG + j, s * HG + j
        if t == 0 and j == 0:
            pe.wait_ge(self.shift_loaded.sem, self.shift_loaded.at(i, 2 * G * (a - 1) + 2 * (g + 1)))
        pe.wait_ge(self.s_free.sem, self.s_free.at(i, a * UNITS + self.last_use(k, len(self.s_banks)) + 1))
        q0 = t * P if self.causal else 0
        out = self.s_banks[k % len(self.s_banks)]
        last = nc.tensor.matmul(out[:, q0:S], self.ka[b][:, h, t * P:(t + 1) * P], self.qa[b][:, h, q0:S], start=True, stop=not self.causal)
        if self.causal:
            last = nc.tensor.matmul(out[:, q0:q0 + P], self.identb[:, :], self.mask[1][:, :], start=False, stop=True)
        last.then_inc(self.s_ready.sem, 1)

    def tensor_values(self, pe, i, a, s):
        nc, b = self.nc, a % 2
        g, t = divmod(s, T)
        pe.wait_ge(self.s_free.sem, self.s_free.at(i, a * UNITS + (s + 1) * HG))
        if t == 0:
            pe.wait_ge(self.c_copied.sem, self.c_copied.at(i, a * G + g))
        q0 = t * P if self.causal else 0
        for j in range(HG):
            h = g * HG + j
            last = nc.tensor.matmul(self.bank[6][32 * j:32 * (j + 1), q0:S], self.v[b][:, t, h * 32:(h + 1) * 32],
                                    self.prob[:, s % 2, j, q0:S], start=t == 0, stop=t == T - 1)
        last.then_inc(self.pv_ready.sem, 1)

    def tensor_turn_context(self, pe, i, a, g):
        pe.wait_ge(self.c_copied.sem, self.c_copied.at(i, a * G + g + 1))
        self.wait_misc(pe, i)
        for t in range(T):
            last = self.nc.tensor.transpose(self.bank[7][:, t * P:(t + 1) * P], self.c[:, t * P:(t + 1) * P], self.K("ident"))
        last.then_inc(self.ct_ready.sem, 1)

    def tensor_whole_context(self, pe, i, a):
        pe.wait_ge(self.ctxn_ready.sem, self.ctxn_ready.at(i, a + 1))
        self.wait_misc(pe, i)
        for t in range(T):
            last = self.nc.tensor.transpose(self.bank[7][:, t * P:(t + 1) * P], self.ctxn[:, t, :], self.K("ident"))
        last.then_inc(self.ctxt_ready.sem, 1)

    def tensor_turn(self, pe, i, a, extra):
        scores_i, maxima_i = copied(pe, i, f"{self.name}_scores{a}"), copied(pe, i, f"{self.name}_maxima{a}")
        for s in range(SLOTS):
            units = list(self.max_units(a, s))
            for j in range(HG):
                for k in units[j * len(units) // HG:(j + 1) * len(units) // HG]:
                    self.tensor_maxima(pe, maxima_i, a, k)
                self.tensor_scores(pe, scores_i, a, s, j)
            if s:
                self.tensor_values(pe, i, a, s - 1)
            elif a:
                self.tensor_values(pe, i, a - 1, SLOTS - 1)
            if s > T and s % T == 1:
                self.tensor_turn_context(pe, i, a, s // T - 1)
            elif s == 1 and a:
                self.tensor_turn_context(pe, i, a - 1, G - 1)
            for g in self.groups_ended(a, s):
                self.tensor_turn_maxima(pe, i, a, g)
            extra(s)

    def tensor_tail(self, pe, i, a):
        self.tensor_values(pe, i, a, SLOTS - 1)
        self.tensor_turn_context(pe, i, a, G - 1)

    def tensor_early(self, pe):
        a = self.turns - 1
        for k in range(UNITS):
            self.tensor_maxima(pe, -1, a, k)
            if (k + 1) % (HG * T) == 0:
                self.tensor_turn_maxima(pe, -1, a, k // (HG * T))

    def groups_ended(self, a, s):
        units = self.max_units(a, s)
        return [g for g in range(G) if (g + 1) * HG * T - 1 in units]

    def scalar_exponentials(self, act, i, a, s, j):
        g, t = divmod(s, T)
        k = s * HG + j
        if j == 0:
            act.wait_ge(self.pv_ready.sem, self.pv_ready.at(i, a * SLOTS + s - 1))
        act.wait_ge(self.s_ready.sem, self.s_ready.at(i, a * UNITS + k + 1))
        q0 = t * P if self.causal else 0
        self.nc.scalar.activation(self.prob[:, s % 2, j, q0:S], self.s_banks[k % len(self.s_banks)][:, q0:S], ACT.Exp, scale=SCALE
                                  ).then_inc(self.s_free.sem, 1)

    def scalar_context(self, act, i, a, g):
        act.wait_ge(self.pv_ready.sem, self.pv_ready.at(i, a * SLOTS + (g + 1) * T))
        act.wait_ge(self.ct_ready.sem, self.ct_ready.at(i, a * G + g))
        self.nc.scalar.activation(self.c[:, :], self.bank[6], ACT.Copy).then_inc(self.c_copied.sem, 1)

    def scalar_turn(self, act, i, a, extra):
        scores_i = copied(act, i, f"{self.name}_scores{a}")
        for s in range(SLOTS):
            for j in range(HG):
                self.scalar_exponentials(act, scores_i, a, s, j)
            if s and s % T == 0:
                self.scalar_context(act, i, a, s // T - 1)
            elif s == 0 and a:
                self.scalar_context(act, i, a - 1, G - 1)
            extra(s)

    def vector_maxima(self, dve, i, a, k):
        t = k % T
        w = (t + 1) * P if self.causal else S
        dve.wait_ge(self.m_ready.sem, self.m_ready.at(i, a * UNITS + k + 1))
        self.nc.vector.reduce_max(self.maxima[:, k // (HG * T) % 2, k % (HG * T):k % (HG * T) + 1], self.m_banks[k % len(self.m_banks)][:, 0:w], X
                                  ).then_inc(self.m_free.sem, 1)

    def vector_shift(self, dve, i, a, g, own):
        nc = self.nc
        dve.wait_ge(self.maxt_ready.sem, self.maxt_ready.at(i, a * G + g + 1))
        dve.wait_ge(self.shift_loaded.sem, self.shift_loaded.at(i, 2 * (a * G + g)))
        own.done(nc.vector.tensor_scalar(self.shift[:, 0, :], self.bank[7][0:HG * T, 0:P], -1.0, None, ALU.mult))
        nc.vector.scalar_tensor_tensor(self.shift[:, 1, :], self.bank[7][0:HG * T, 0:P], -1.0, self.shift[:, 0, :], ALU.mult, ALU.subtract
                                       ).then_inc(self.shift_ready.sem, 1)
        dve.wait_ge(self.shift_ready.sem, self.shift_ready.at(i, a * G + g + 1))
        nc.vector.sem_inc(self.misc_free.sem, 1)

    def vector_context(self, dve, i, a, g, own):
        nc = self.nc
        dve.wait_ge(self.ct_ready.sem, self.ct_ready.at(i, a * G + g + 1))
        if g == 0:
            dve.wait_ge(self.ctxt_ready.sem, self.ctxt_ready.at(i, a))
        src = self.bank[7].rearrange("p (t j x) -> p t j x", t=T, x=32)
        own.done(nc.vector.reciprocal(self.rsum[:, :, :], src[:, :, :, DH]))
        out = self.ctxn[:, :, g * HG * DH:(g + 1) * HG * DH].rearrange("p t (j d) -> p t j d", d=DH)
        own.done(nc.vector.tensor_tensor(out, src[:, :, :, 0:DH], self.rsum[:, :, :].unsqueeze(3).broadcast_to([P, T, HG, DH]), ALU.mult))
        nc.vector.sem_inc(self.misc_free.sem, 1)
        if g == G - 1:
            nc.vector.sem_inc(self.ctxn_ready.sem, 1)


    def vector_turn(self, dve, i, a, own, extra):
        maxima_i = copied(dve, i, f"{self.name}_maxima{a}")
        for s in range(SLOTS):
            for k in self.max_units(a, s):
                self.vector_maxima(dve, maxima_i, a, k)
            if s > T and s % T == 1:
                self.vector_context(dve, i, a, s // T - 1, own)
            elif s == 1 and a:
                self.vector_context(dve, i, a - 1, G - 1, own)
            for g in self.groups_ended(a, s):
                self.vector_shift(dve, i, a, g, own)
            extra(s)

    def vector_early(self, dve, own):
        a = self.turns - 1
        for k in range(UNITS):
            self.vector_maxima(dve, -1, a, k)
            if (k + 1) % (HG * T) == 0:
                self.vector_shift(dve, -1, a, k // (HG * T), own)


SHIFT_STEPS = 1
CONTEXT_STEPS = 2


def spread(first, last=SLOTS):
    n = last - first
    cut = [round(UNITS * max(0, min(n, s - first)) / n) for s in range(SLOTS + 1)]
    return [(cut[s], cut[s + 1]) for s in range(SLOTS)]


def layer0(nc, ctx0, K, ps, bank, x, xnt_d, mem, chosen, xnt2_d, table_d, sum_d):
    with ExitStack() as ctx:
        def sb(name, shape, dt=F32):
            return ctx.enter_context(nc.sbuf_tensor("a_" + name, shape, dt))

        def sig(name, **kw):
            return Signal(ctx0, nc, "a_" + name, **kw)

        xt = sb("xt", [P, S + 2])
        xc = sb("xc", [P, S])
        att = Attention(ctx, ctx0, nc, K, ps, bank, "a", False, 1)

        def row(j, t):
            return att.prob[:, 0, j, t, :]

        def slot(j, t):
            return row(j, t).rearrange("p (t d) -> p t d", t=T)

        x1h = slot(0, 1)
        x1t = row(1, 1)
        gsm = sb("gsm", [P, T, E0])
        pexp = sb("pexp", [P, T, E0])
        gprob = sb("gprob", [P, T, E0])
        gmax = sb("gmax", [P, T])
        gpt = sb("gpt", [P, S])
        acc = sb("acc", [P, T, D])
        hid = att.prob[:, :, :, 0, :]
        stats = sb("stats", [P, T, 6])
        mv = sb("mv", [P, T, 2])
        var = sb("var", [P, T])
        rstd = sb("rstd", [P, T])
        tmp = sb("tmp", [P, T])
        q2 = slot(1, 2)
        qt = row(0, 3)
        ht = att.prob[:, 0, 2, 1:3, :]
        yy = slot(1, 3)
        ss = sb("ss", [P, T])
        xin = sb("xin", [P, T, D])
        xn2 = sb("xn2", [P, T, D])
        xt2 = sb("xt2", [P, S])
        rl = sb("rl", [P, T, E1])
        top = sb("top", [P, T, 8])
        left = sb("left", [P, T, E1])
        wts = sb("wts", [P, T, E1])
        spare_rows = att.prob[:, 0, 0, 0, 0:D + E1]

        zero_ready = sig("zero_ready")
        zero_stored = sig("zero_stored", unit=16)
        edges_ready = sig("edges_ready")
        x_loaded = sig("x_loaded", unit=16)
        conv_ready = sig("conv_ready", first=1)
        xc_ready = sig("xc_ready")
        qkp_ready = sig("qkp_ready")
        vp_ready = sig("vp_ready")
        v_ready = sig("v_ready")
        z_ready = sig("z_ready")
        x1h_ready = sig("x1h_ready")
        x1p_ready = sig("x1p_ready")
        x1t_ready = sig("x1t_ready")
        gate_ready = sig("gate_ready")
        gsm_ready = sig("gsm_ready")
        gexp_ready = sig("gexp_ready")
        gprob_ready = sig("gprob_ready")
        gpp_ready = sig("gpp_ready")
        gpt_ready = sig("gpt_ready")
        base_ready = sig("base_ready")
        acc_ready = sig("acc_ready")
        up_ready = sig("up_ready", per=E0 * FC)
        hid_ready = sig("hid_ready", per=E0 * FC)
        down_ready = sig("down_ready", per=E0)
        down_used = sig("down_used", per=E0)
        mq_ready = sig("mq_ready", first=1)
        mqt_ready = sig("mqt_ready")
        mq2_ready = sig("mq2_ready")
        mqp_ready = sig("mqp_ready")
        mqtt_ready = sig("mqtt_ready")
        mz_ready = sig("mz_ready")
        mtanh_ready = sig("mtanh_ready")
        mh_ready = sig("mh_ready")
        my_ready = sig("my_ready")
        my_copied = sig("my_copied")
        my_squared = sig("my_squared")
        xin_loaded = sig("xin_loaded", unit=16)
        sum_ready = sig("sum_ready")
        xn2_ready = sig("xn2_ready")
        xn2p_ready = sig("xn2p_ready")
        xt2_ready = sig("xt2_ready")
        route_ready = sig("route_ready")
        rl_ready = sig("rl_ready")
        rexp_ready = sig("rexp_ready")
        wts_ready = sig("wts_ready")
        stored = sig("stored", per=4, first=4, unit=16)
        item_done = sig("item_done", first=1)

        def tiled(b):
            return bank[b].rearrange("p (t d) -> p t d", t=T)

        with nc.Block() as block:
            @block.sync
            def _(sp):
                att.setup_sync(sp)
                sp.wait_ge(zero_ready.sem, 1)
                sp.dma_start(table_d[N:ROWS, :], spare_rows).then_inc(zero_stored.sem, 16)
                sp.dma_start(sum_d[N:ROWS, :], spare_rows[:, 0:D]).then_inc(zero_stored.sem, 16)
                sp.wait_ge(zero_stored.sem, 32)
                sp.sem_inc(stored.sem, 64)
                with sp.Fori(0, NB) as b:
                    sp.wait_ge(conv_ready.sem, conv_ready.at(b, 0))
                    sp.wait_ge(mq_ready.sem, mq_ready.at(b, 0))
                    sp.dma_start(xt[:, 1:S + 1], xnt_d[bass.ds(b * P, P), :]).then_inc(x_loaded.sem, 16)
                    sp.wait_ge(item_done.sem, item_done.at(b, 0))
                    sp.dma_start(xin[:, :, :], x[bass.ds(b, 1), :, :].rearrange("o (t p) d -> p (o t) d", p=P)
                                 ).then_inc(xin_loaded.sem, 16)
                    att.sync(sp, b, 0, 2)
                    sp.wait_ge(sum_ready.sem, sum_ready.at(b, 1))
                    sp.dma_start(sum_d[bass.ds(b * S, S), :].rearrange("(t p) d -> p t d", p=P), acc[:, :, :]).then_inc(stored.sem, 16)
                    sp.wait_ge(xn2_ready.sem, xn2_ready.at(b, 1))
                    sp.dma_start(table_d[bass.ds(b * S, S), 0:D].rearrange("(t p) d -> p t d", p=P), xn2[:, :, :]).then_inc(stored.sem, 16)
                    sp.wait_ge(xt2_ready.sem, xt2_ready.at(b, 1))
                    sp.dma_start(xnt2_d[bass.ds(b * P, P), :], xt2[:, :]).then_inc(stored.sem, 16)
                    sp.wait_ge(wts_ready.sem, wts_ready.at(b, 1))
                    sp.dma_start(table_d[bass.ds(b * S, S), D:D + E1].rearrange("(t p) d -> p t d", p=P), wts[:, :, :]).then_inc(stored.sem, 16)
                sp.wait_ge(stored.sem, stored.at(NB, 0))

            @block.tensor
            def _(pe):
                att.setup_tensor(pe)
                pe.sem_inc(conv_ready.sem, 1)
                pe.sem_inc(mq_ready.sem, 1)
                pe.wait_ge(edges_ready.sem, 1)
                with pe.Fori(0, NB) as b:
                    pe.wait_ge(x_loaded.sem, x_loaded.at(b, 1))
                    pe.wait_ge(item_done.sem, item_done.at(b, 0))
                    for tap in range(3):
                        last = nc.tensor.matmul(bank[0], K("conv0", tap * D, D), xt[:, tap:tap + S], start=tap == 0, stop=tap == 2)
                    last.then_inc(conv_ready.sem, 1)
                    pe.wait_ge(xc_ready.sem, xc_ready.at(b, 1))
                    nc.tensor.matmul(bank[1], K("q0"), xc[:, :], start=True, stop=True)
                    nc.tensor.matmul(bank[2], K("k0"), xc[:, :], start=True, stop=True).then_inc(qkp_ready.sem, 1)
                    for t in range(T):
                        last = nc.tensor.matmul(bank[3 + t], xc[:, t * P:(t + 1) * P], K("v0"), start=True, stop=True)
                    last.then_inc(vp_ready.sem, 1)
                    att.tensor(pe, b, 0, v_ready.sem, v_ready.at(b, 1))
                    for t in range(T):
                        last = nc.tensor.matmul(tiled(1)[:, t, :], xt[:, 1 + t * P:1 + (t + 1) * P], K("wq"), start=True, stop=True)
                    last.then_inc(mq_ready.sem, 1)
                    pe.wait_ge(att.ctxt_copied.sem, att.ctxt_copied.at(b, 1))
                    for t in range(T):
                        cols = slice(t * P, (t + 1) * P)
                        nc.tensor.matmul(tiled(0)[:, t, :], att.ctxt[:, cols], K("out0"), start=True, stop=False)
                        nc.tensor.matmul(tiled(0)[:, t, :], xc[:, cols], K("ident"), start=False, stop=False)
                        last = nc.tensor.matmul(tiled(0)[:, t, :], K("ones")[0:1, :], K("outb0")[0:1, :], start=False, stop=True)
                    last.then_inc(z_ready.sem, 1)
                    pe.wait_ge(mq2_ready.sem, mq2_ready.at(b, 1))
                    for t in range(T):
                        last = nc.tensor.transpose(tiled(3)[:, t, :], q2[:, t, :], K("ident"))
                    last.then_inc(mqp_ready.sem, 1)
                    pe.wait_ge(x1h_ready.sem, x1h_ready.at(b, 1))
                    for t in range(T):
                        last = nc.tensor.transpose(tiled(2)[:, t, :], x1h[:, t, :], K("ident"))
                    last.then_inc(x1p_ready.sem, 1)
                    pe.wait_ge(mqtt_ready.sem, mqtt_ready.at(b, 1))
                    for f in range(2):
                        last = nc.tensor.matmul(bank[5 + f], mem[:, f * P:(f + 1) * P], qt[:, :], start=True, stop=True)
                    last.then_inc(mz_ready.sem, 1)
                    pe.wait_ge(x1t_ready.sem, x1t_ready.at(b, 1))
                    for t in range(T):
                        nc.tensor.matmul(bank[4][:, t * E0:(t + 1) * E0], x1t[:, t * P:(t + 1) * P], K("gate0"), start=True, stop=False)
                        last = nc.tensor.matmul(bank[4][:, t * E0:(t + 1) * E0], K("ones")[0:1, :], K("gateb0")[0:1, :], start=False, stop=True)
                    last.then_inc(gate_ready.sem, 1)
                    pe.wait_ge(mh_ready.sem, mh_ready.at(b, 1))
                    for t in range(T):
                        for f in range(2):
                            last = nc.tensor.matmul(tiled(1)[:, t, :], ht[:, f, t * P:(t + 1) * P], mem[:, INTER + f * D:INTER + (f + 1) * D],
                                                    start=f == 0, stop=f == 1)
                    last.then_inc(my_ready.sem, 1)
                    pe.wait_ge(gprob_ready.sem, gprob_ready.at(b, 1))
                    for t in range(T):
                        last = nc.tensor.transpose(bank[7][0:E0, t * P:(t + 1) * P], gprob[:, t, :], K("ident"))
                    last.then_inc(gpp_ready.sem, 1)

                    def up(e):
                        for f in range(FC):
                            u = e * FC + f
                            if u >= 4:
                                pe.wait_ge(hid_ready.sem, hid_ready.at(b, u - 3))
                            nc.tensor.matmul(bank[4 + u % 4], K("up0", e * F0 + f * P, P), x1t[:, :], start=True, stop=True
                                             ).then_inc(up_ready.sem, 1)

                    def down(e):
                        pe.wait_ge(hid_ready.sem, hid_ready.at(b, (e + 1) * FC))
                        if e >= 2:
                            pe.wait_ge(down_used.sem, down_used.at(b, e - 1))
                        for t in range(T):
                            for f in range(FC):
                                last = nc.tensor.matmul(tiled(2 + e % 2)[:, t, :], hid[:, e % 2, f, t * P:(t + 1) * P],
                                                        K("down0", (e * FC + f) * D, D), start=f == 0, stop=f == FC - 1)
                        last.then_inc(down_ready.sem, 1)

                    pe.wait_ge(gpt_ready.sem, gpt_ready.at(b, 1))
                    for t in range(T):
                        nc.tensor.matmul(tiled(0)[:, t, :], x1t[:, t * P:(t + 1) * P], K("ident"), start=True, stop=False)
                        last = nc.tensor.matmul(tiled(0)[:, t, :], gpt[0:E0, t * P:(t + 1) * P], K("downb0")[0:E0, :], start=False, stop=True)
                    last.then_inc(base_ready.sem, 1)
                    up(0)
                    for e in range(E0):
                        if e + 1 < E0:
                            up(e + 1)
                        down(e)
                    pe.wait_ge(xn2_ready.sem, xn2_ready.at(b, 1))
                    for t in range(T):
                        last = nc.tensor.transpose(tiled(0)[:, t, :], xn2[:, t, :], K("ident"))
                    last.then_inc(xn2p_ready.sem, 1)
                    pe.wait_ge(xt2_ready.sem, xt2_ready.at(b, 1))
                    for t in range(T):
                        last = nc.tensor.matmul(bank[1][:, t * E1:(t + 1) * E1], xt2[:, t * P:(t + 1) * P], K("router"), start=True, stop=True)
                    last.then_inc(route_ready.sem, 1)

            @block.scalar
            def _(act):
                att.setup_scalar(act)
                act.wait_ge(zero_stored.sem, 32)
                cols = K("cols0")
                with act.Fori(0, NB) as b:
                    act.wait_ge(conv_ready.sem, conv_ready.at(b, 1))
                    act.wait_ge(item_done.sem, item_done.at(b, 0))
                    nc.scalar.activation(xc[:, :], bank[0], ACT.Identity, bias=cols[:, 0:1]).then_inc(xc_ready.sem, 1)
                    act.wait_ge(qkp_ready.sem, qkp_ready.at(b, 1))
                    att.before_qk(act, b, 0)
                    nc.scalar.activation(att.qk[:, 0, :], bank[1], ACT.Identity, bias=cols[:, 1:2])
                    nc.scalar.activation(att.qk[:, 1, :], bank[2], ACT.Identity, bias=cols[:, 2:3]).then_inc(att.qk_ready.sem, 1)
                    att.split_scalar(act, b, 0, 2)
                    att.scalar(act, b, 0)
                    att.copy_ctxt(act, att.ctxt[:, :])
                    att.free_misc(act, b, 0)
                    act.wait_ge(mq_ready.sem, mq_ready.at(b, 1))
                    nc.scalar.activation(q2[:, :, :], tiled(1), ACT.Tanh, scale=0.5).then_inc(mqt_ready.sem, 1)
                    act.wait_ge(mqp_ready.sem, mqp_ready.at(b, 1))
                    nc.scalar.activation(qt[:, :], bank[3], ACT.Copy).then_inc(mqtt_ready.sem, 1)
                    act.wait_ge(x1p_ready.sem, x1p_ready.at(b, 1))
                    nc.scalar.activation(x1t[:, :], bank[2], ACT.Identity, bias=cols[:, 4:5], scale=cols[:, 3:4]).then_inc(x1t_ready.sem, 1)
                    act.wait_ge(mz_ready.sem, mz_ready.at(b, 1))
                    nc.scalar.activation(ht[:, :, :], ps[:, 5:7, :], ACT.Tanh, scale=0.5).then_inc(mtanh_ready.sem, 1)
                    act.wait_ge(gsm_ready.sem, gsm_ready.at(b, 1))
                    nc.scalar.activation(pexp[:, :, :], gsm[:, :, :], ACT.Exp).then_inc(gexp_ready.sem, 1)
                    act.wait_ge(gpp_ready.sem, gpp_ready.at(b, 1))
                    nc.scalar.activation(gpt[0:E0, :], bank[7][0:E0, :], ACT.Copy).then_inc(gpt_ready.sem, 1)
                    act.wait_ge(my_ready.sem, my_ready.at(b, 1))
                    nc.scalar.activation(yy[:, :, :], tiled(1), ACT.Copy).then_inc(my_copied.sem, 1)
                    act.wait_ge(my_copied.sem, my_copied.at(b, 1))
                    act.wait_ge(stored.sem, stored.at(b, 0))
                    nc.scalar.activation(xn2[:, :, :], yy[:, :, :], ACT.Square).then_inc(my_squared.sem, 1)
                    for e in range(E0):
                        if e >= 2:
                            act.wait_ge(down_ready.sem, down_ready.at(b, e - 1))
                        for f in range(FC):
                            u = e * FC + f
                            act.wait_ge(up_ready.sem, up_ready.at(b, u + 1))
                            nc.scalar.activation(hid[:, e % 2, f, :], bank[4 + u % 4], ACT.Relu, bias=K("upb0", u, 1)).then_inc(hid_ready.sem, 1)
                    act.wait_ge(xn2p_ready.sem, xn2p_ready.at(b, 1))
                    nc.scalar.activation(xt2[:, :], bank[0], ACT.Copy).then_inc(xt2_ready.sem, 1)
                    act.wait_ge(rl_ready.sem, rl_ready.at(b, 1))
                    nc.scalar.activation(rl[:, :, :], rl[:, :, :], ACT.Exp).then_inc(rexp_ready.sem, 1)

            @block.gpsimd
            def _(pool):
                nc.gpsimd.memset(spare_rows, 0.0).then_inc(zero_ready.sem, 1)
                nc.gpsimd.memset(xt[:, 0:1], 0.0)
                nc.gpsimd.memset(xt[:, S + 1:S + 2], 0.0).then_inc(edges_ready.sem, 1)
                att.setup_pool(pool)

            @block.vector
            def _(dve):
                att.setup_vector(dve)
                dve.sem_inc(item_done.sem, 1)
                steps = ATTENTION_STEPS + 3 * NORMALISE_STEPS + 2 * RSQRT_STEPS + 4 + 3 + 5 + 1 + E0 + 3 + 8
                own = Own(ctx0, nc, "a_own", dve, steps)
                with dve.Fori(0, NB) as b:
                    own.start(b)
                    att.split_vector(dve, b, 0, 2)
                    dve.wait_ge(vp_ready.sem, vp_ready.at(b, 1))
                    for t in range(T):
                        last = nc.vector.tensor_tensor(att.v[:, t, :], bank[3 + t], K("vbias0"), ALU.add)
                    last.then_inc(v_ready.sem, 1)
                    att.vector(dve, b, 0, own)

                    dve.wait_ge(mqt_ready.sem, mqt_ready.at(b, 1))
                    own.done(nc.vector.scalar_tensor_tensor(q2[:, :, :], q2[:, :, :], 1.0, tiled(1), ALU.add, ALU.mult))
                    own.done(nc.vector.tensor_tensor(yy[:, :, :], q2[:, :, :], q2[:, :, :], ALU.mult))
                    own.done(nc.vector.tensor_reduce(ss[:, :], yy[:, :, :], X, ALU.add))
                    own.done(nc.vector.tensor_scalar(ss[:, :], ss[:, :], 1.0 / D, 4e-6, ALU.mult, ALU.add))
                    rsqrt(nc, own, rstd[:, :], ss[:, :], tmp[:, :])
                    for t in range(T):
                        last = nc.vector.scalar_tensor_tensor(q2[:, t, :], q2[:, t, :], rstd[:, t:t + 1], K("qnorm"), ALU.mult, ALU.mult)
                    last.then_inc(mq2_ready.sem, 1)

                    dve.wait_ge(z_ready.sem, z_ready.at(b, 1))
                    last = normalise(nc, own, x1h, tiled(0), stats, mv, var[:, :], rstd[:, :], tmp[:, :], 1e-5)
                    last.then_inc(x1h_ready.sem, 1)

                    dve.wait_ge(mtanh_ready.sem, mtanh_ready.at(b, 1))
                    nc.vector.scalar_tensor_tensor(ht[:, :, :], ht[:, :, :], 1.0, ps[:, 5:7, :], ALU.add, ALU.mult).then_inc(mh_ready.sem, 1)

                    dve.wait_ge(gate_ready.sem, gate_ready.at(b, 1))
                    gl = bank[4][:, 0:T * E0].rearrange("p (t e) -> p t e", t=T)
                    own.done(nc.vector.reduce_max(gmax[:, :], gl, X))
                    nc.vector.tensor_tensor(gsm[:, :, :], gl, along(gmax[:, :], E0), ALU.subtract).then_inc(gsm_ready.sem, 1)
                    dve.wait_ge(gexp_ready.sem, gexp_ready.at(b, 1))
                    own.done(nc.vector.tensor_reduce(gmax[:, :], pexp[:, :, :], X, ALU.add))
                    own.done(nc.vector.reciprocal(gmax[:, :], gmax[:, :]))
                    nc.vector.tensor_tensor(gprob[:, :, :], pexp[:, :, :], along(gmax[:, :], E0), ALU.mult).then_inc(gprob_ready.sem, 1)

                    dve.wait_ge(my_squared.sem, my_squared.at(b, 1))
                    own.done(nc.vector.tensor_reduce(ss[:, :], xn2[:, :, :], X, ALU.add))
                    own.done(nc.vector.tensor_scalar(ss[:, :], ss[:, :], 1.0 / D, 4e-6, ALU.mult, ALU.add))
                    rsqrt(nc, own, rstd[:, :], ss[:, :], tmp[:, :])
                    for t in range(T):
                        last = nc.vector.scalar_tensor_tensor(yy[:, t, :], yy[:, t, :], rstd[:, t:t + 1], mem[:, 2 * INTER:2 * INTER + D], ALU.mult, ALU.mult)
                    own.done(last)
                    own.done(nc.vector.tensor_tensor(q2[:, :, :], q2[:, :, :], yy[:, :, :], ALU.add))
                    dve.wait_ge(xin_loaded.sem, xin_loaded.at(b, 1))
                    own.done(nc.vector.tensor_tensor(q2[:, :, :], q2[:, :, :], xin[:, :, :], ALU.add))

                    dve.wait_ge(base_ready.sem, base_ready.at(b, 1))
                    dve.wait_ge(stored.sem, stored.at(b, 0))
                    own.done(nc.vector.tensor_copy(acc[:, :, :], tiled(0)))
                    for e in range(E0):
                        dve.wait_ge(down_ready.sem, down_ready.at(b, e + 1))
                        for t in range(T):
                            last = nc.vector.scalar_tensor_tensor(acc[:, t, :], tiled(2 + e % 2)[:, t, :], gprob[:, t, e:e + 1], acc[:, t, :], ALU.mult, ALU.add)
                        own.done(last)
                        nc.vector.sem_inc(down_used.sem, 1)

                    own.done(normalise(nc, own, x1h, acc, stats, mv, var[:, :], rstd[:, :], tmp[:, :], 1e-5))
                    own.done(nc.vector.tensor_tensor(x1h[:, :, :], x1h[:, :, :], over(K("ln2g"), T), ALU.mult))
                    own.done(nc.vector.tensor_tensor(x1h[:, :, :], x1h[:, :, :], over(K("ln2b"), T), ALU.add))
                    nc.vector.tensor_tensor(acc[:, :, :], x1h[:, :, :], q2[:, :, :], ALU.add).then_inc(sum_ready.sem, 1)
                    dve.wait_ge(sum_ready.sem, sum_ready.at(b, 1))

                    last = normalise(nc, own, xn2, acc, stats, mv, var[:, :], rstd[:, :], tmp[:, :], 1e-5)
                    last.then_inc(xn2_ready.sem, 1)

                    dve.wait_ge(route_ready.sem, route_ready.at(b, 1))
                    lg = bank[1][:, 0:T * E1].rearrange("p (t e) -> p t e", t=T)
                    own.done(nc.vector.reduce_max(gmax[:, :], lg, X))
                    nc.vector.tensor_tensor(rl[:, :, :], lg, along(gmax[:, :], E1), ALU.subtract).then_inc(rl_ready.sem, 1)
                    dve.wait_ge(rexp_ready.sem, rexp_ready.at(b, 1))
                    own.hold(nc)
                    for t in range(T):
                        last = nc.vector.max(top[:, t, :], rl[:, t, :])
                    own.done(last)
                    own.hold(nc)
                    for t in range(T):
                        last = nc.vector.match_replace(left[:, t, :], top[:, t, :], rl[:, t, :], -1.0)
                    own.done(last)
                    own.done(nc.vector.tensor_scalar(left[:, :, :], left[:, :, :], 0.0, None, ALU.is_lt))
                    own.done(nc.vector.tensor_reduce(gmax[:, :], top[:, :, :], X, ALU.add))
                    own.done(nc.vector.reciprocal(gmax[:, :], gmax[:, :]))
                    own.done(nc.vector.tensor_tensor(wts[:, :, :], rl[:, :, :], left[:, :, :], ALU.mult))
                    own.hold(nc)
                    own.done(nc.vector.tensor_copy(chosen[:, bass.ds(b * T * E1, T * E1)], left[:, :, :].rearrange("p t e -> p (t e)")))
                    nc.vector.tensor_tensor(wts[:, :, :], wts[:, :, :], along(gmax[:, :], E1), ALU.mult).then_inc(wts_ready.sem, 1)
                    dve.wait_ge(wts_ready.sem, wts_ready.at(b, 1))
                    nc.vector.sem_inc(item_done.sem, 1)
                    own.end()


Q = 4


def routed(nc, ctx0, K, ps, bank, chosen, gate_up, down, table_d, sum_d):
    with ExitStack() as ctx:
        def sb(name, shape, dt=F32):
            return ctx.enter_context(nc.sbuf_tensor("r_" + name, shape, dt))

        def sig(name, **kw):
            return Signal(ctx0, nc, "r_" + name, **kw)

        upto = sb("upto", [P, P], BF16)
        pick = sb("pick", [P, Q, NT], BF16)
        total = sb("total", [P, Q])
        excl = sb("excl", [NT, Q])
        incl = sb("incl", [NT, Q])
        count = sb("count", [NT, Q, P], BF16)
        onehot = sb("onehot", [NT, Q, CAP], BF16)
        passed = sb("passed", [NT, Q, CAP], BF16)
        onesb = sb("onesb", [NT, 1], BF16)
        below = sb("below", [P, Q, P])
        slot = sb("slot", [P, Q])
        token = sb("token", [P, Q])
        tiles_before = sb("tiles_before", [P, Q])
        index = sb("index", [P, Q], I32)
        row = sb("row", [P, Q, D + E1])
        rt = sb("rt", [P, Q, P])
        wgu = [sb(f"wgu{u}", [P, Q, 2 * F1]) for u in range(2)]
        wdn = [sb(f"wdn{u}", [F1, Q, D]) for u in range(2)]
        th = sb("th", [P, Q, F1])
        h = sb("h", [P, Q, F1])
        ht = sb("ht", [F1, Q, P])
        share = sb("share", [P, Q, 1])
        out = sb("out", [P, Q, D])
        still = sb("still", [P, 2])

        held = sig("held", per=Q + 1, first=1)
        zeroed = sig("zeroed")
        upto_ready = sig("upto_ready")
        loaded = [sig(f"loaded{u}", per=2, unit=16) for u in range(2)]
        pick_ready = sig("pick_ready")
        local_ready = sig("local_ready")
        total_ready = sig("total_ready")
        excl_ready = sig("excl_ready")
        hot_ready = sig("hot_ready")
        sel_ready = sig("sel_ready")
        index_ready = sig("index_ready")
        gathered = sig("gathered", per=Q, unit=16)
        rt_ready = sig("rt_ready")
        rt_copied = sig("rt_copied")
        gu_ready = sig("gu_ready")
        tanh_ready = sig("tanh_ready")
        h_ready = sig("h_ready")
        ht_ready = sig("ht_ready")
        ht_copied = sig("ht_copied")
        eo_ready = sig("eo_ready", first=1)
        out_ready = sig("out_ready")
        added = sig("added", per=Q, unit=16)
        round_done = sig("round_done", first=1)

        local_ps = bank[0].rearrange("p (q s) -> p q s", q=Q)
        excl_ps = bank[1][0:NT, 0:Q]
        sel_ps = bank[2].rearrange("p (q s) -> p q s", q=Q)
        tiles_ps = bank[3][:, 0:Q]
        rt_ps = bank[4].rearrange("p (q s) -> p q s", q=Q)
        gu_ps = ps[:, 5:7, :].rearrange("p b (q s) -> p (b q) s", q=2)[:, :, 0:2 * F1]
        ht_ps = bank[7][0:F1, :].rearrange("p (q s) -> p q s", q=Q)
        eo_ps = bank[0].rearrange("p (q s) -> p q s", q=Q)
        LOOPS = E1 // Q

        with nc.Block() as block:
            @block.sync
            def _(sp):
                for u in range(2):
                    sp.dma_start(wgu[u][:, :, :], gate_up[:, u * Q:(u + 1) * Q, :]).then_inc(loaded[u].sem, 16)
                    sp.dma_start(wdn[u][:, :, :], down[:, u * Q:(u + 1) * Q, :]).then_inc(loaded[u].sem, 16)
                with sp.Fori(0, LOOPS // 2 - 1) as pair:
                    for u in range(2):
                        sp.wait_ge(eo_ready.sem, eo_ready.at(pair * 2, u + 1))
                        sp.dma_start(wgu[u][:, :, :], gate_up[:, bass.ds(pair * (2 * Q) + (2 + u) * Q, Q), :]).then_inc(loaded[u].sem, 16)
                        sp.dma_start(wdn[u][:, :, :], down[:, bass.ds(pair * (2 * Q) + (2 + u) * Q, Q), :]).then_inc(loaded[u].sem, 16)

            @block.tensor
            def _(pe):
                pe.wait_ge(upto_ready.sem, 1)
                pe.sem_inc(eo_ready.sem, 1)
                with pe.Fori(0, LOOPS // 2) as pair:
                    g = pair * 2
                    for u in range(2):
                        pe.wait_ge(pick_ready.sem, pick_ready.at(g, u + 1))
                        for q in range(Q):
                            last = nc.tensor.matmul(local_ps[0:NT, q, :], pick[:, q, :], upto[:, :], start=True, stop=True)
                        last.then_inc(local_ready.sem, 1)
                        pe.wait_ge(total_ready.sem, total_ready.at(g, u + 1))
                        nc.tensor.matmul(excl_ps, K("before"), total[:, :], start=True, stop=True).then_inc(excl_ready.sem, 1)
                        pe.wait_ge(hot_ready.sem, hot_ready.at(g, u + 1))
                        for q in range(Q):
                            nc.tensor.matmul(sel_ps[:, q, :], onehot[:, q, :], count[:, q, :], start=True, stop=True)
                        for q in range(Q):
                            last = nc.tensor.matmul(tiles_ps[:, q:q + 1], passed[:, q, :], onesb[:, :], start=True, stop=True)
                        last.then_inc(sel_ready.sem, 1)
                        pe.wait_ge(gathered.sem, gathered.at(g, (u + 1) * Q))
                        for q in range(Q):
                            last = nc.tensor.transpose(rt_ps[:, q, :], row[:, q, 0:D], K("ident"))
                        last.then_inc(rt_ready.sem, 1)
                        pe.wait_ge(rt_copied.sem, rt_copied.at(g, u + 1))
                        pe.wait_ge(loaded[u].sem, pair * 32 + 32)
                        for q in range(Q):
                            last = nc.tensor.matmul(gu_ps[:, q, :], rt[:, q, :], wgu[u][:, q, :], start=True, stop=True)
                        last.then_inc(gu_ready.sem, 1)
                        pe.wait_ge(h_ready.sem, h_ready.at(g, u + 1))
                        for q in range(Q):
                            last = nc.tensor.transpose(ht_ps[:, q, :], h[:, q, :], K("ident"))
                        last.then_inc(ht_ready.sem, 1)
                        pe.wait_ge(ht_copied.sem, ht_copied.at(g, u + 1))
                        for q in range(Q):
                            last = nc.tensor.matmul(eo_ps[:, q, :], ht[:, q, :], wdn[u][:, q, :], start=True, stop=True)
                        last.then_inc(eo_ready.sem, 1)

            @block.scalar
            def _(act):
                with act.Fori(0, LOOPS) as g:
                    act.wait_ge(rt_ready.sem, rt_ready.at(g, 1))
                    nc.scalar.activation(rt[:, :, :], rt_ps, ACT.Copy).then_inc(rt_copied.sem, 1)
                    act.wait_ge(gu_ready.sem, gu_ready.at(g, 1))
                    nc.scalar.activation(th[:, :, :], gu_ps[:, :, 0:F1], ACT.Tanh, scale=0.5).then_inc(tanh_ready.sem, 1)
                    act.wait_ge(ht_ready.sem, ht_ready.at(g, 1))
                    nc.scalar.activation(ht[:, :, :], ht_ps, ACT.Copy).then_inc(ht_copied.sem, 1)

            @block.gpsimd
            def _(pool):
                nc.gpsimd.tensor_copy(upto[:, :], K("upto"))
                nc.gpsimd.memset(still[:, :], 0.0)
                nc.gpsimd.memset(onesb[:, :], 1.0).then_inc(upto_ready.sem, 1)
                pool.wait_ge(upto_ready.sem, 1)
                pool.sem_inc(round_done.sem, 1)

                pool.sem_inc(held.sem, 1)

                def hold(g, k):
                    pool.wait_ge(held.sem, held.at(g, k))
                    nc.gpsimd.tensor_tensor(still[:, 0:1], still[:, 1:2], still[:, 1:2], ALU.add).then_inc(held.sem, 1)

                with pool.Fori(0, LOOPS) as g:
                    pool.wait_ge(index_ready.sem, index_ready.at(g, 1))
                    hold(g, 0)
                    for q in range(Q):
                        nc.gpsimd.indirect_dma_start(out=row[:, q, :], out_offset=None, in_=table_d,
                                                     in_offset=bass.IndirectOffsetOnAxis(ap=index[:, q:q + 1], axis=0)
                                                     ).then_inc(gathered.sem, 16)
                    pool.wait_ge(out_ready.sem, out_ready.at(g, 1))
                    hold(g, 1)
                    for q in range(Q):
                        if q:
                            pool.wait_ge(added.sem, added.at(g, q))
                            hold(g, q + 1)
                        nc.gpsimd.indirect_dma_start(out=sum_d, out_offset=bass.IndirectOffsetOnAxis(ap=index[:, q:q + 1], axis=0),
                                                     in_=out[:, q, :], in_offset=None, compute_op=ALU.add
                                                     ).then_inc(added.sem, 16)
                    pool.wait_ge(added.sem, added.at(g, Q))
                    pool.sem_inc(round_done.sem, 1)

            @block.vector
            def _(dve):
                own = Own(ctx0, nc, "r_own", dve, 14)
                nc.vector.memset(total[:, :], 0.0).then_inc(zeroed.sem, 1)
                dve.wait_ge(zeroed.sem, 1)
                with dve.Fori(0, LOOPS) as g:
                    own.start(g)
                    own.hold(nc)
                    nc.vector.tensor_copy(pick[:, :, :], chosen[:, :].rearrange("p (t e) -> p e t", e=E1)[:, bass.ds(g * Q, Q), :]
                                          ).then_inc(pick_ready.sem, 1)
                    dve.wait_ge(local_ready.sem, local_ready.at(g, 1))
                    nc.vector.tensor_copy(total[0:NT, :], local_ps[0:NT, :, P - 1]).then_inc(total_ready.sem, 1)
                    dve.wait_ge(excl_ready.sem, excl_ready.at(g, 1))
                    own.done(nc.vector.tensor_copy(excl[:, :], excl_ps))
                    own.done(nc.vector.tensor_tensor(incl[:, :], excl[:, :], total[0:NT, :], ALU.add))
                    for q in range(Q):
                        nc.vector.tensor_scalar(count[:, q, :], local_ps[0:NT, q, :], excl[:, q:q + 1], float(CAP + 1), ALU.add, ALU.min)
                        last = nc.vector.tensor_scalar(passed[:, q, :], K("slots")[0:NT, :], incl[:, q:q + 1], None, ALU.is_ge)
                    own.done(last)
                    for q in range(Q):
                        last = nc.vector.tensor_scalar(onehot[:, q, :], K("slots")[0:NT, :], excl[:, q:q + 1], None, ALU.is_ge)
                    own.done(last)
                    nc.vector.tensor_tensor(onehot[:, :, :], onehot[:, :, :], passed[:, :, :], ALU.subtract).then_inc(hot_ready.sem, 1)
                    dve.wait_ge(sel_ready.sem, sel_ready.at(g, 1))
                    own.done(nc.vector.tensor_scalar(tiles_before[:, :], tiles_ps, float(P), None, ALU.mult))
                    own.done(nc.vector.tensor_scalar(below[:, :, :], sel_ps, K("slot"), None, ALU.is_le))
                    own.done(nc.vector.tensor_reduce(slot[:, :], below[:, :, :], X, ALU.add))
                    own.done(nc.vector.tensor_tensor(token[:, :], tiles_before[:, :], slot[:, :], ALU.add))
                    own.done(nc.vector.tensor_scalar(token[:, :], token[:, :], K("spare"), None, ALU.min))
                    dve.wait_ge(round_done.sem, round_done.at(g, 0))
                    nc.vector.tensor_copy(index[:, :], token[:, :]).then_inc(index_ready.sem, 1)
                    dve.wait_ge(tanh_ready.sem, tanh_ready.at(g, 1))
                    own.done(nc.vector.scalar_tensor_tensor(th[:, :, :], th[:, :, :], 1.0, gu_ps[:, :, 0:F1], ALU.add, ALU.mult))
                    own.done(nc.vector.tensor_tensor(h[:, :, :], th[:, :, :], gu_ps[:, :, F1:2 * F1], ALU.mult))
                    nc.vector.sem_inc(h_ready.sem, 1)
                    own.hold(nc)
                    for q in range(Q):
                        last = nc.vector.tensor_copy(share[:, q, :], row[:, q, bass.ds(g * Q + (D + q), 1)])
                    own.done(last)
                    own.done(nc.vector.tensor_scalar(share[:, :, :], share[:, :, :], 0.5, None, ALU.mult))
                    dve.wait_ge(eo_ready.sem, eo_ready.at(g, 1))
                    for q in range(Q):
                        last = nc.vector.tensor_scalar(out[:, q, :], eo_ps[:, q, :], share[:, q, :], None, ALU.mult)
                    own.done(last)
                    nc.vector.sem_inc(out_ready.sem, 1)
                    assert own.k == own.per, own.k


def layer1(nc, ctx0, K, ps, bank, xnt2_d, sum_d, result):
    with ExitStack() as ctx:
        def sb(name, shape, dt=F32):
            return ctx.enter_context(nc.sbuf_tensor("b_" + name, shape, dt))

        def sig(name, **kw):
            return Signal(ctx0, nc, "b_" + name, **kw)

        xt = [sb(f"xt{n}", [P, S]) for n in range(2)]
        cpad = sb("cpad", [P, S + 2])
        ctxt = sb("ctxt", [P, S])
        before = sb("before", [P, T, D])
        res = sb("res", [P, T, D])
        both, queries = 1 + 2 * PARTS, 1 + PARTS
        starts = (3, 7, 7, 3)
        att = TurnAttention(ctx, ctx0, nc, K, ps, bank, "b", True, 4, [bank[0], bank[1]], [bank[3], bank[4]],
                        [spread(n) for n in starts], [both, queries, queries, both])
        misc = 4 * (2 * G + 1)
        att.misc_free = sig("misc_free", per=misc, first=G + 1)
        PAIRS = NB // 2

        copied = sig("copied", unit=16)
        x_loaded = [sig(f"x_loaded{n}", first=1, unit=16) for n in range(2)]
        before_loaded = sig("before_loaded", per=2, unit=16)
        edges_ready = sig("edges_ready")
        proj_ready = sig("proj_ready", per=2, first=1)
        vp_ready = sig("vp_ready", per=2 * T, first=T)
        v_ready = sig("v_ready", per=2 * T, first=T)
        cpad_ready = sig("cpad_ready", per=2)
        conv_ready = sig("conv_ready", per=2)
        ctxt_copied = sig("ctxt_copied", per=2)
        out_ready = sig("out_ready", per=2, first=1)
        res_ready = sig("res_ready", per=2, first=1)
        res_stored = sig("res_stored", per=2, first=1, unit=16)

        def tiled(ap):
            return ap.rearrange("p (t d) -> p t d", t=T)

        def load_x(sp, item, n):
            sp.dma_start(xt[n][:, :], xnt2_d[bass.ds(item * P, P), :]).then_inc(x_loaded[n].sem, 16)

        with nc.Block() as block:
            @block.sync
            def _(sp):
                sp.dma_start(xnt2_d[NB * P:(NB + 2) * P, :], xnt2_d[0:2 * P, :]).then_inc(copied.sem, 16)
                for n in range(2):
                    load_x(sp, n, n)
                att.setup_sync(sp)
                sp.sem_inc(res_stored.sem, 16)
                sp.wait_ge(copied.sem, 16)
                att.load_rows(sp, -1, 3, 2)
                att.load_shifts(sp, -1, 3)
                with sp.Fori(0, PAIRS) as i:
                    att.load_rows(sp, i, 0, 2)
                    att.load_shifts(sp, i, 0)
                    att.load_rows(sp, i, 1, 1)
                    sp.wait_ge(vp_ready.sem, vp_ready.at(i, 0))
                    load_x(sp, i * 2 + 2, 0)
                    att.load_shifts(sp, i, 1)
                    att.load_rows(sp, i, 2, 1)
                    sp.wait_ge(vp_ready.sem, vp_ready.at(i, T))
                    load_x(sp, i * 2 + 3, 1)
                    sp.wait_ge(res_ready.sem, res_ready.at(i, 0))
                    sp.dma_start(before[:, :, :], sum_d[bass.ds(i * (2 * S), S), :].rearrange("(t p) d -> p t d", p=P)
                                 ).then_inc(before_loaded.sem, 16)
                    att.load_shifts(sp, i, 2)
                    att.load_rows(sp, i, 3, 2)
                    att.load_shifts(sp, i, 3)
                    sp.wait_ge(res_ready.sem, res_ready.at(i, 1))
                    sp.dma_start(result[bass.ds(i * 2, 1), :, :].rearrange("o (t p) d -> p (o t) d", p=P), res[:, :, :]
                                 ).then_inc(res_stored.sem, 16)
                    sp.dma_start(before[:, :, :], sum_d[bass.ds(i * (2 * S) + S, S), :].rearrange("(t p) d -> p t d", p=P)
                                 ).then_inc(before_loaded.sem, 16)
                    sp.wait_ge(res_ready.sem, res_ready.at(i, 2))
                    sp.dma_start(result[bass.ds(i * 2 + 1, 1), :, :].rearrange("o (t p) d -> p (o t) d", p=P), res[:, :, :]
                                 ).then_inc(res_stored.sem, 16)
                sp.wait_ge(res_stored.sem, res_stored.at(PAIRS, 0))

            @block.gpsimd
            def _(pool):
                nc.gpsimd.memset(cpad[:, 0:1], 0.0)
                nc.gpsimd.memset(cpad[:, S + 1:S + 2], 0.0).then_inc(edges_ready.sem, 1)
                att.setup_pool(pool)

            @block.tensor
            def _(pe):
                def project(i, n, k):
                    pe.wait_ge(x_loaded[n].sem, x_loaded[n].at(i + k, 0))
                    nc.tensor.matmul(bank[2], K("q1"), xt[n][:, :], start=True, stop=True)
                    nc.tensor.matmul(bank[5], K("k1"), xt[n][:, :], start=True, stop=True).then_inc(proj_ready.sem, 1)

                def values(i, n, k, t):
                    if t < 2:
                        pe.wait_ge(att.qk_ready.sem, k)
                    else:
                        pe.wait_ge(v_ready.sem, v_ready.at(i, (0 if n else T) + t - 1))
                    nc.tensor.matmul(bank[2 if t % 2 == 0 else 5], xt[n][:, t * P:(t + 1) * P], K("v1"), start=True, stop=True
                                     ).then_inc(vp_ready.sem, 1)

                def convolve(i, k):
                    pe.wait_ge(cpad_ready.sem, cpad_ready.at(i, k + 1))
                    pe.wait_ge(v_ready.sem, v_ready.at(i, T))
                    for tap in range(3):
                        last = nc.tensor.matmul(bank[2], K("conv1", tap * D, D), cpad[:, tap:tap + S], start=tap == 0, stop=tap == 2)
                    last.then_inc(conv_ready.sem, 1)

                def output(i, k):
                    pe.wait_ge(ctxt_copied.sem, ctxt_copied.at(i, k + 1))
                    pe.wait_ge(v_ready.sem, v_ready.at(i, T + T * 1))
                    for t in range(T):
                        nc.tensor.matmul(tiled(bank[5])[:, t, :], ctxt[:, t * P:(t + 1) * P], K("out1"), start=True, stop=False)
                        last = nc.tensor.matmul(tiled(bank[5])[:, t, :], K("ones")[0:1, :], K("outb1")[0:1, :], start=False, stop=True)
                    last.then_inc(out_ready.sem, 1)

                att.setup_tensor(pe)
                pe.sem_inc(out_ready.sem, 1)
                pe.wait_ge(edges_ready.sem, 1)
                att.misc_used = misc - G
                pe.wait_ge(x_loaded[0].sem, 16)
                nc.tensor.matmul(bank[2], K("q1"), xt[0][:, :], start=True, stop=True)
                nc.tensor.matmul(bank[5], K("k1"), xt[0][:, :], start=True, stop=True).then_inc(proj_ready.sem, 1)
                for t in range(T):
                    if t == 0:
                        pe.wait_ge(att.qk_ready.sem, 1)
                    if t >= 2:
                        pe.wait_ge(v_ready.sem, t - 1)
                    nc.tensor.matmul(bank[2 if t % 2 == 0 else 5], xt[0][:, t * P:(t + 1) * P], K("v1"), start=True, stop=True
                                     ).then_inc(vp_ready.sem, 1)
                att.tensor_early(pe)
                pe.wait_ge(v_ready.sem, T)
                with pe.Fori(0, PAIRS) as i:
                    att.misc_used = 0

                    def odd_start(s):
                        if s == 0:
                            pe.wait_ge(res_ready.sem, res_ready.at(i, 0))
                            project(i, 1, 0)
                        if s in (5, 6, 7, 8):
                            values(i, 1, att.qk_ready.at(i, 1), s - 5)

                    def even_queries(s):
                        if s == 2:
                            att.tensor_whole_context(pe, i, 0)
                        if s == 3:
                            convolve(i, 0)

                    def odd_queries(s):
                        if s == 2:
                            att.tensor_whole_context(pe, i, 1)
                        if s == 3:
                            pe.wait_ge(att.qk_ready.sem, att.qk_ready.at(i, 2))
                            convolve(i, 1)

                    def next_start(s):
                        if s == 0:
                            pe.wait_ge(att.qk_ready.sem, att.qk_ready.at(i, 3))
                            project(i, 0, 1)
                        if s == 2:
                            att.tensor_whole_context(pe, i, 2)
                        if s in (5, 6, 7, 8):
                            values(i, 0, att.qk_ready.at(i, 4), s - 5)
                        if s == 10:
                            output(i, 0)

                    att.tensor_turn(pe, i, 0, odd_start)
                    att.tensor_turn(pe, i, 1, even_queries)
                    att.tensor_turn(pe, i, 2, odd_queries)
                    att.tensor_turn(pe, i, 3, next_start)
                    att.tensor_tail(pe, i, 3)
                    att.tensor_whole_context(pe, i, 3)
                    pe.wait_ge(res_ready.sem, res_ready.at(i, 1))
                    output(i, 1)
                    assert att.misc_used == misc

            @block.scalar
            def _(act):
                cols = K("cols1")

                def queries_keys(i, a, k):
                    act.wait_ge(proj_ready.sem, proj_ready.at(i, k))
                    att.before_qk(act, i, a)
                    nc.scalar.activation(att.qk[:, 0, :], bank[2], ACT.Identity, bias=cols[:, 0:1])
                    nc.scalar.activation(att.qk[:, 1, :], bank[5], ACT.Identity, bias=cols[:, 1:2]).then_inc(att.qk_ready.sem, 1)
                    att.split_hi(act, i, a, 2)

                def second_queries(i, a, k):
                    act.wait_ge(conv_ready.sem, conv_ready.at(i, k))
                    att.before_qk(act, i, a)
                    nc.scalar.activation(att.qk[:, 0, :], bank[2], ACT.Identity, bias=cols[:, 2:3]).then_inc(att.qk_ready.sem, 1)
                    att.split_hi(act, i, a, 1)

                def whole_context(i, a, out, signal, k):
                    act.wait_ge(att.ctxt_ready.sem, att.ctxt_ready.at(i, a + 1))
                    nc.scalar.activation(out, bank[7], ACT.Copy).then_inc(signal.sem, 1)
                    act.wait_ge(signal.sem, signal.at(i, k))
                    act.sem_inc(att.misc_free.sem, 1)

                att.setup_scalar(act)
                queries_keys(-1, 3, 2)
                att.split_mid(act, -1, 3, 2)
                with act.Fori(0, PAIRS) as i:
                    def first_start(s, a, k):
                        if s == 0:
                            queries_keys(i, a, k)
                        if s == 1:
                            att.split_mid(act, i, a, 2)

                    def second(s, a, k):
                        if s == 2:
                            whole_context(i, a - 1, cpad[:, 1:S + 1], cpad_ready, k)
                        if s == 3:
                            second_queries(i, a, k)
                        if s == 4:
                            att.split_mid(act, i, a, 1)

                    def last(s):
                        first_start(s, 3, 2)
                        if s == 2:
                            act.wait_ge(out_ready.sem, out_ready.at(i, 0))
                            whole_context(i, 2, ctxt[:, :], ctxt_copied, 1)

                    att.scalar_turn(act, i, 0, lambda s: first_start(s, 0, 1))
                    att.scalar_turn(act, i, 1, lambda s: second(s, 1, 1))
                    att.scalar_turn(act, i, 2, lambda s: second(s, 2, 2))
                    att.scalar_turn(act, i, 3, last)
                    att.scalar_context(act, i, 3, G - 1)
                    act.wait_ge(out_ready.sem, out_ready.at(i, 1))
                    whole_context(i, 3, ctxt[:, :], ctxt_copied, 2)

            @block.vector
            def _(dve):
                def values(i, n, k, t):
                    dve.wait_ge(vp_ready.sem, vp_ready.at(i, k + t + 1))
                    nc.vector.tensor_tensor(att.v[n][:, t, :], bank[2 if t % 2 == 0 else 5], K("vbias1"), ALU.add
                                            ).then_inc(v_ready.sem, 1)

                def finish(i, k):
                    dve.wait_ge(before_loaded.sem, before_loaded.at(i, k + 1))
                    dve.wait_ge(res_stored.sem, res_stored.at(i, k))
                    dve.wait_ge(out_ready.sem, out_ready.at(i, k + 1))
                    nc.vector.tensor_tensor(res[:, :, :], tiled(bank[5]), before[:, :, :], ALU.add).then_inc(res_ready.sem, 1)

                att.setup_vector(dve)
                dve.sem_inc(res_ready.sem, 1)
                per = 4 * G * (SHIFT_STEPS + CONTEXT_STEPS)
                own = Own(ctx0, nc, "b_own", dve, per, first=G * SHIFT_STEPS)
                own.start(-1, per - G * SHIFT_STEPS)
                att.split_rest(dve, -1, 3, 2)
                att.split_lo(dve, -1, 3, 2)
                for t in range(T):
                    values(-1, 0, T, t)
                att.vector_early(dve, own)
                with dve.Fori(0, PAIRS) as i:
                    own.start(i)

                    def first_start(s, a, n, k):
                        if s == 0:
                            att.split_rest(dve, i, a, 2)
                        if s == 1:
                            att.split_lo(dve, i, a, 2)
                        if s in (5, 6, 7, 8):
                            values(i, n, k, s - 5)

                    def second(s, a):
                        if s == 3:
                            att.split_rest(dve, i, a, 1)
                        if s == 4:
                            att.split_lo(dve, i, a, 1)

                    def last(s):
                        first_start(s, 3, 0, T)
                        if s == 10:
                            finish(i, 0)

                    att.vector_turn(dve, i, 0, own, lambda s: first_start(s, 0, 1, 0))
                    att.vector_turn(dve, i, 1, own, lambda s: second(s, 1))
                    att.vector_turn(dve, i, 2, own, lambda s: second(s, 2))
                    att.vector_turn(dve, i, 3, own, last)
                    att.vector_context(dve, i, 3, G - 1, own)
                    finish(i, 1)
                    own.end()


def fused(nc, x, shared, memory, layer0_in, layer1_in, gate_up, down, result):
    given = {"shared": shared, "memory": memory, "layer0": layer0_in, "layer1": layer1_in}
    with ExitStack() as ctx:
        consts = {}
        loaded = ctx.enter_context(nc.semaphore("consts_loaded"))
        loaded0 = ctx.enter_context(nc.semaphore("consts0_loaded"))

        def hold(stack, part):
            consts[part] = stack.enter_context(nc.sbuf_tensor("consts_" + part, [P, WIDTH[part]], F32))

        def K(name, offset=0, width=None):
            part, start, w = PLACE[name]
            return consts[part][:, start + offset:start + offset + (w if width is None else width)]

        hold(ctx, "shared")
        mem = ctx.enter_context(nc.sbuf_tensor("mem", [P, 2 * INTER + D], F32))
        chosen = ctx.enter_context(nc.sbuf_tensor("chosen", [P, NT * E1], BF16))
        spare = ctx.enter_context(nc.sbuf_tensor("spare_column", [P, 1], F32))
        Own.column = spare[:, :]
        psum = ctx.enter_context(nc.psum_tensor("psum", [P, 8, 512], F32))
        ps = psum[:, :, :]
        bank = [psum[:, i, :] for i in range(8)]

        xnt_d = nc.dram_tensor("xnt", [NB * P, S], F32, kind="Internal").ap()
        kn_d = nc.dram_tensor("kn", [NC, NB * CHUNK, D], F32, kind="Internal").ap()
        vn_d = nc.dram_tensor("vn", [NC, NB * CHUNK, D], F32, kind="Internal").ap()
        xnt2_d = nc.dram_tensor("xnt2", [(NB + 2) * P, S], F32, kind="Internal").ap()
        table_d = nc.dram_tensor("table", [ROWS, D + E1], F32, kind="Internal").ap()
        sum_d = nc.dram_tensor("sum", [ROWS, D], F32, kind="Internal").ap()

        with ExitStack() as first:
            hold(first, "layer0")
            with ExitStack() as start:
                hold(start, "memory")
                memw1 = start.enter_context(nc.sbuf_tensor("memw1", [P, INTER], F32))
                R = start.enter_context(nc.sbuf_tensor("gate_parts", [P, 3 * NT], F32))
                with nc.Block() as block:
                    @block.sync
                    def _(sp):
                        for part in ("shared", "memory"):
                            sp.dma_start(consts[part][:, :], given[part]).then_inc(loaded, 16)
                        sp.dma_start(consts["layer0"][:, :], given["layer0"]).then_inc(loaded0, 16)
                        sp.wait_ge(loaded, 32)
                with Semaphores() as sems:
                    project(nc, sems, K, bank, x, xnt_d, kn_d, vn_d, R)
                    sems.clear(nc)
                with Semaphores() as sems:
                    learn(nc, sems, K, ps, bank, kn_d, vn_d, R, mem, memw1)
                    sems.clear(nc)
            with nc.Block() as block:
                @block.sync
                def _(sp):
                    sp.wait_ge(loaded0, 16)
            with Semaphores() as sems:
                layer0(nc, sems, K, ps, bank, x, xnt_d, mem, chosen, xnt2_d, table_d, sum_d)
                sems.clear(nc)
        with ExitStack() as second:
            hold(second, "layer1")
            with nc.Block() as block:
                @block.sync
                def _(sp):
                    sp.dma_start(consts["layer1"][:, :], given["layer1"]).then_inc(loaded, 16)
                    sp.wait_ge(loaded, 48)
            with Semaphores() as sems:
                routed(nc, sems, K, ps, bank, chosen, gate_up, down, table_d, sum_d)
                sems.clear(nc)
            with Semaphores() as sems:
                layer1(nc, sems, K, ps, bank, xnt2_d, sum_d, result)


def pack(inputs):
    import numpy as np

    a = {k: np.asarray(v) for k, v in inputs.items()}
    out = {part: np.zeros((P, width), np.float32) for part, width in WIDTH.items()}

    def put(name, m, offset=0):
        part, start, _ = PLACE[name]
        out[part][:m.shape[0], start + offset:start + offset + m.shape[1]] = m

    def rows(v):
        return np.broadcast_to(v.reshape(1, -1), (P, v.size))

    p = np.arange(P)
    put("ident", np.eye(P, dtype=np.float32))
    put("ones", np.ones((P, P), np.float32))
    for w, name in enumerate(("alpha", "theta", "eta")):
        put("gates", np.concatenate([a[f"L0_attn_{name}_w"].reshape(CHUNK, D)] * 2), w * D)
    for h in range(2):
        put("half", np.broadcast_to(((p // CHUNK) == h).astype(np.float32)[:, None], (P, P)), h * D)
    put("wk", a["L0_attn_wk_w"].T)
    put("wv", a["L0_attn_wv_w"].T)
    put("wq", a["L0_attn_wq_w"].T)
    put("knorm", rows(a["L0_attn_k_norm_w"]))
    put("qnorm", rows(a["L0_attn_q_norm_w"]))
    w1 = a["L0_attn_mem_w1"]
    put("mem", a["L0_attn_mem_w0"].T)
    put("mem", w1.T[0:P], INTER)
    put("mem", w1.T[P:2 * P], INTER + D)
    put("mem", rows(a["L0_attn_mem_ln_w"]), 2 * INTER)
    put("memw1", w1)

    order = np.arange(D).reshape(H, DH).T.reshape(-1)
    for layer, wqkv, bqkv in ((0, a["L0_ffn_wqkv"], a["L0_ffn_bqkv"]), (1, a["L1_attn_Wqkv_w"], a["L1_attn_Wqkv_b"])):
        put(f"q{layer}", wqkv[0:D][order].T)
        put(f"k{layer}", wqkv[D:2 * D][order].T)
        wv = np.zeros((D, H, 32), np.float32)
        bv = np.zeros((H, 32), np.float32)
        wv[:, :, 0:DH] = wqkv[2 * D:].T.reshape(D, H, DH)
        bv[:, 0:DH] = bqkv[2 * D:].reshape(H, DH)
        bv[:, DH] = 1.0
        put(f"v{layer}", wv.reshape(D, -1))
        put(f"vbias{layer}", rows(bv))
    b0, b1 = a["L0_ffn_bqkv"], a["L1_attn_Wqkv_b"]
    conv = a["L0_ffn_conv_w"]
    for tap in range(3):
        put("conv0", conv[:, :, tap].T, tap * D)
        put("conv1", a["L1_attn_conv_w"][order, :, tap].T, tap * D)
    put("cols0", np.stack([a["L0_ffn_conv_b"], b0[0:D][order], b0[D:2 * D][order], a["L0_ffn_ln1_g"], a["L0_ffn_ln1_b"]], 1))
    put("cols1", np.stack([b1[0:D][order], b1[D:2 * D][order], a["L1_attn_conv_b"][order]], 1))
    put("out0", a["L0_ffn_wo"].T)
    put("outb0", a["L0_ffn_bo"].reshape(1, -1))
    put("gate0", a["L0_ffn_gate_w"])
    put("gateb0", a["L0_ffn_gate_b"].reshape(1, -1))
    put("up0", a["L0_ffn_w1"].transpose(1, 0, 2).reshape(D, -1))
    put("upb0", a["L0_ffn_b1"].reshape(E0 * FC, P).T)
    put("down0", a["L0_ffn_w2"].reshape(E0 * FC, P, D).transpose(1, 0, 2).reshape(P, -1))
    put("downb0", a["L0_ffn_b2"])
    put("ln2g", rows(a["L0_ffn_ln2_g"]))
    put("ln2b", rows(a["L0_ffn_ln2_b"]))
    put("out1", a["L1_attn_out_w"].T)
    put("outb1", a["L1_attn_out_b"].reshape(1, -1))
    put("router", a["L1_ffn_gate_weight"].T)
    put("maskq", np.where(p[None, :] > p[:, None], np.float32(NEG), np.float32(0)))
    put("maskk", np.where(p[:, None] > p[None, :], np.float32(NEG), np.float32(0)))
    put("upto", (p[:, None] <= p[None, :]).astype(np.float32))
    q = np.arange(NT)
    put("before", (q[:, None] < q[None, :]).astype(np.float32))
    put("slots", rows(np.arange(CAP, dtype=np.float32)))
    put("slot", p.astype(np.float32)[:, None])
    put("spare", (N + p).astype(np.float32)[:, None])
    return out


def kernel(**inputs):
    import numpy as np
    import concourse.bacc as bacc
    from concourse.bass_utils import run_bass_kernel_spmd

    nc = bacc.Bacc("TRN2", target_bir_lowering=False, num_devices=1)
    arrays = {
        "x": np.ascontiguousarray(inputs["L0_attn_x"]),
        **{f"{part}_in": a for part, a in pack(inputs).items()},
        "gate_up": np.ascontiguousarray(np.asarray(inputs["L1_ffn_gate_up_proj"]).transpose(2, 0, 1)),
        "down": np.ascontiguousarray(np.asarray(inputs["L1_ffn_down_proj"]).transpose(2, 0, 1)),
    }
    args = [nc.dram_tensor(n, a.shape, mybir.dt.from_np(a.dtype), kind="ExternalInput").ap() for n, a in arrays.items()]
    result = nc.dram_tensor("result", (NB, S, D), F32, kind="ExternalOutput").ap()
    fused(nc, *args, result)
    r = run_bass_kernel_spmd(nc, [arrays], core_ids=[0])
    return r.results[0]["result"]
```

```python
from contextlib import ExitStack

import concourse.bass as bass
from concourse import mybir

F32 = mybir.dt.float32
BF16 = mybir.dt.bfloat16
I32 = mybir.dt.int32
ACT = mybir.ActivationFunctionType
ALU = mybir.AluOpType
X = mybir.AxisListType.X

P = 128
D = 128
NB = 16
S = 512
T = S // P
NT = NB * T
N = NB * S
CHUNK = 64
NC = S // CHUNK
CT = NB * CHUNK // P
INTER = 256
H = 16
DH = 8
G = 4
HG = H // G
E0 = 8
F0 = 512
FC = F0 // P
E1 = 32
F1 = 96
CAP = 128
ROWS = N + CAP
SCALE = DH ** -0.5
NEG = -1.0e30
MAGIC = 0x5F3759DF

COLUMNS = {
    "shared": [("ident", D), ("ones", D), ("wq", D), ("qnorm", D)],
    "memory": [("gates", 3 * D), ("half", 2 * D), ("wk", D), ("wv", D), ("knorm", D),
               ("mem", 2 * INTER + D), ("memw1", INTER)],
    "layer0": [("conv0", 3 * D), ("q0", D), ("k0", D), ("v0", G * D), ("vbias0", G * D), ("out0", D),
               ("cols0", 5), ("outb0", D), ("gate0", E0), ("gateb0", E0), ("up0", E0 * F0),
               ("upb0", E0 * FC), ("down0", E0 * F0), ("downb0", D), ("ln2g", D), ("ln2b", D),
               ("router", E1)],
    "layer1": [("q1", D), ("k1", D), ("v1", G * D), ("vbias1", G * D), ("conv1", 3 * D), ("cols1", 3),
               ("out1", D), ("outb1", D), ("maskq", D), ("maskk", D), ("upto", D), ("before", NT),
               ("slots", CAP), ("spare", 1), ("slot", 1)],
}
PLACE = {name: (part, sum(w for _, w in columns[:n]), width)
         for part, columns in COLUMNS.items() for n, (name, width) in enumerate(columns)}
WIDTH = {part: sum(w for _, w in columns) for part, columns in COLUMNS.items()}


class Semaphores(ExitStack):

    def __init__(self):
        super().__init__()
        self.made = []

    def enter_context(self, semaphore):
        self.made.append(super().enter_context(semaphore))
        return self.made[-1]

    def clear(self, nc):
        with nc.Block() as block:
            @block.sync
            def _(sp):
                for sem in self.made:
                    sp.sem_clear(sem)


class Signal:

    def __init__(self, ctx, nc, name, per=1, first=0, unit=1):
        self.sem = ctx.enter_context(nc.semaphore(name))
        self.per, self.first, self.unit = per, first, unit

    def at(self, i, k):
        return i * (self.per * self.unit) + (self.first + k) * self.unit


class Own:

    column = None

    def __init__(self, ctx, nc, name, engine, per, first=0):
        self.sem = ctx.enter_context(nc.semaphore(name))
        self.engine, self.per, self.first, self.k, self.i = engine, per, first, 0, 0

    def start(self, i, k=0):
        self.i, self.k = i, k

    def done(self, instruction):
        self.k += 1
        instruction.then_inc(self.sem, 1)
        self.engine.wait_ge(self.sem, self.i * self.per + (self.first + self.k))

    def hold(self, nc):
        nc.vector.memset(self.column, 0.0)

    def end(self):
        assert self.k == self.per, (self.sem, self.k)


def rsqrt(nc, own, y, v, t):
    own.done(nc.vector.tensor_scalar(y.bitcast(I32), v.bitcast(I32), -0.5, float(MAGIC), ALU.mult, ALU.add))
    for _ in range(3):
        own.done(nc.vector.scalar_tensor_tensor(t, y, -0.5, y, ALU.mult, ALU.mult))
        own.done(nc.vector.tensor_tensor(t, t, v, ALU.mult))
        own.done(nc.vector.scalar_tensor_tensor(y, t, 1.5, y, ALU.add, ALU.mult))


RSQRT_STEPS = 10


def normalise(nc, own, out, src, stats, mv, var, rstd, tmp, eps):
    for t in range(T):
        last = nc.vector.bn_stats(stats[:, t, :], src[:, t, :])
    own.done(last)
    own.hold(nc)
    for t in range(T):
        last = nc.vector.bn_aggr(mv[:, t, :], stats[:, t, :])
    own.done(last)
    own.done(nc.vector.tensor_scalar(var, mv[:, :, 1], eps, None, ALU.add))
    rsqrt(nc, own, rstd, var, tmp)
    for t in range(T):
        last = nc.vector.tensor_scalar(out[:, t, :], src[:, t, :], mv[:, t, 0:1], rstd[:, t:t + 1],
                                       ALU.subtract, ALU.mult)
    return last


NORMALISE_STEPS = 3 + RSQRT_STEPS


def over(ap, n):
    return ap.unsqueeze(1).broadcast_to([P, n, ap.shape[-1]])


def along(ap, n):
    return ap.unsqueeze(2).broadcast_to([P, ap.shape[-1], n])


def project(nc, ctx0, K, bank, x, xnt_d, kn_d, vn_d, R):
    with ExitStack() as ctx:
        def sb(name, shape, dt=F32):
            return ctx.enter_context(nc.sbuf_tensor("p_" + name, shape, dt))

        xin = sb("xin", [P, T, D])
        xn = sb("xn", [P, T, D])
        xt = sb("xt", [P, S])
        tk = sb("tk", [P, T, D])
        tv = sb("tv", [P, T, D])
        sk = sb("sk", [P, T, D])
        sq = sb("sq", [P, T, D])
        kn = sb("kn", [P, T, D])
        vn = sb("vn", [P, T, D])
        prod = sb("prod", [P, 3, T, D])
        stats = sb("stats", [P, T, 6])
        mv = sb("mv", [P, T, 2])
        var = sb("var", [P, T])
        rstd = sb("rstd", [P, T])
        tmp = sb("tmp", [P, T])
        ss = sb("ss", [P, T])

        x_loaded = Signal(ctx0, nc, "p_x_loaded", unit=16)
        x_free = Signal(ctx0, nc, "p_x_free")
        xn_ready = Signal(ctx0, nc, "p_xn_ready")
        t_ready = Signal(ctx0, nc, "p_t_ready")
        xt_ready = Signal(ctx0, nc, "p_xt_ready")
        kv_ready = Signal(ctx0, nc, "p_kv_ready")
        tanh_ready = Signal(ctx0, nc, "p_tanh_ready")
        kv_free = Signal(ctx0, nc, "p_kv_free", first=1)
        kn_ready = Signal(ctx0, nc, "p_kn_ready")
        vs_ready = Signal(ctx0, nc, "p_vs_ready")
        vn_ready = Signal(ctx0, nc, "p_vn_ready")
        prod_ready = Signal(ctx0, nc, "p_prod_ready")
        prod_free = Signal(ctx0, nc, "p_prod_free", first=1)
        xt_stored = Signal(ctx0, nc, "p_xt_stored", first=1, unit=16)
        kn_stored = Signal(ctx0, nc, "p_kn_stored", first=1, per=T, unit=16)
        vn_stored = Signal(ctx0, nc, "p_vn_stored", first=1, per=T, unit=16)

        def rows_of(table, b, t):
            return table[2 * t:2 * t + 2, bass.ds(b * CHUNK, CHUNK), :]

        with nc.Block() as block:
            @block.sync
            def _(sp):
                sp.sem_inc(xt_stored.sem, 16)
                sp.sem_inc(kn_stored.sem, 16)
                sp.sem_inc(vn_stored.sem, 16)

                def load(b):
                    sp.dma_start(xin[:, :, :], x[bass.ds(b, 1), :, :].rearrange("o (t p) d -> p (o t) d", p=P)
                                 ).then_inc(x_loaded.sem, 16)

                def store(b):
                    sp.wait_ge(xt_ready.sem, xt_ready.at(b, 1))
                    sp.dma_start(xnt_d[bass.ds(b * P, P), :], xt[:, :]).then_inc(xt_stored.sem, 16)
                    sp.wait_ge(vn_ready.sem, vn_ready.at(b, 1))
                    for t in range(T):
                        sp.dma_start(rows_of(vn_d, b, t), vn[:, t, :]).then_inc(vn_stored.sem, 16)
                    sp.wait_ge(kn_ready.sem, kn_ready.at(b, 1))
                    for t in range(T):
                        sp.dma_start(rows_of(kn_d, b, t), kn[:, t, :]).then_inc(kn_stored.sem, 16)

                load(0)
                with sp.Fori(0, NB - 1) as b:
                    sp.wait_ge(x_free.sem, x_free.at(b, 1))
                    load(b + 1)
                    store(b)
                store(NB - 1)
                sp.wait_ge(xt_stored.sem, xt_stored.at(NB, 0))
                sp.wait_ge(kn_stored.sem, kn_stored.at(NB, 0))
                sp.wait_ge(vn_stored.sem, vn_stored.at(NB, 0))

            @block.tensor
            def _(pe):
                with pe.Fori(0, NB) as b:
                    pe.wait_ge(xn_ready.sem, xn_ready.at(b, 1))
                    for t in range(T):
                        last = nc.tensor.transpose(bank[0][:, t * P:(t + 1) * P], xn[:, t, :], K("ident"))
                    last.then_inc(t_ready.sem, 1)
                    pe.wait_ge(xt_ready.sem, xt_ready.at(b, 1))
                    pe.wait_ge(kv_free.sem, kv_free.at(b, 0))
                    for t in range(T):
                        nc.tensor.matmul(bank[1][:, t * P:(t + 1) * P], xt[:, t * P:(t + 1) * P], K("wk"), start=True, stop=True)
                    for t in range(T):
                        last = nc.tensor.matmul(bank[2][:, t * P:(t + 1) * P], xt[:, t * P:(t + 1) * P], K("wv"), start=True, stop=True)
                    last.then_inc(kv_ready.sem, 1)

            @block.scalar
            def _(act):
                with act.Fori(0, NB) as b:
                    act.wait_ge(t_ready.sem, t_ready.at(b, 1))
                    act.wait_ge(xt_stored.sem, xt_stored.at(b, 0))
                    nc.scalar.activation(xt[:, :], bank[0][:, :], ACT.Copy).then_inc(xt_ready.sem, 1)
                    act.wait_ge(kv_ready.sem, kv_ready.at(b, 1))
                    nc.scalar.activation(tk[:, :, :], bank[1][:, :].rearrange("p (t d) -> p t d", t=T), ACT.Tanh, scale=0.5)
                    nc.scalar.activation(tv[:, :, :], bank[2][:, :].rearrange("p (t d) -> p t d", t=T), ACT.Tanh, scale=0.5
                                         ).then_inc(tanh_ready.sem, 1)
                    act.wait_ge(vs_ready.sem, vs_ready.at(b, 1))
                    act.wait_ge(vn_stored.sem, vn_stored.at(b, 0))
                    nc.scalar.activation(vn[:, :, :], tv[:, :, :], ACT.Copy, scale=0.5).then_inc(vn_ready.sem, 1)

            @block.gpsimd
            def _(pool):
                with pool.Fori(0, NB) as b:
                    pool.wait_ge(xn_ready.sem, xn_ready.at(b, 1))
                    pool.wait_ge(prod_free.sem, prod_free.at(b, 0))
                    for w in range(3):
                        last = nc.gpsimd.tensor_tensor(prod[:, w], xn[:, :, :], over(K("gates", w * D, D), T), ALU.mult)
                    last.then_inc(prod_ready.sem, 1)

            @block.vector
            def _(dve):
                nc.vector.sem_inc(kv_free.sem, 1)
                nc.vector.sem_inc(prod_free.sem, 1)
                own = Own(ctx0, nc, "p_own", dve, NORMALISE_STEPS + 4 + RSQRT_STEPS, first=NORMALISE_STEPS)

                def norm(b):
                    dve.wait_ge(x_loaded.sem, x_loaded.at(b, 1))
                    last = normalise(nc, own, xn, xin, stats, mv, var[:, :], rstd[:, :], tmp[:, :], 1e-5)
                    last.then_inc(xn_ready.sem, 1)
                    dve.wait_ge(xn_ready.sem, xn_ready.at(b, 1))
                    nc.vector.sem_inc(x_free.sem, 1)

                def silu(b):
                    dve.wait_ge(tanh_ready.sem, tanh_ready.at(b, 1))
                    nc.vector.scalar_tensor_tensor(tv[:, :, :], tv[:, :, :], 1.0, bank[2][:, :].rearrange("p (t d) -> p t d", t=T), ALU.add, ALU.mult
                                                   ).then_inc(vs_ready.sem, 1)
                    own.done(nc.vector.scalar_tensor_tensor(sk[:, :, :], tk[:, :, :], 1.0, bank[1][:, :].rearrange("p (t d) -> p t d", t=T), ALU.add, ALU.mult))
                    nc.vector.sem_inc(kv_free.sem, 1)

                def keys(b):
                    own.done(nc.vector.tensor_tensor(sq[:, :, :], sk[:, :, :], sk[:, :, :], ALU.mult))
                    own.done(nc.vector.tensor_reduce(ss[:, :], sq[:, :, :], X, ALU.add))
                    own.done(nc.vector.tensor_scalar(ss[:, :], ss[:, :], 1.0 / D, 4e-6, ALU.mult, ALU.add))
                    rsqrt(nc, own, rstd[:, :], ss[:, :], tmp[:, :])
                    dve.wait_ge(kn_stored.sem, kn_stored.at(b, 0))
                    for t in range(T):
                        last = nc.vector.scalar_tensor_tensor(kn[:, t, :], sk[:, t, :], rstd[:, t:t + 1], K("knorm"), ALU.mult, ALU.mult)
                    last.then_inc(kn_ready.sem, 1)
                    dve.wait_ge(kn_ready.sem, kn_ready.at(b, 1))

                def gates(b):
                    dve.wait_ge(prod_ready.sem, prod_ready.at(b, 1))
                    own.hold(nc)
                    for w in range(3):
                        last = nc.vector.tensor_reduce(R[:, bass.ds(b * T + w * NT, T)], prod[:, w], X, ALU.add)
                    last.then_inc(prod_free.sem, 1)

                own.start(0, -NORMALISE_STEPS)
                norm(0)
                with dve.Fori(0, NB - 1) as b:
                    own.start(b)
                    silu(b)
                    dve.wait_ge(prod_ready.sem, prod_ready.at(b, 1))
                    norm(b + 1)
                    keys(b)
                    gates(b)
                    own.end()
                own.start(NB - 1)
                silu(NB - 1)
                keys(NB - 1)
                gates(NB - 1)
                dve.wait_ge(prod_free.sem, prod_free.at(NB, 0))


def learn(nc, ctx0, K, ps, bank, kn_d, vn_d, R, mem, memw1):
    with ExitStack() as ctx:
        def sb(name, shape, dt=F32):
            return ctx.enter_context(nc.sbuf_tensor("m_" + name, shape, dt))

        M = 2 * INTER + D
        kn = [sb(f"kn{i}", [P, CT, D]) for i in range(2)]
        vn = [sb(f"vn{i}", [P, CT, D]) for i in range(2)]
        kv = sb("kv", [P, CT, D])
        kt = sb("kt", [P, CT * P])
        tz = sb("tz", [P, CT, INTER])
        hid = sb("hid", [P, CT, INTER])
        slope = sb("slope", [P, CT, INTER])
        hs = sb("hs", [P, CT, INTER])
        ht = sb("ht", [P, 2, CT * P])
        ys = sb("ys", [P, CT, D])
        nrm = sb("nrm", [P, CT, D])
        e = sb("e", [P, CT, D])
        en = sb("en", [P, CT, D])
        dn = sb("dn", [P, CT, D])
        dy = sb("dy", [P, CT, D])
        dyt = sb("dyt", [P, CT * P])
        dz = sb("dz", [P, CT, INTER])
        keep = sb("keep", [P, M])
        surp = sb("surp", [P, M])
        sqs = sb("sqs", [P, M])
        logits = sb("logits", [P, 2, 3 * NT])
        tgate = sb("tgate", [P, 2, NT])
        decay = sb("decay", [P, 3, 2, T])
        th = sb("th", [P, NC, CT])
        eta_beta = sb("eta_beta", [P, NC, 2])
        eb = sb("eb", [P, 2])
        ths = sb("ths", [P, CT])
        ss = sb("ss", [P, CT])
        r = sb("r", [P, CT])
        tmp = sb("tmp", [P, CT])
        dot = sb("dot", [P, CT])
        gs = sb("gs", [P, 4])
        tot = sb("tot", [P, 1])
        rt = sb("rt", [P, 1])
        t1 = sb("t1", [P, 1])
        clip = sb("clip", [P, 1])

        def S1(name, **kw):
            return Signal(ctx0, nc, "m_" + name, **kw)

        gate_sums = S1("gate_sums")
        gate_copied = S1("gate_copied")
        gate_means = S1("gate_means")
        gate_tanh = S1("gate_tanh")
        kv_loaded = [S1(f"kv_loaded{i}", per=2, unit=16) for i in range(2)]
        step_done = S1("step_done", first=1)
        kt_ready = S1("kt_ready")
        kt_copied = S1("kt_copied")
        z_ready = S1("z_ready")
        tanh_ready = S1("tanh_ready")
        h_ready = S1("h_ready")
        slope_ready = S1("slope_ready", per=3)
        kv_ready = S1("kv_ready")
        ht_ready = S1("ht_ready")
        ht_copied = S1("ht_copied")
        y_ready = S1("y_ready")
        y_copied = S1("y_copied")
        y_squared = S1("y_squared")
        e_ready = S1("e_ready")
        en_ready = S1("en_ready")
        dy_ready = S1("dy_ready")
        dyt_ready = S1("dyt_ready")
        dyt_copied = S1("dyt_copied")
        dh_ready = S1("dh_ready")
        dz_ready = S1("dz_ready")
        grads_ready = S1("grads_ready")
        squares_ready = S1("squares_ready", per=3)
        part_ready = S1("part_ready")
        norm_ready = S1("norm_ready")
        keep_ready = S1("keep_ready")
        mem_ready = S1("mem_ready")
        w1_ready = S1("w1_ready")
        w1_copied = S1("w1_copied")

        w0t = mem[:, 0:INTER]
        w1t = [mem[:, INTER + f * D:INTER + (f + 1) * D] for f in range(2)]
        ln = mem[:, 2 * INTER:M]

        def tiles(ap, w):
            return ap.rearrange("p (t w) -> p t w", w=w)

        z_ps = ps[:, 0:4, :].rearrange("p b (t w) -> p (b t) w", w=INTER)
        y_ps = ps[:, 0:2, :].rearrange("p b (t w) -> p (b t) w", w=D)
        ht_ps = ps[:, 4:8, :].rearrange("p (f b) w -> p f (b w)", f=2)
        kt_ps = ps[:, 4:6, :].rearrange("p b w -> p (b w)")
        dyt_ps = ps[:, 2:4, :].rearrange("p b w -> p (b w)")
        dh_ps = ps[:, 4:8, :].rearrange("p b (t w) -> p (b t) w", w=INTER)
        g_w = ps[:, 0, :]
        g_ln = ps[:, 1, 0:D]
        norm_ps = ps[:, 2, 0:1]
        w1_ps = ps[:, 3, 0:INTER]

        with nc.Block() as block:
            @block.sync
            def _(sp):
                sp.dma_start(kn[0][:, :, :], kn_d[0].rearrange("(t p) d -> p t d", p=P)).then_inc(kv_loaded[0].sem, 16)
                sp.dma_start(vn[0][:, :, :], vn_d[0].rearrange("(t p) d -> p t d", p=P)).then_inc(kv_loaded[0].sem, 16)
                sp.dma_start(kn[1][:, :, :], kn_d[1].rearrange("(t p) d -> p t d", p=P)).then_inc(kv_loaded[1].sem, 16)
                sp.dma_start(vn[1][:, :, :], vn_d[1].rearrange("(t p) d -> p t d", p=P)).then_inc(kv_loaded[1].sem, 16)
                with sp.Fori(0, NC // 2 - 1) as pair:
                    c = pair * 2
                    for u in range(2):
                        sp.wait_ge(grads_ready.sem, grads_ready.at(c, u + 1))
                        sp.dma_start(kn[u][:, :, :], kn_d[bass.ds(c + (u + 2), 1)].rearrange("o (t p) d -> p (o t) d", p=P)
                                     ).then_inc(kv_loaded[u].sem, 16)
                        sp.dma_start(vn[u][:, :, :], vn_d[bass.ds(c + (u + 2), 1)].rearrange("o (t p) d -> p (o t) d", p=P)
                                     ).then_inc(kv_loaded[u].sem, 16)

            @block.tensor
            def _(pe):
                for h in range(2):
                    last = nc.tensor.matmul(bank[6 + h][:, 0:3 * NT], K("half", h * D, D), R[:, :], start=True, stop=True)
                last.then_inc(gate_sums.sem, 1)
                pe.wait_ge(gate_copied.sem, 1)
                with pe.Fori(0, NC // 2) as pair:
                    c = pair * 2
                    for u in range(2):
                        pe.wait_ge(kv_loaded[u].sem, c * 16 + 32)
                        pe.wait_ge(step_done.sem, step_done.at(c, u))
                        for t in range(CT):
                            last = nc.tensor.transpose(kt_ps[:, t * P:(t + 1) * P], kn[u][:, t, :], K("ident"))
                        last.then_inc(kt_ready.sem, 1)
                        pe.wait_ge(kt_copied.sem, kt_copied.at(c, u + 1))
                        for t in range(CT):
                            last = nc.tensor.matmul(z_ps[:, t, :], kt[:, t * P:(t + 1) * P], w0t, start=True, stop=True)
                        last.then_inc(z_ready.sem, 1)
                        pe.wait_ge(h_ready.sem, h_ready.at(c, u + 1))
                        for f in range(2):
                            for t in range(CT):
                                last = nc.tensor.transpose(ht_ps[:, f, t * P:(t + 1) * P], hid[:, t, f * P:(f + 1) * P], K("ident"))
                        last.then_inc(ht_ready.sem, 1)
                        pe.wait_ge(ht_copied.sem, ht_copied.at(c, u + 1))
                        for t in range(CT):
                            for f in range(2):
                                last = nc.tensor.matmul(y_ps[:, t, :], ht[:, f, t * P:(t + 1) * P], w1t[f], start=f == 0, stop=f == 1)
                        last.then_inc(y_ready.sem, 1)
                        pe.wait_ge(dy_ready.sem, dy_ready.at(c, u + 1))
                        for t in range(CT):
                            last = nc.tensor.transpose(dyt_ps[:, t * P:(t + 1) * P], dy[:, t, :], K("ident"))
                        last.then_inc(dyt_ready.sem, 1)
                        for f in range(2):
                            for t in range(CT):
                                nc.tensor.matmul(g_w[:, INTER + f * D:INTER + (f + 1) * D], hid[:, t, f * P:(f + 1) * P], dy[:, t, :],
                                                 start=t == 0, stop=t == CT - 1)
                        pe.wait_ge(dyt_copied.sem, dyt_copied.at(c, u + 1))
                        for t in range(CT):
                            last = nc.tensor.matmul(dh_ps[:, t, :], dyt[:, t * P:(t + 1) * P], memw1[:, :], start=True, stop=True)
                        last.then_inc(dh_ready.sem, 1)
                        pe.wait_ge(en_ready.sem, en_ready.at(c, u + 1))
                        for t in range(CT):
                            nc.tensor.matmul(g_ln, K("ones"), en[:, t, :], start=t == 0, stop=t == CT - 1)
                        pe.wait_ge(dz_ready.sem, dz_ready.at(c, u + 1))
                        for t in range(CT):
                            last = nc.tensor.matmul(g_w[:, 0:INTER], kn[u][:, t, :], dz[:, t, :], start=t == 0, stop=t == CT - 1)
                        last.then_inc(grads_ready.sem, 1)
                        pe.wait_ge(part_ready.sem, part_ready.at(c, u + 1))
                        nc.tensor.matmul(norm_ps, K("ones"), gs[:, 3:4], start=True, stop=True).then_inc(norm_ready.sem, 1)
                        pe.wait_ge(mem_ready.sem, mem_ready.at(c, u + 1))
                        for f in range(2):
                            last = nc.tensor.transpose(w1_ps[:, f * P:(f + 1) * P], w1t[f], K("ident"))
                        last.then_inc(w1_ready.sem, 1)

            @block.scalar
            def _(act):
                act.wait_ge(gate_sums.sem, 1)
                nc.scalar.activation(logits[:, 0, :], bank[6][:, 0:3 * NT], ACT.Copy)
                nc.scalar.activation(logits[:, 1, :], bank[7][:, 0:3 * NT], ACT.Copy).then_inc(gate_copied.sem, 1)
                act.wait_ge(gate_copied.sem, 1)
                nc.scalar.activation(tgate[:, :, :], logits[:, :, NT:2 * NT], ACT.Tanh, scale=0.5)
                act.wait_ge(gate_means.sem, 1)
                nc.scalar.activation(decay[:, :, :, :], decay[:, :, :, :], ACT.Tanh, scale=0.5 / NB).then_inc(gate_tanh.sem, 1)
                with act.Fori(0, NC // 2) as pair:
                    c = pair * 2
                    for u in range(2):
                        act.wait_ge(kt_ready.sem, kt_ready.at(c, u + 1))
                        nc.scalar.activation(kt[:, :], kt_ps, ACT.Copy).then_inc(kt_copied.sem, 1)
                        act.wait_ge(z_ready.sem, z_ready.at(c, u + 1))
                        nc.scalar.activation(tz[:, :, :], z_ps, ACT.Tanh, scale=0.5).then_inc(tanh_ready.sem, 1)
                        act.wait_ge(ht_ready.sem, ht_ready.at(c, u + 1))
                        nc.scalar.activation(ht[:, :, :], ht_ps, ACT.Copy).then_inc(ht_copied.sem, 1)
                        act.wait_ge(y_ready.sem, y_ready.at(c, u + 1))
                        nc.scalar.activation(ys[:, :, :], y_ps, ACT.Copy).then_inc(y_copied.sem, 1)
                        act.wait_ge(y_copied.sem, y_copied.at(c, u + 1))
                        nc.scalar.activation(nrm[:, :, :], ys[:, :, :], ACT.Square).then_inc(y_squared.sem, 1)
                        act.wait_ge(dyt_ready.sem, dyt_ready.at(c, u + 1))
                        nc.scalar.activation(dyt[:, :], dyt_ps, ACT.Copy).then_inc(dyt_copied.sem, 1)
                        act.wait_ge(grads_ready.sem, grads_ready.at(c, u + 1))
                        nc.scalar.activation(sqs[:, 0:INTER], g_w[:, 0:INTER], ACT.Square, accum_out=gs[:, 0:1]).then_inc(squares_ready.sem, 1)
                        nc.scalar.activation(sqs[:, INTER:2 * INTER], g_w[:, INTER:2 * INTER], ACT.Square, accum_out=gs[:, 1:2]).then_inc(squares_ready.sem, 1)
                        nc.scalar.activation(sqs[:, 2 * INTER:M], g_ln, ACT.Square, accum_out=gs[:, 2:3]).then_inc(squares_ready.sem, 1)
                        act.wait_ge(w1_ready.sem, w1_ready.at(c, u + 1))
                        nc.scalar.activation(memw1[:, :], w1_ps, ACT.Copy).then_inc(w1_copied.sem, 1)

            @block.gpsimd
            def _(pool):
                with pool.Fori(0, NC // 2) as pair:
                    c = pair * 2
                    for u in range(2):
                        pool.wait_ge(kv_loaded[u].sem, c * 16 + 32)
                        pool.wait_ge(step_done.sem, step_done.at(c, u))
                        nc.gpsimd.tensor_tensor(kv[:, :, :], kn[u][:, :, :], vn[u][:, :, :], ALU.subtract).then_inc(kv_ready.sem, 1)
                        pool.wait_ge(h_ready.sem, h_ready.at(c, u + 1))
                        nc.gpsimd.tensor_tensor(hs[:, :, :], hid[:, :, :], tz[:, :, :], ALU.mult).then_inc(slope_ready.sem, 1)
                        nc.gpsimd.tensor_tensor(slope[:, :, :], hid[:, :, :], tz[:, :, :], ALU.add).then_inc(slope_ready.sem, 1)
                        pool.wait_ge(slope_ready.sem, slope_ready.at(c, 3 * u + 2))
                        nc.gpsimd.tensor_tensor(slope[:, :, :], slope[:, :, :], hs[:, :, :], ALU.subtract).then_inc(slope_ready.sem, 1)
                        pool.wait_ge(e_ready.sem, e_ready.at(c, u + 1))
                        nc.gpsimd.tensor_tensor(en[:, :, :], e[:, :, :], nrm[:, :, :], ALU.mult).then_inc(en_ready.sem, 1)

            @block.vector
            def _(dve):
                setup = Own(ctx0, nc, "m_setup", dve, 4)
                setup.start(0)
                setup.done(nc.vector.tensor_copy(mem[:, :], K("mem")))
                setup.done(nc.vector.tensor_copy(memw1[:, :], K("memw1")))
                setup.done(nc.vector.memset(surp[:, :], 0.0))
                dve.wait_ge(gate_copied.sem, 1)
                for g in range(3):
                    last = nc.vector.tensor_reduce(decay[:, g], logits[:, :, g * NT:(g + 1) * NT].rearrange("p h (b t) -> p h t b", t=T), X, ALU.add)
                last.then_inc(gate_means.sem, 1)
                dve.wait_ge(gate_tanh.sem, 1)
                k_th = 0.01 * 0.5 * 2.0 / (NB * CHUNK * D)
                for half in range(2):
                    rows = slice(half * CHUNK, (half + 1) * CHUNK)
                    for h in range(2):
                        src = tgate[rows, h, :].rearrange("p (t b q) -> p t b q", b=2, q=T)[:, :, half, :]
                        dst = th[rows, :, :].rearrange("p (q h) t -> p t h q", h=2)[:, :, h, :]
                        nc.vector.tensor_scalar(dst, src, 1.0, k_th, ALU.add, ALU.mult)
                for h in range(2):
                    dst = eta_beta[:, :, :].rearrange("p (q h) x -> p h q x", h=2)[:, h]
                    nc.vector.tensor_scalar(dst[:, :, 0], decay[:, 2, h, :], 0.5, 0.5, ALU.mult, ALU.add)
                    last = nc.vector.tensor_scalar(dst[:, :, 1], decay[:, 0, h, :], -0.5, 0.5, ALU.mult, ALU.add)
                setup.done(last)
                nc.vector.sem_inc(step_done.sem, 1)
                steps = 21 + 2 * RSQRT_STEPS
                own = Own(ctx0, nc, "m_own", dve, steps)
                with dve.Fori(0, NC // 2) as pair:
                    c = pair * 2
                    for u in range(2):
                        own.start(c)
                        own.k = u * steps
                        own.hold(nc)
                        nc.vector.tensor_copy(eb[:, :], eta_beta[:, bass.ds(c + u, 1), :].rearrange("p o x -> p (o x)"))
                        own.done(nc.vector.tensor_copy(ths[:, :], th[:, bass.ds(c + u, 1), :].rearrange("p o x -> p (o x)")))
                        dve.wait_ge(tanh_ready.sem, tanh_ready.at(c, u + 1))
                        own.done(nc.vector.tensor_scalar(tz[:, :, :], tz[:, :, :], 0.5, 0.5, ALU.mult, ALU.add))
                        nc.vector.tensor_tensor(hid[:, :, :], tz[:, :, :], z_ps, ALU.mult).then_inc(h_ready.sem, 1)
                        own.done(nc.vector.tensor_scalar(keep[:, :], surp[:, :], eb[:, 0:1], None, ALU.mult))
                        dve.wait_ge(y_squared.sem, y_squared.at(c, u + 1))
                        own.done(nc.vector.tensor_reduce(ss[:, :], nrm[:, :, :], X, ALU.add))
                        own.done(nc.vector.tensor_scalar(ss[:, :], ss[:, :], 1.0 / D, 1e-6, ALU.mult, ALU.add))
                        rsqrt(nc, own, r[:, :], ss[:, :], tmp[:, :])
                        own.done(nc.vector.tensor_tensor(nrm[:, :, :], ys[:, :, :], along(r[:, :], D), ALU.mult))
                        own.done(nc.vector.tensor_tensor(e[:, :, :], nrm[:, :, :], over(ln, CT), ALU.mult))
                        dve.wait_ge(kv_ready.sem, kv_ready.at(c, u + 1))
                        own.done(nc.vector.tensor_tensor(e[:, :, :], e[:, :, :], kv[:, :, :], ALU.add))
                        nc.vector.tensor_tensor(e[:, :, :], e[:, :, :], along(ths[:, :], D), ALU.mult).then_inc(e_ready.sem, 1)
                        dve.wait_ge(e_ready.sem, e_ready.at(c, u + 1))
                        own.done(nc.vector.tensor_tensor(dn[:, :, :], e[:, :, :], over(ln, CT), ALU.mult))
                        own.done(nc.vector.tensor_tensor(dy[:, :, :], dn[:, :, :], nrm[:, :, :], ALU.mult))
                        own.done(nc.vector.tensor_reduce(dot[:, :], dy[:, :, :], X, ALU.add))
                        own.done(nc.vector.tensor_scalar(dot[:, :], dot[:, :], 1.0 / D, None, ALU.mult))
                        own.done(nc.vector.tensor_tensor(dy[:, :, :], nrm[:, :, :], along(dot[:, :], D), ALU.mult))
                        own.done(nc.vector.tensor_tensor(dy[:, :, :], dn[:, :, :], dy[:, :, :], ALU.subtract))
                        nc.vector.tensor_tensor(dy[:, :, :], dy[:, :, :], along(r[:, :], D), ALU.mult).then_inc(dy_ready.sem, 1)
                        dve.wait_ge(slope_ready.sem, slope_ready.at(c, 3 * u + 3))
                        dve.wait_ge(dh_ready.sem, dh_ready.at(c, u + 1))
                        nc.vector.tensor_tensor(dz[:, :, :], slope[:, :, :], dh_ps, ALU.mult).then_inc(dz_ready.sem, 1)
                        dve.wait_ge(squares_ready.sem, squares_ready.at(c, 3 * u + 3))
                        own.done(nc.vector.scalar_tensor_tensor(gs[:, 3:4], gs[:, 2:3], 1.0 / P, gs[:, 0:1], ALU.mult, ALU.add))
                        nc.vector.tensor_tensor(gs[:, 3:4], gs[:, 3:4], gs[:, 1:2], ALU.add).then_inc(part_ready.sem, 1)
                        dve.wait_ge(norm_ready.sem, norm_ready.at(c, u + 1))
                        own.done(nc.vector.tensor_scalar(tot[:, :], norm_ps, 1e-36, None, ALU.max))
                        rsqrt(nc, own, rt[:, :], tot[:, :], t1[:, :])
                        own.done(nc.vector.tensor_tensor(rt[:, :], rt[:, :], tot[:, :], ALU.mult))
                        own.done(nc.vector.tensor_scalar(rt[:, :], rt[:, :], 1e-6, None, ALU.add))
                        own.done(nc.vector.reciprocal(clip[:, :], rt[:, :]))
                        own.done(nc.vector.tensor_scalar(clip[:, :], clip[:, :], 1.0, -1.0, ALU.min, ALU.mult))
                        nc.vector.scalar_tensor_tensor(surp[:, 0:2 * INTER], g_w, clip[:, 0:1], keep[:, 0:2 * INTER], ALU.mult, ALU.add)
                        own.done(nc.vector.scalar_tensor_tensor(surp[:, 2 * INTER:M], g_ln, clip[:, 0:1], keep[:, 2 * INTER:M], ALU.mult, ALU.add))
                        nc.vector.scalar_tensor_tensor(mem[:, :], mem[:, :], eb[:, 1:2], surp[:, :], ALU.mult, ALU.add).then_inc(mem_ready.sem, 1)
                        dve.wait_ge(mem_ready.sem, mem_ready.at(c, u + 1))
                        dve.wait_ge(w1_copied.sem, w1_copied.at(c, u + 1))
                        nc.vector.sem_inc(step_done.sem, 1)
                        assert own.k == (u + 1) * steps, own.k
                dve.wait_ge(step_done.sem, step_done.at(NC, 0))


PARTS = 6
Q_PARTS = (0, 0, 0, 1, 1, 2)
K_PARTS = (0, 1, 2, 0, 1, 0)
SHIFT = PARTS * DH


SLOTS = G * T
UNITS = H * T
PAIRS = UNITS // 2
GROUP_PAIRS = PAIRS // G


def copied(engine, i, name):
    register = engine.alloc_register(name)
    engine.reg_mov(register, i)
    return engine.snap(register, min_val=0, max_val=NB)


class TurnAttention:

    def __init__(self, ctx, csem, nc, K, ps, bank, name, causal, turns, m_slots, loads):
        def sb(n, shape, dt=F32):
            return ctx.enter_context(nc.sbuf_tensor(f"{name}_{n}", shape, dt))

        def sig(n, per, first=0, unit=1):
            return Signal(csem, nc, f"{name}_{n}", per=per * turns, first=first, unit=unit)

        self.name = name
        self.nc, self.K, self.ps, self.bank, self.causal, self.turns = nc, K, ps, bank, causal, turns
        self.m_slots, self.loads = m_slots, loads
        self.s_banks = [bank[0], bank[1]]
        self.m_banks = [ps[:, 2:4, :], ps[:, 4:6, :]]
        self.qk = sb("qk", [P, 2, S])
        self.part = [sb(f"part{n}", [P, 2, S], BF16) for n in range(3)]
        self.rest = sb("rest", [P, 2, S])
        self.qa = [sb(f"qa{n}", [P, H, S], BF16) for n in range(2)]
        self.ka = [sb(f"ka{n}", [P, H, S], BF16) for n in range(2)]
        self.zero = sb("zero", [2, S], BF16)
        self.one = sb("one", [2, S], BF16)
        self.v = [sb(f"v{n}", [P, T, H * 32]) for n in range(2)]
        self.maxima = sb("maxima", [P, 2, HG * T])
        self.shift = sb("shift", [HG * T, 2, P], BF16)
        self.prob = sb("prob", [P, 2, HG, S])
        self.c = sb("c", [P, S])
        self.rsum = sb("rsum", [P, T, HG])
        self.ctxn = sb("ctxn", [P, T, D])
        if causal:
            self.mask = [sb(f"mask{n}", [P, P], BF16) for n in range(2)]
            self.identb = sb("identb", [P, P], BF16)
        self.setup_done = Signal(csem, nc, f"{name}_setup_done")
        self.ones_loaded = Signal(csem, nc, f"{name}_ones_loaded", unit=16)
        self.qk_ready = sig("qk_ready", 1, first=1)
        self.hi_ready = sig("hi_ready", 1, first=1)
        self.rest_ready = sig("rest_ready", 1, first=2)
        self.mid_ready = sig("mid_ready", 1, first=1)
        self.lo_ready = sig("lo_ready", 1, first=1)
        self.rows_loaded = Signal(csem, nc, f"{name}_rows_loaded", per=sum(loads), first=loads[-1] + 1, unit=16)
        self.m_ready = sig("m_ready", PAIRS, first=PAIRS)
        self.m_free = sig("m_free", PAIRS, first=PAIRS + 2)
        self.maxt_ready = sig("maxt_ready", G, first=G)
        self.shift_ready = sig("shift_ready", G, first=G)
        self.shift_loaded = sig("shift_loaded", 2 * G, first=2 * G + 2, unit=16)
        self.s_ready = sig("s_ready", UNITS, first=1)
        self.s_free = sig("s_free", UNITS, first=2)
        self.pv_ready = sig("pv_ready", SLOTS, first=2)
        self.c_copied = sig("c_copied", G, first=1)
        self.ct_ready = sig("ct_ready", G, first=1)
        self.ctxn_ready = sig("ctxn_ready", 1)
        self.ctxt_ready = sig("ctxt_ready", 1, first=1)
        self.misc_free = None
        self.misc_used = 0

    def setup_pool(self, pool):
        nc = self.nc
        for n in range(2):
            nc.gpsimd.memset(self.qa[n][:, :, :], 0.0)
            nc.gpsimd.memset(self.ka[n][:, :, :], 0.0)
        nc.gpsimd.memset(self.zero[:, :], 0.0)
        last = nc.gpsimd.memset(self.one[:, :], 1.0)
        if self.causal:
            nc.gpsimd.tensor_copy(self.mask[0][:, :], self.K("maskq"))
            nc.gpsimd.tensor_copy(self.mask[1][:, :], self.K("maskk"))
            last = nc.gpsimd.tensor_copy(self.identb[:, :], self.K("ident"))
        last.then_inc(self.setup_done.sem, 1)

    def setup_sync(self, sp):
        sp.wait_ge(self.setup_done.sem, 1)
        for n in range(2):
            sp.dma_start(self.ka[n][SHIFT:SHIFT + 2, :, :], self.one[0:2, :].unsqueeze(1).broadcast_to([2, H, S])
                         ).then_inc(self.ones_loaded.sem, 16)
        sp.sem_inc(self.rows_loaded.sem, 16)
        sp.sem_inc(self.shift_loaded.sem, 32)

    def setup_tensor(self, pe):
        pe.sem_inc(self.s_ready.sem, 1)
        pe.sem_inc(self.pv_ready.sem, 2)
        pe.sem_inc(self.ct_ready.sem, 1)
        pe.sem_inc(self.ctxt_ready.sem, 1)
        pe.wait_ge(self.ones_loaded.sem, 32)
        pe.wait_ge(self.setup_done.sem, 1)

    def setup_scalar(self, act):
        act.sem_inc(self.s_free.sem, 2)
        act.sem_inc(self.c_copied.sem, 1)
        act.wait_ge(self.setup_done.sem, 1)

    def setup_vector(self, dve):
        dve.sem_inc(self.rest_ready.sem, 1)
        dve.sem_inc(self.m_free.sem, 2)
        dve.sem_inc(self.misc_free.sem, 1)
        dve.wait_ge(self.setup_done.sem, 1)

    def before_qk(self, act, i, a):
        act.wait_ge(self.rest_ready.sem, self.rest_ready.at(i, a))

    def loaded_before(self, a):
        return sum(self.loads[:a])

    def split_hi(self, act, i, a, n):
        act.wait_ge(self.qk_ready.sem, self.qk_ready.at(i, a + 1))
        act.wait_ge(self.rows_loaded.sem, self.rows_loaded.at(i, self.loaded_before(a)))
        self.nc.scalar.activation(self.part[0][:, 0:n, :], self.qk[:, 0:n, :], ACT.Copy).then_inc(self.hi_ready.sem, 1)

    def split_rest(self, dve, i, a, n):
        dve.wait_ge(self.hi_ready.sem, self.hi_ready.at(i, a + 1))
        self.nc.vector.tensor_tensor(self.rest[:, 0:n, :], self.qk[:, 0:n, :], self.part[0][:, 0:n, :], ALU.subtract
                                     ).then_inc(self.rest_ready.sem, 1)

    def split_mid(self, act, i, a, n):
        act.wait_ge(self.rest_ready.sem, self.rest_ready.at(i, a + 1))
        self.nc.scalar.activation(self.part[1][:, 0:n, :], self.rest[:, 0:n, :], ACT.Copy).then_inc(self.mid_ready.sem, 1)

    def split_lo(self, dve, i, a, n):
        dve.wait_ge(self.mid_ready.sem, self.mid_ready.at(i, a + 1))
        self.nc.vector.tensor_tensor(self.part[2][:, 0:n, :], self.rest[:, 0:n, :], self.part[1][:, 0:n, :], ALU.subtract
                                     ).then_inc(self.lo_ready.sem, 1)

    def load_rows(self, sp, i, a, n):
        b = (a + 1) % 2
        sp.wait_ge(self.lo_ready.sem, self.lo_ready.at(i, a + 1))
        sem = self.rows_loaded.sem
        sp.dma_start(self.qa[b][SHIFT:SHIFT + 2, :, :], self.zero[0:2, :].unsqueeze(1).broadcast_to([2, H, S])).then_inc(sem, 16)
        for r in range(PARTS):
            rows = slice(r * DH, (r + 1) * DH)
            sp.dma_start(self.qa[b][rows, :, :], self.part[Q_PARTS[r]][:, 0, :]).then_inc(sem, 16)
            if n == 2:
                sp.dma_start(self.ka[b][rows, :, :], self.part[K_PARTS[r]][:, 1, :]).then_inc(sem, 16)

    def load_shifts(self, sp, i, a):
        b = (a + 1) % 2
        for g in range(G):
            sp.wait_ge(self.shift_ready.sem, self.shift_ready.at(i, a * G + g + 1))
            for w in range(2):
                sp.dma_start(self.qa[b][SHIFT + w:SHIFT + w + 1, g * HG:(g + 1) * HG, :], self.shift[:, w, :]
                             ).then_inc(self.shift_loaded.sem, 16)

    def wait_misc(self, pe, i):
        pe.wait_ge(self.misc_free.sem, self.misc_free.at(i, self.misc_used))
        self.misc_used += 1

    def max_units(self, a, slot):
        return range(*self.m_slots[a][slot])

    def maxima_done(self, pe, i, a):
        pe.wait_ge(self.m_free.sem, self.m_free.at(i, a * PAIRS))

    def tensor_maxima(self, pe, i, a, k):
        nc, b = self.nc, (a + 1) % 2
        if k == 0:
            pe.wait_ge(self.rows_loaded.sem, self.rows_loaded.at(i, self.loaded_before(a + 1)))
        pair, t = divmod(k, T)
        w = (t + 1) * P if self.causal else S
        pe.wait_ge(self.m_free.sem, self.m_free.at(i, a * PAIRS + k - 1))
        for n in range(2):
            h, out = 2 * pair + n, self.m_banks[k % 2][:, n, :]
            last = nc.tensor.matmul(out[:, 0:w], self.qa[b][:, h, t * P:(t + 1) * P], self.ka[b][:, h, 0:w], start=True, stop=not self.causal)
            if self.causal:
                last = nc.tensor.matmul(out[:, t * P:w], self.identb[:, :], self.mask[0][:, :], start=False, stop=True)
        last.then_inc(self.m_ready.sem, 1)

    def tensor_turn_maxima(self, pe, i, a, g):
        pe.wait_ge(self.m_free.sem, self.m_free.at(i, a * PAIRS + (g + 1) * GROUP_PAIRS))
        self.wait_misc(pe, i)
        self.nc.tensor.transpose(self.bank[7][0:HG * T, 0:P], self.maxima[:, g % 2, :], self.K("ident")).then_inc(self.maxt_ready.sem, 1)

    def tensor_scores(self, pe, i, a, s, j):
        nc, b = self.nc, a % 2
        g, t = divmod(s, T)
        h, k = g * HG + j, s * HG + j
        if t == 0 and j == 0:
            pe.wait_ge(self.shift_loaded.sem, self.shift_loaded.at(i, 2 * G * (a - 1) + 2 * (g + 1)))
        pe.wait_ge(self.s_free.sem, self.s_free.at(i, a * UNITS + k - 1))
        q0 = t * P if self.causal else 0
        out = self.s_banks[k % len(self.s_banks)]
        last = nc.tensor.matmul(out[:, q0:S], self.ka[b][:, h, t * P:(t + 1) * P], self.qa[b][:, h, q0:S], start=True, stop=not self.causal)
        if self.causal:
            last = nc.tensor.matmul(out[:, q0:q0 + P], self.identb[:, :], self.mask[1][:, :], start=False, stop=True)
        last.then_inc(self.s_ready.sem, 1)

    def tensor_values(self, pe, i, a, s):
        nc, b = self.nc, a % 2
        g, t = divmod(s, T)
        pe.wait_ge(self.s_free.sem, self.s_free.at(i, a * UNITS + (s + 1) * HG))
        if t == 0:
            pe.wait_ge(self.c_copied.sem, self.c_copied.at(i, a * G + g))
        q0 = t * P if self.causal else 0
        for j in range(HG):
            h = g * HG + j
            last = nc.tensor.matmul(self.bank[6][32 * j:32 * (j + 1), q0:S], self.v[b][:, t, h * 32:(h + 1) * 32],
                                    self.prob[:, s % 2, j, q0:S], start=t == 0, stop=t == T - 1)
        last.then_inc(self.pv_ready.sem, 1)

    def tensor_turn_context(self, pe, i, a, g):
        pe.wait_ge(self.c_copied.sem, self.c_copied.at(i, a * G + g + 1))
        self.wait_misc(pe, i)
        for t in range(T):
            last = self.nc.tensor.transpose(self.bank[7][:, t * P:(t + 1) * P], self.c[:, t * P:(t + 1) * P], self.K("ident"))
        last.then_inc(self.ct_ready.sem, 1)

    def tensor_whole_context(self, pe, i, a):
        pe.wait_ge(self.ctxn_ready.sem, self.ctxn_ready.at(i, a + 1))
        self.wait_misc(pe, i)
        for t in range(T):
            last = self.nc.tensor.transpose(self.bank[7][:, t * P:(t + 1) * P], self.ctxn[:, t, :], self.K("ident"))
        last.then_inc(self.ctxt_ready.sem, 1)

    def tensor_turn(self, pe, i, a, extra):
        scores_i, maxima_i = copied(pe, i, f"{self.name}_scores{a}"), copied(pe, i, f"{self.name}_maxima{a}")
        for s in range(SLOTS):
            units = list(self.max_units(a, s))
            for j in range(HG):
                for k in units[j * len(units) // HG:(j + 1) * len(units) // HG]:
                    self.tensor_maxima(pe, maxima_i, a, k)
                self.tensor_scores(pe, scores_i, a, s, j)
            if s:
                self.tensor_values(pe, i, a, s - 1)
            elif a:
                self.tensor_values(pe, i, a - 1, SLOTS - 1)
            if s > T and s % T == 1:
                self.tensor_turn_context(pe, i, a, s // T - 1)
            elif s == 1 and a:
                self.tensor_turn_context(pe, i, a - 1, G - 1)
            for g in self.groups_ended(a, s):
                self.tensor_turn_maxima(pe, i, a, g)
            extra(s)

    def tensor_tail(self, pe, i, a):
        self.tensor_values(pe, i, a, SLOTS - 1)
        self.tensor_turn_context(pe, i, a, G - 1)

    def tensor_early(self, pe):
        a = self.turns - 1
        for k in range(PAIRS):
            self.tensor_maxima(pe, -1, a, k)
            if (k + 1) % GROUP_PAIRS == 0:
                self.tensor_turn_maxima(pe, -1, a, k // GROUP_PAIRS)

    def groups_ended(self, a, s):
        units = self.max_units(a, s)
        return [g for g in range(G) if (g + 1) * GROUP_PAIRS - 1 in units]

    def scalar_exponentials(self, act, i, a, s, j):
        g, t = divmod(s, T)
        k = s * HG + j
        if j == 0:
            act.wait_ge(self.pv_ready.sem, self.pv_ready.at(i, a * SLOTS + s - 1))
        act.wait_ge(self.s_ready.sem, self.s_ready.at(i, a * UNITS + k + 1))
        q0 = t * P if self.causal else 0
        self.nc.scalar.activation(self.prob[:, s % 2, j, q0:S], self.s_banks[k % len(self.s_banks)][:, q0:S], ACT.Exp, scale=SCALE
                                  ).then_inc(self.s_free.sem, 1)

    def scalar_context(self, act, i, a, g):
        act.wait_ge(self.pv_ready.sem, self.pv_ready.at(i, a * SLOTS + (g + 1) * T))
        act.wait_ge(self.ct_ready.sem, self.ct_ready.at(i, a * G + g))
        self.nc.scalar.activation(self.c[:, :], self.bank[6], ACT.Copy).then_inc(self.c_copied.sem, 1)

    def scalar_turn(self, act, i, a, extra):
        scores_i = copied(act, i, f"{self.name}_scores{a}")
        for s in range(SLOTS):
            for j in range(HG):
                self.scalar_exponentials(act, scores_i, a, s, j)
            if s and s % T == 0:
                self.scalar_context(act, i, a, s // T - 1)
            elif s == 0 and a:
                self.scalar_context(act, i, a - 1, G - 1)
            extra(s)

    def vector_maxima(self, dve, i, a, k):
        pair, t = divmod(k, T)
        g, j = divmod(2 * pair, HG)
        w = (t + 1) * P if self.causal else S
        out = self.maxima[:, g % 2, :].rearrange("p (j t) -> p j t", t=T)[:, j:j + 2, t]
        dve.wait_ge(self.m_ready.sem, self.m_ready.at(i, a * PAIRS + k + 1))
        self.nc.vector.reduce_max(out, self.m_banks[k % 2][:, :, 0:w], X).then_inc(self.m_free.sem, 1)

    def vector_shift(self, dve, i, a, g, own):
        nc = self.nc
        dve.wait_ge(self.maxt_ready.sem, self.maxt_ready.at(i, a * G + g + 1))
        dve.wait_ge(self.shift_loaded.sem, self.shift_loaded.at(i, 2 * (a * G + g)))
        own.done(nc.vector.tensor_scalar(self.shift[:, 0, :], self.bank[7][0:HG * T, 0:P], -1.0, None, ALU.mult))
        nc.vector.scalar_tensor_tensor(self.shift[:, 1, :], self.bank[7][0:HG * T, 0:P], -1.0, self.shift[:, 0, :], ALU.mult, ALU.subtract
                                       ).then_inc(self.shift_ready.sem, 1)
        dve.wait_ge(self.shift_ready.sem, self.shift_ready.at(i, a * G + g + 1))
        nc.vector.sem_inc(self.misc_free.sem, 1)

    def vector_context(self, dve, i, a, g, own):
        nc = self.nc
        dve.wait_ge(self.ct_ready.sem, self.ct_ready.at(i, a * G + g + 1))
        if g == 0:
            dve.wait_ge(self.ctxt_ready.sem, self.ctxt_ready.at(i, a))
        src = self.bank[7].rearrange("p (t j x) -> p t j x", t=T, x=32)
        own.done(nc.vector.reciprocal(self.rsum[:, :, :], src[:, :, :, DH]))
        out = self.ctxn[:, :, g * HG * DH:(g + 1) * HG * DH].rearrange("p t (j d) -> p t j d", d=DH)
        own.done(nc.vector.tensor_tensor(out, src[:, :, :, 0:DH], self.rsum[:, :, :].unsqueeze(3).broadcast_to([P, T, HG, DH]), ALU.mult))
        nc.vector.sem_inc(self.misc_free.sem, 1)
        if g == G - 1:
            nc.vector.sem_inc(self.ctxn_ready.sem, 1)


    def vector_turn(self, dve, i, a, own, extra):
        maxima_i = copied(dve, i, f"{self.name}_maxima{a}")
        for s in range(SLOTS):
            for k in self.max_units(a, s):
                self.vector_maxima(dve, maxima_i, a, k)
            if s > T and s % T == 1:
                self.vector_context(dve, i, a, s // T - 1, own)
            elif s == 1 and a:
                self.vector_context(dve, i, a - 1, G - 1, own)
            for g in self.groups_ended(a, s):
                self.vector_shift(dve, i, a, g, own)
            extra(s)

    def vector_early(self, dve, own):
        a = self.turns - 1
        for k in range(PAIRS):
            self.vector_maxima(dve, -1, a, k)
            if (k + 1) % GROUP_PAIRS == 0:
                self.vector_shift(dve, -1, a, k // GROUP_PAIRS, own)


SHIFT_STEPS = 1
CONTEXT_STEPS = 2


def spread(first, last=SLOTS):
    n = last - first
    cut = [round(PAIRS * max(0, min(n, s - first)) / n) for s in range(SLOTS + 1)]
    return [(cut[s], cut[s + 1]) for s in range(SLOTS)]


def attend0(nc, ctx0, K, ps, bank, xnt_d, xc_d, ctxt_d):
    with ExitStack() as ctx:
        def sb(name, shape, dt=F32):
            return ctx.enter_context(nc.sbuf_tensor("c_" + name, shape, dt))

        TURNS = 4
        LOOPS = NB // TURNS
        AHEAD = 3
        MAXIMA = 7

        def sig(name, **kw):
            return Signal(ctx0, nc, "c_" + name, **kw)

        xt = sb("xt", [P, S + 2])
        xc = sb("xc", [P, S])
        ctxt = sb("ctxt", [P, S])
        both = 1 + 2 * PARTS
        att = TurnAttention(ctx, ctx0, nc, K, ps, bank, "c", False, TURNS,
                            [spread(MAXIMA)] * TURNS, [both] * TURNS)
        misc = TURNS * (2 * G + 1)
        att.misc_free = sig("misc_free", per=misc, first=G + 1)

        copied_ahead = sig("copied_ahead", unit=16)
        edges_ready = sig("edges_ready")
        x_loaded = sig("x_loaded", per=TURNS, first=2, unit=16)
        conv_ready = sig("conv_ready", per=TURNS, first=1)
        xc_ready = sig("xc_ready", per=TURNS, first=1)
        xc_stored = sig("xc_stored", per=TURNS, first=1, unit=16)
        proj_ready = sig("proj_ready", per=TURNS, first=1)
        vp_ready = sig("vp_ready", per=TURNS * T, first=T)
        v_ready = sig("v_ready", per=TURNS * T, first=T)
        ctxt_copied = sig("ctxt_copied", per=TURNS)
        ctxt_stored = sig("ctxt_stored", per=TURNS, first=1, unit=16)

        with nc.Block() as block:
            @block.sync
            def _(sp):
                def load_x(item):
                    sp.dma_start(xt[:, 1:S + 1], xnt_d[bass.ds(item * P, P), :]).then_inc(x_loaded.sem, 16)

                def store_xc(item):
                    sp.dma_start(xc_d[bass.ds(item * P, P), :], xc[:, :]).then_inc(xc_stored.sem, 16)

                def store_context(i, a):
                    sp.wait_ge(ctxt_copied.sem, ctxt_copied.at(i, a + 1))
                    sp.dma_start(ctxt_d[bass.ds(i * (TURNS * P) + a * P, P), :], ctxt[:, :]).then_inc(ctxt_stored.sem, 16)

                sp.dma_start(xnt_d[NB * P:(NB + 2) * P, :], xnt_d[0:2 * P, :]).then_inc(copied_ahead.sem, 16)
                load_x(0)
                att.setup_sync(sp)
                sp.sem_inc(ctxt_stored.sem, 16)
                sp.wait_ge(conv_ready.sem, 1)
                load_x(1)
                sp.wait_ge(xc_ready.sem, 1)
                store_xc(0)
                sp.wait_ge(copied_ahead.sem, 16)
                att.load_rows(sp, -1, TURNS - 1, 2)
                att.load_shifts(sp, -1, TURNS - 1)
                with sp.Fori(0, LOOPS) as i:
                    for a in range(TURNS):
                        sp.wait_ge(conv_ready.sem, conv_ready.at(i, a + 1))
                        load_x(i * TURNS + (a + 2))
                        sp.wait_ge(xc_ready.sem, xc_ready.at(i, a + 1))
                        store_xc(i * TURNS + (a + 1))
                        att.load_rows(sp, i, a, 2)
                        if a:
                            store_context(i, a - 1)
                        att.load_shifts(sp, i, a)
                    store_context(i, TURNS - 1)
                sp.wait_ge(ctxt_stored.sem, ctxt_stored.at(LOOPS, 0))
                sp.wait_ge(xc_stored.sem, xc_stored.at(LOOPS, 0))
                sp.wait_ge(x_loaded.sem, x_loaded.at(LOOPS, 0))

            @block.gpsimd
            def _(pool):
                nc.gpsimd.memset(xt[:, 0:1], 0.0)
                nc.gpsimd.memset(xt[:, S + 1:S + 2], 0.0).then_inc(edges_ready.sem, 1)
                att.setup_pool(pool)

            @block.tensor
            def _(pe):
                def convolve():
                    for tap in range(3):
                        last = nc.tensor.matmul(bank[2], K("conv0", tap * D, D), xt[:, tap:tap + S], start=tap == 0, stop=tap == 2)
                    last.then_inc(conv_ready.sem, 1)

                def project(i, a):
                    pe.wait_ge(xc_ready.sem, xc_ready.at(i, a + 1))
                    nc.tensor.matmul(bank[2], K("q0"), xc[:, :], start=True, stop=True)
                    nc.tensor.matmul(bank[5], K("k0"), xc[:, :], start=True, stop=True).then_inc(proj_ready.sem, 1)

                def values(i, a, t):
                    if t < 2:
                        pe.wait_ge(att.qk_ready.sem, att.qk_ready.at(i, a + 1))
                    else:
                        pe.wait_ge(v_ready.sem, v_ready.at(i, a * T + t - 1))
                    nc.tensor.matmul(bank[2 if t % 2 == 0 else 5], xc[:, t * P:(t + 1) * P], K("v0"), start=True, stop=True
                                     ).then_inc(vp_ready.sem, 1)

                att.setup_tensor(pe)
                pe.wait_ge(edges_ready.sem, 1)
                att.misc_used = misc - G
                pe.wait_ge(x_loaded.sem, 16)
                convolve()
                project(-1, TURNS - 1)
                for t in range(T):
                    values(-1, TURNS - 1, t)
                pe.wait_ge(v_ready.sem, T)
                att.tensor_early(pe)
                with pe.Fori(0, LOOPS) as i:
                    att.misc_used = 0

                    def start(s, a):
                        if s == 0:
                            pe.wait_ge(x_loaded.sem, x_loaded.at(i, a))
                            att.maxima_done(pe, i, a)
                            convolve()
                        if s == 1:
                            project(i, a)
                        if s == 2 and a:
                            att.tensor_whole_context(pe, i, a - 1)
                        if AHEAD <= s < AHEAD + T:
                            values(i, a, s - AHEAD)
                        if s == MAXIMA - 1:
                            pe.wait_ge(v_ready.sem, v_ready.at(i, (a + 1) * T))

                    for a in range(TURNS):
                        att.tensor_turn(pe, i, a, lambda s: start(s, a))
                    att.tensor_tail(pe, i, TURNS - 1)
                    att.tensor_whole_context(pe, i, TURNS - 1)
                    assert att.misc_used == misc

            @block.scalar
            def _(act):
                cols = K("cols0")

                def convolved(i, a):
                    act.wait_ge(conv_ready.sem, conv_ready.at(i, a + 1))
                    nc.scalar.activation(xc[:, :], bank[2], ACT.Identity, bias=cols[:, 0:1]).then_inc(xc_ready.sem, 1)

                def queries_keys(i, a):
                    act.wait_ge(proj_ready.sem, proj_ready.at(i, a + 1))
                    att.before_qk(act, i, a)
                    nc.scalar.activation(att.qk[:, 0, :], bank[2], ACT.Identity, bias=cols[:, 1:2])
                    nc.scalar.activation(att.qk[:, 1, :], bank[5], ACT.Identity, bias=cols[:, 2:3]).then_inc(att.qk_ready.sem, 1)
                    att.split_hi(act, i, a, 2)

                def whole_context(i, a):
                    act.wait_ge(att.ctxt_ready.sem, att.ctxt_ready.at(i, a + 1))
                    act.wait_ge(ctxt_stored.sem, ctxt_stored.at(i, a))
                    nc.scalar.activation(ctxt[:, :], bank[7], ACT.Copy).then_inc(ctxt_copied.sem, 1)
                    act.wait_ge(ctxt_copied.sem, ctxt_copied.at(i, a + 1))
                    act.sem_inc(att.misc_free.sem, 1)

                att.setup_scalar(act)
                convolved(-1, TURNS - 1)
                queries_keys(-1, TURNS - 1)
                att.split_mid(act, -1, TURNS - 1, 2)
                with act.Fori(0, LOOPS) as i:
                    def start(s, a):
                        if s == 0:
                            act.wait_ge(xc_stored.sem, xc_stored.at(i, a))
                            act.wait_ge(vp_ready.sem, vp_ready.at(i, a * T))
                            convolved(i, a)
                        if s == 1:
                            queries_keys(i, a)
                        if s == 2:
                            att.split_mid(act, i, a, 2)
                            if a:
                                whole_context(i, a - 1)

                    for a in range(TURNS):
                        att.scalar_turn(act, i, a, lambda s: start(s, a))
                    att.scalar_context(act, i, TURNS - 1, G - 1)
                    whole_context(i, TURNS - 1)

            @block.vector
            def _(dve):
                def values(i, a, t):
                    dve.wait_ge(vp_ready.sem, vp_ready.at(i, a * T + t + 1))
                    nc.vector.tensor_tensor(att.v[(a + 1) % 2][:, t, :], bank[2 if t % 2 == 0 else 5], K("vbias0"), ALU.add
                                            ).then_inc(v_ready.sem, 1)

                att.setup_vector(dve)
                per = TURNS * G * (SHIFT_STEPS + CONTEXT_STEPS)
                own = Own(ctx0, nc, "c_own", dve, per, first=G * SHIFT_STEPS)
                own.start(-1, per - G * SHIFT_STEPS)
                att.split_rest(dve, -1, TURNS - 1, 2)
                att.split_lo(dve, -1, TURNS - 1, 2)
                for t in range(T):
                    values(-1, TURNS - 1, t)
                att.vector_early(dve, own)
                with dve.Fori(0, LOOPS) as i:
                    own.start(i)

                    def start(s, a):
                        if s == 1:
                            att.split_rest(dve, i, a, 2)
                        if s == 2:
                            att.split_lo(dve, i, a, 2)
                        if AHEAD <= s < AHEAD + T:
                            values(i, a, s - AHEAD)

                    for a in range(TURNS):
                        att.vector_turn(dve, i, a, own, lambda s: start(s, a))
                    att.vector_context(dve, i, TURNS - 1, G - 1, own)
                    own.end()


def mixture(nc, ctx0, K, ps, bank, x, xnt_d, xc_d, ctxt_d, mem, chosen, xnt2_d, table_d, sum_d):
    with ExitStack() as ctx:
        def sb(name, shape, dt=F32):
            return ctx.enter_context(nc.sbuf_tensor("a_" + name, shape, dt))

        def sig(name, **kw):
            return Signal(ctx0, nc, "a_" + name, **kw)

        def tiled(b):
            return bank[b].rearrange("p (t d) -> p t d", t=T)

        UNITS0 = E0 * FC
        xt = sb("xt", [P, S])
        xc = sb("xc", [P, S])
        ctxt = sb("ctxt", [P, S])
        xin = sb("xin", [P, T, D])
        zeros = sb("zeros", [P, D + E1])
        x1h = sb("x1h", [P, T, D])
        x1t = [sb(f"x1t{n}", [P, S]) for n in range(2)]
        gsm = sb("gsm", [P, T, E0])
        pexp = sb("pexp", [P, T, E0])
        gprob = [sb(f"gprob{n}", [P, T, E0]) for n in range(2)]
        gmax = sb("gmax", [P, T])
        rmax = sb("rmax", [P, T])
        gpt = sb("gpt", [P, S])
        acc = [sb(f"acc{n}", [P, T, D]) for n in range(2)]
        hid = sb("hid", [P, 2, FC, S])
        stats = sb("stats", [P, T, 6])
        mv = sb("mv", [P, T, 2])
        var = sb("var", [P, T])
        rstd = sb("rstd", [P, T])
        tmp = sb("tmp", [P, T])
        ss = sb("ss", [P, T])
        q2 = [sb(f"q2{n}", [P, T, D]) for n in range(2)]
        qt = sb("qt", [P, S])
        ht = sb("ht", [P, 2, S])
        yy = sb("yy", [P, T, D])
        sq = sb("sq", [P, T, D])
        x2 = sb("x2", [P, T, D])
        xn2 = sb("xn2", [P, T, D])
        xt2 = sb("xt2", [P, S])
        rl = sb("rl", [P, T, E1])
        top = sb("top", [P, T, 8])
        left = sb("left", [P, T, E1])
        wts = sb("wts", [P, T, E1])

        zero_ready = sig("zero_ready")
        zero_stored = sig("zero_stored", unit=16)
        xt_loaded = sig("xt_loaded", unit=16)
        context_loaded = sig("context_loaded", per=2, unit=16)
        xin_loaded = sig("xin_loaded", unit=16)
        mq_ready = sig("mq_ready")
        mqt_ready = sig("mqt_ready")
        mq2_ready = sig("mq2_ready")
        mqp_ready = sig("mqp_ready")
        mqtt_ready = sig("mqtt_ready")
        mz_ready = sig("mz_ready")
        mtanh_ready = sig("mtanh_ready")
        mh_ready = sig("mh_ready")
        my_ready = sig("my_ready")
        my_copied = sig("my_copied")
        my_squared = sig("my_squared")
        memory_ready = sig("memory_ready")
        z_ready = sig("z_ready")
        x1h_ready = sig("x1h_ready")
        x1p_ready = sig("x1p_ready")
        x1t_ready = sig("x1t_ready")
        gate_ready = sig("gate_ready")
        gsm_ready = sig("gsm_ready")
        gexp_ready = sig("gexp_ready")
        gprob_ready = sig("gprob_ready")
        gpp_ready = sig("gpp_ready")
        gpt_ready = sig("gpt_ready")
        base_ready = sig("base_ready")
        acc_ready = sig("acc_ready")
        up_ready = sig("up_ready", per=UNITS0)
        hid_ready = sig("hid_ready", per=UNITS0)
        down_ready = sig("down_ready", per=E0)
        down_used = sig("down_used", per=E0)
        sum_ready = sig("sum_ready")
        xn2_ready = sig("xn2_ready")
        xn2p_ready = sig("xn2p_ready")
        xt2_ready = sig("xt2_ready")
        route_ready = sig("route_ready")
        rl_ready = sig("rl_ready")
        rexp_ready = sig("rexp_ready")
        wts_ready = sig("wts_ready")
        sum_stored = sig("sum_stored", unit=16)
        xn2_stored = sig("xn2_stored", unit=16)
        xt2_stored = sig("xt2_stored", unit=16)
        wts_stored = sig("wts_stored", unit=16)

        def made(engine, signal, m):
            engine.wait_ge(signal.sem, signal.at(m, signal.per))

        def made_before(engine, signal, m, ago=1):
            if not isinstance(m, int) or m >= ago:
                engine.wait_ge(signal.sem, signal.at(m - ago, signal.per))

        def steps(engine, ahead, experts, behind, looped=lambda i: None, after=lambda: None):
            for e in range(E0):
                ahead(0, 0, e)
            experts(0, 0, lambda e: ahead(1, 1, e))
            with engine.Fori(0, NB // 2 - 1) as i:
                looped(i)
                for n in (1, 0):
                    m = i * 2 + (2 - n)

                    def between(e):
                        behind(m - 1, 1 - n, e)
                        ahead(m + 1, 1 - n, e)

                    experts(m, n, between)
            after()
            experts(NB - 1, 1, lambda e: behind(NB - 2, 0, e))
            for e in range(E0):
                behind(NB - 1, 1, e)

        with nc.Block() as block:
            @block.sync
            def _(sp):
                sp.wait_ge(zero_ready.sem, 1)
                sp.dma_start(table_d[N:ROWS, :], zeros[:, :]).then_inc(zero_stored.sem, 16)
                sp.dma_start(sum_d[N:ROWS, :], zeros[:, 0:D]).then_inc(zero_stored.sem, 16)
                sp.wait_ge(zero_stored.sem, 32)

                def ahead(m, n, e):
                    if e == 0:
                        made_before(sp, mq_ready, m)
                        sp.dma_start(xt[:, :], xnt_d[bass.ds(m * P, P), :]).then_inc(xt_loaded.sem, 16)
                        made_before(sp, z_ready, m)
                        sp.dma_start(xc[:, :], xc_d[bass.ds(m * P, P), :]).then_inc(context_loaded.sem, 16)
                        sp.dma_start(ctxt[:, :], ctxt_d[bass.ds(m * P, P), :]).then_inc(context_loaded.sem, 16)
                        made_before(sp, memory_ready, m)
                        sp.dma_start(xin[:, :, :], x[bass.ds(m, 1), :, :].rearrange("o (t p) d -> p (o t) d", p=P)
                                     ).then_inc(xin_loaded.sem, 16)

                def behind(m, n, e):
                    if e == 0:
                        made(sp, sum_ready, m)
                        sp.dma_start(sum_d[bass.ds(m * S, S), :].rearrange("(t p) d -> p t d", p=P), acc[n][:, :, :]
                                     ).then_inc(sum_stored.sem, 16)
                    if e == 1:
                        made(sp, xn2_ready, m)
                        sp.dma_start(table_d[bass.ds(m * S, S), 0:D].rearrange("(t p) d -> p t d", p=P), xn2[:, :, :]
                                     ).then_inc(xn2_stored.sem, 16)
                    if e == 2:
                        made(sp, xt2_ready, m)
                        sp.dma_start(xnt2_d[bass.ds(m * P, P), :], xt2[:, :]).then_inc(xt2_stored.sem, 16)
                    if e == 6:
                        made(sp, wts_ready, m)
                        sp.dma_start(table_d[bass.ds(m * S, S), D:D + E1].rearrange("(t p) d -> p t d", p=P), wts[:, :, :]
                                     ).then_inc(wts_stored.sem, 16)

                def experts(m, n, between):
                    for e in range(E0):
                        between(e)

                steps(sp, ahead, experts, behind)
                for signal in (sum_stored, xn2_stored, xt2_stored, wts_stored):
                    sp.wait_ge(signal.sem, signal.at(NB, 0))

            @block.tensor
            def _(pe):
                def ahead(m, n, e):
                    if e == 1:
                        made(pe, xt_loaded, m)
                        made_before(pe, my_copied, m)
                        for t in range(T):
                            last = nc.tensor.matmul(tiled(1)[:, t, :], xt[:, t * P:(t + 1) * P], K("wq"), start=True, stop=True)
                        last.then_inc(mq_ready.sem, 1)
                        made(pe, context_loaded, m)
                        made_before(pe, acc_ready, m)
                        for t in range(T):
                            cols = slice(t * P, (t + 1) * P)
                            nc.tensor.matmul(tiled(0)[:, t, :], ctxt[:, cols], K("out0"), start=True, stop=False)
                            nc.tensor.matmul(tiled(0)[:, t, :], xc[:, cols], K("ident"), start=False, stop=False)
                            last = nc.tensor.matmul(tiled(0)[:, t, :], K("ones")[0:1, :], K("outb0")[0:1, :], start=False, stop=True)
                        last.then_inc(z_ready.sem, 1)
                    if e == 3:
                        made(pe, x1h_ready, m)
                        for t in range(T):
                            last = nc.tensor.transpose(tiled(0)[:, t, :], x1h[:, t, :], K("ident"))
                        last.then_inc(x1p_ready.sem, 1)
                    if e == 4:
                        made(pe, x1t_ready, m)
                        for t in range(T):
                            nc.tensor.matmul(bank[0][:, t * E0:(t + 1) * E0], x1t[n][:, t * P:(t + 1) * P], K("gate0"), start=True, stop=False)
                            last = nc.tensor.matmul(bank[0][:, t * E0:(t + 1) * E0], K("ones")[0:1, :], K("gateb0")[0:1, :], start=False, stop=True)
                        last.then_inc(gate_ready.sem, 1)
                        made(pe, mq2_ready, m)
                        for t in range(T):
                            last = nc.tensor.transpose(tiled(1)[:, t, :], q2[n][:, t, :], K("ident"))
                        last.then_inc(mqp_ready.sem, 1)
                    if e == 5:
                        made(pe, gsm_ready, m)
                        made(pe, mqtt_ready, m)
                        for f in range(2):
                            last = nc.tensor.matmul(bank[f], mem[:, f * P:(f + 1) * P], qt[:, :], start=True, stop=True)
                        last.then_inc(mz_ready.sem, 1)
                    if e == 6:
                        made(pe, mh_ready, m)
                        for t in range(T):
                            for f in range(2):
                                last = nc.tensor.matmul(tiled(1)[:, t, :], ht[:, f, t * P:(t + 1) * P], mem[:, INTER + f * D:INTER + (f + 1) * D],
                                                        start=f == 0, stop=f == 1)
                        last.then_inc(my_ready.sem, 1)
                        made(pe, gprob_ready, m)
                        for t in range(T):
                            last = nc.tensor.transpose(bank[0][0:E0, t * P:(t + 1) * P], gprob[n][:, t, :], K("ident"))
                        last.then_inc(gpp_ready.sem, 1)
                    if e == 7:
                        made(pe, gpt_ready, m)
                        for t in range(T):
                            nc.tensor.matmul(tiled(0)[:, t, :], x1t[n][:, t * P:(t + 1) * P], K("ident"), start=True, stop=False)
                            last = nc.tensor.matmul(tiled(0)[:, t, :], gpt[0:E0, t * P:(t + 1) * P], K("downb0")[0:E0, :], start=False, stop=True)
                        last.then_inc(base_ready.sem, 1)

                def behind(m, n, e):
                    if e == 2:
                        made(pe, xn2_ready, m)
                        for t in range(T):
                            last = nc.tensor.transpose(tiled(7)[:, t, :], xn2[:, t, :], K("ident"))
                        last.then_inc(xn2p_ready.sem, 1)
                    if e == 3:
                        made(pe, xt2_ready, m)
                        for t in range(T):
                            last = nc.tensor.matmul(bank[7][:, t * E1:(t + 1) * E1], xt2[:, t * P:(t + 1) * P], K("router"), start=True, stop=True)
                        last.then_inc(route_ready.sem, 1)

                def up(m, n, e):
                    for f in range(FC):
                        u = e * FC + f
                        before = u - 3 if u >= 3 else max(k for k in range(UNITS0) if k % 3 == u) - UNITS0
                        if before >= 0 or not isinstance(m, int) or m:
                            pe.wait_ge(hid_ready.sem, hid_ready.at(m, before + 1))
                        nc.tensor.matmul(bank[4 + u % 3], K("up0", e * F0 + f * P, P), x1t[n][:, :], start=True, stop=True
                                         ).then_inc(up_ready.sem, 1)

                def down(m, n, e):
                    pe.wait_ge(hid_ready.sem, hid_ready.at(m, (e + 1) * FC))
                    if e >= 2 or not isinstance(m, int) or m:
                        pe.wait_ge(down_used.sem, down_used.at(m, e - 1))
                    for t in range(T):
                        for f in range(FC):
                            last = nc.tensor.matmul(tiled(2 + e % 2)[:, t, :], hid[:, e % 2, f, t * P:(t + 1) * P],
                                                    K("down0", (e * FC + f) * D, D), start=f == 0, stop=f == FC - 1)
                    last.then_inc(down_ready.sem, 1)

                def experts(m, n, between):
                    up(m, n, 0)
                    for e in range(E0):
                        if e + 1 < E0:
                            up(m, n, e + 1)
                        down(m, n, e)
                        between(e)

                steps(pe, ahead, experts, behind)

            @block.scalar
            def _(act):
                cols = K("cols0")

                def ahead(m, n, e):
                    if e == 1:
                        made(act, mq_ready, m)
                        made_before(act, sum_ready, m, 2)
                        nc.scalar.activation(q2[n][:, :, :], tiled(1), ACT.Tanh, scale=0.5).then_inc(mqt_ready.sem, 1)
                    if e == 3:
                        made(act, x1p_ready, m)
                        nc.scalar.activation(x1t[n][:, :], bank[0], ACT.Identity, bias=cols[:, 4:5], scale=cols[:, 3:4]).then_inc(x1t_ready.sem, 1)
                    if e == 4:
                        made(act, mqp_ready, m)
                        nc.scalar.activation(qt[:, :], bank[1], ACT.Copy).then_inc(mqtt_ready.sem, 1)
                        made(act, gsm_ready, m)
                        nc.scalar.activation(pexp[:, :, :], gsm[:, :, :], ACT.Exp).then_inc(gexp_ready.sem, 1)
                    if e == 5:
                        made(act, mz_ready, m)
                        nc.scalar.activation(ht[:, :, :], ps[:, 0:2, :], ACT.Tanh, scale=0.5).then_inc(mtanh_ready.sem, 1)
                    if e == 6:
                        made(act, my_ready, m)
                        nc.scalar.activation(yy[:, :, :], tiled(1), ACT.Copy).then_inc(my_copied.sem, 1)
                        made(act, gpp_ready, m)
                        nc.scalar.activation(gpt[0:E0, :], bank[0][0:E0, :], ACT.Copy).then_inc(gpt_ready.sem, 1)
                        made(act, my_copied, m)
                        nc.scalar.activation(sq[:, :, :], yy[:, :, :], ACT.Square).then_inc(my_squared.sem, 1)

                def behind(m, n, e):
                    if e == 2:
                        made(act, xn2p_ready, m)
                        made_before(act, xt2_stored, m)
                        nc.scalar.activation(xt2[:, :], bank[7], ACT.Copy).then_inc(xt2_ready.sem, 1)
                    if e == 4:
                        made(act, rl_ready, m)
                        nc.scalar.activation(rl[:, :, :], rl[:, :, :], ACT.Exp).then_inc(rexp_ready.sem, 1)

                def hidden(m, e):
                    if e >= 2 or not isinstance(m, int) or m:
                        act.wait_ge(down_ready.sem, down_ready.at(m, e - 1))
                    for f in range(FC):
                        u = e * FC + f
                        act.wait_ge(up_ready.sem, up_ready.at(m, u + 1))
                        nc.scalar.activation(hid[:, e % 2, f, :], bank[4 + u % 3], ACT.Relu, bias=K("upb0", u, 1)).then_inc(hid_ready.sem, 1)

                def experts(m, n, between):
                    hidden(m, 0)
                    for e in range(E0):
                        if e + 1 < E0:
                            hidden(m, e + 1)
                        between(e)

                steps(act, ahead, experts, behind)

            @block.gpsimd
            def _(pool):
                nc.gpsimd.memset(zeros[:, :], 0.0).then_inc(zero_ready.sem, 1)

            @block.vector
            def _(dve):
                per = 2 * (2 + E0 + AHEAD_STEPS + BEHIND_STEPS) - 4
                own = Own(ctx0, nc, "a_own", dve, per)

                def ahead(m, n, e):
                    if e == 2:
                        made(dve, z_ready, m)
                        last = normalise(nc, own, x1h, tiled(0), stats, mv, var[:, :], rstd[:, :], tmp[:, :], 1e-5)
                        last.then_inc(x1h_ready.sem, 1)
                    if e == 3:
                        made(dve, mqt_ready, m)
                        own.done(nc.vector.scalar_tensor_tensor(q2[n][:, :, :], q2[n][:, :, :], 1.0, tiled(1), ALU.add, ALU.mult))
                        own.done(nc.vector.tensor_tensor(x2[:, :, :], q2[n][:, :, :], q2[n][:, :, :], ALU.mult))
                        own.done(nc.vector.tensor_reduce(ss[:, :], x2[:, :, :], X, ALU.add))
                        own.done(nc.vector.tensor_scalar(ss[:, :], ss[:, :], 1.0 / D, 4e-6, ALU.mult, ALU.add))
                        rsqrt(nc, own, rstd[:, :], ss[:, :], tmp[:, :])
                        for t in range(T):
                            last = nc.vector.scalar_tensor_tensor(q2[n][:, t, :], q2[n][:, t, :], rstd[:, t:t + 1], K("qnorm"), ALU.mult, ALU.mult)
                        last.then_inc(mq2_ready.sem, 1)
                    if e == 4:
                        made(dve, gate_ready, m)
                        gl = bank[0][:, 0:T * E0].rearrange("p (t e) -> p t e", t=T)
                        own.done(nc.vector.reduce_max(gmax[:, :], gl, X))
                        nc.vector.tensor_tensor(gsm[:, :, :], gl, along(gmax[:, :], E0), ALU.subtract).then_inc(gsm_ready.sem, 1)
                    if e == 5:
                        made(dve, gexp_ready, m)
                        own.done(nc.vector.tensor_reduce(gmax[:, :], pexp[:, :, :], X, ALU.add))
                        own.done(nc.vector.reciprocal(gmax[:, :], gmax[:, :]))
                        nc.vector.tensor_tensor(gprob[n][:, :, :], pexp[:, :, :], along(gmax[:, :], E0), ALU.mult).then_inc(gprob_ready.sem, 1)
                        made(dve, mtanh_ready, m)
                        nc.vector.scalar_tensor_tensor(ht[:, :, :], ht[:, :, :], 1.0, ps[:, 0:2, :], ALU.add, ALU.mult).then_inc(mh_ready.sem, 1)
                    if e == 7:
                        made(dve, my_squared, m)
                        own.done(nc.vector.tensor_reduce(ss[:, :], sq[:, :, :], X, ALU.add))
                        own.done(nc.vector.tensor_scalar(ss[:, :], ss[:, :], 1.0 / D, 4e-6, ALU.mult, ALU.add))
                        rsqrt(nc, own, rstd[:, :], ss[:, :], tmp[:, :])
                        for t in range(T):
                            last = nc.vector.scalar_tensor_tensor(yy[:, t, :], yy[:, t, :], rstd[:, t:t + 1], mem[:, 2 * INTER:2 * INTER + D], ALU.mult, ALU.mult)
                        own.done(last)
                        own.done(nc.vector.tensor_tensor(q2[n][:, :, :], q2[n][:, :, :], yy[:, :, :], ALU.add))
                        made(dve, xin_loaded, m)
                        nc.vector.tensor_tensor(q2[n][:, :, :], q2[n][:, :, :], xin[:, :, :], ALU.add).then_inc(memory_ready.sem, 1)
                        made(dve, base_ready, m)
                        made_before(dve, sum_stored, m, 2)
                        nc.vector.tensor_copy(acc[n][:, :, :], tiled(0)).then_inc(acc_ready.sem, 1)

                def behind(m, n, e):
                    if e == 0:
                        own.done(normalise(nc, own, x2, acc[n], stats, mv, var[:, :], rstd[:, :], tmp[:, :], 1e-5))
                        own.done(nc.vector.tensor_tensor(x2[:, :, :], x2[:, :, :], over(K("ln2g"), T), ALU.mult))
                        own.done(nc.vector.tensor_tensor(x2[:, :, :], x2[:, :, :], over(K("ln2b"), T), ALU.add))
                        made(dve, memory_ready, m)
                        nc.vector.tensor_tensor(acc[n][:, :, :], x2[:, :, :], q2[n][:, :, :], ALU.add).then_inc(sum_ready.sem, 1)
                    if e == 1:
                        made(dve, sum_ready, m)
                        made_before(dve, xn2_stored, m)
                        last = normalise(nc, own, xn2, acc[n], stats, mv, var[:, :], rstd[:, :], tmp[:, :], 1e-5)
                        last.then_inc(xn2_ready.sem, 1)
                    if e == 4:
                        made(dve, route_ready, m)
                        lg = bank[7][:, 0:T * E1].rearrange("p (t e) -> p t e", t=T)
                        own.done(nc.vector.reduce_max(rmax[:, :], lg, X))
                        nc.vector.tensor_tensor(rl[:, :, :], lg, along(rmax[:, :], E1), ALU.subtract).then_inc(rl_ready.sem, 1)
                    if e == 6:
                        made(dve, rexp_ready, m)
                        made_before(dve, wts_stored, m)
                        own.hold(nc)
                        for t in range(T):
                            last = nc.vector.max(top[:, t, :], rl[:, t, :])
                        own.done(last)
                        own.hold(nc)
                        for t in range(T):
                            last = nc.vector.match_replace(left[:, t, :], top[:, t, :], rl[:, t, :], -1.0)
                        own.done(last)
                        own.done(nc.vector.tensor_scalar(left[:, :, :], left[:, :, :], 0.0, None, ALU.is_lt))
                        own.done(nc.vector.tensor_reduce(rmax[:, :], top[:, :, :], X, ALU.add))
                        own.done(nc.vector.reciprocal(rmax[:, :], rmax[:, :]))
                        own.done(nc.vector.tensor_tensor(wts[:, :, :], rl[:, :, :], left[:, :, :], ALU.mult))
                        own.hold(nc)
                        own.done(nc.vector.tensor_copy(chosen[:, bass.ds(m * (T * E1), T * E1)], left[:, :, :].rearrange("p t e -> p (t e)")))
                        nc.vector.tensor_tensor(wts[:, :, :], wts[:, :, :], along(rmax[:, :], E1), ALU.mult).then_inc(wts_ready.sem, 1)

                def experts(m, n, between):
                    made(dve, acc_ready, m)
                    for e in range(E0):
                        made_expert = down_ready.at(m, e + 1)
                        dve.wait_ge(down_ready.sem, made_expert)
                        for t in range(T):
                            last = nc.vector.scalar_tensor_tensor(acc[n][:, t, :], tiled(2 + e % 2)[:, t, :], gprob[n][:, t, e:e + 1], acc[n][:, t, :], ALU.mult, ALU.add)
                        own.done(last)
                        nc.vector.sem_inc(down_used.sem, 1)
                        between(e)

                def looped(i):
                    own.first, own.k, own.i = own.k, 0, i

                def after():
                    own.end()
                    own.k, own.i = 0, NB // 2 - 1

                steps(dve, ahead, experts, behind, looped, after)


AHEAD_STEPS = NORMALISE_STEPS + 4 + RSQRT_STEPS + 1 + 2 + 4 + RSQRT_STEPS
BEHIND_STEPS = 2 * NORMALISE_STEPS + 3 + 1 + 7


Q = 4


def routed(nc, ctx0, K, ps, bank, chosen, gate_up, down, table_d, sum_d):
    with ExitStack() as ctx:
        def sb(name, shape, dt=F32):
            return ctx.enter_context(nc.sbuf_tensor("r_" + name, shape, dt))

        def sig(name, **kw):
            return Signal(ctx0, nc, "r_" + name, **kw)

        upto = sb("upto", [P, P], BF16)
        pick = sb("pick", [P, Q, NT], BF16)
        total = sb("total", [P, Q])
        excl = sb("excl", [NT, Q])
        incl = sb("incl", [NT, Q])
        count = sb("count", [NT, Q, P], BF16)
        onehot = sb("onehot", [NT, Q, CAP], BF16)
        passed = sb("passed", [NT, Q, CAP], BF16)
        onesb = sb("onesb", [NT, 1], BF16)
        below = sb("below", [P, Q, P])
        slot = sb("slot", [P, Q])
        token = sb("token", [P, Q])
        tiles_before = sb("tiles_before", [P, Q])
        index = sb("index", [P, Q], I32)
        row = sb("row", [P, Q, D + E1])
        rt = sb("rt", [P, Q, P])
        wgu = [sb(f"wgu{u}", [P, Q, 2 * F1]) for u in range(2)]
        wdn = [sb(f"wdn{u}", [F1, Q, D]) for u in range(2)]
        th = sb("th", [P, Q, F1])
        h = sb("h", [P, Q, F1])
        ht = sb("ht", [F1, Q, P])
        share = sb("share", [P, Q, 1])
        out = sb("out", [P, Q, D])
        still = sb("still", [P, 2])

        held = sig("held", per=Q + 1, first=1)
        zeroed = sig("zeroed")
        upto_ready = sig("upto_ready")
        loaded = [sig(f"loaded{u}", per=2, unit=16) for u in range(2)]
        pick_ready = sig("pick_ready")
        local_ready = sig("local_ready")
        total_ready = sig("total_ready")
        excl_ready = sig("excl_ready")
        hot_ready = sig("hot_ready")
        sel_ready = sig("sel_ready")
        index_ready = sig("index_ready")
        gathered = sig("gathered", per=Q, unit=16)
        rt_ready = sig("rt_ready")
        rt_copied = sig("rt_copied")
        gu_ready = sig("gu_ready")
        tanh_ready = sig("tanh_ready")
        h_ready = sig("h_ready")
        ht_ready = sig("ht_ready")
        ht_copied = sig("ht_copied")
        eo_ready = sig("eo_ready", first=1)
        out_ready = sig("out_ready")
        added = sig("added", per=Q, unit=16)
        round_done = sig("round_done", first=1)

        local_ps = bank[0].rearrange("p (q s) -> p q s", q=Q)
        excl_ps = bank[1][0:NT, 0:Q]
        sel_ps = bank[2].rearrange("p (q s) -> p q s", q=Q)
        tiles_ps = bank[3][:, 0:Q]
        rt_ps = bank[4].rearrange("p (q s) -> p q s", q=Q)
        gu_ps = ps[:, 5:7, :].rearrange("p b (q s) -> p (b q) s", q=2)[:, :, 0:2 * F1]
        ht_ps = bank[7][0:F1, :].rearrange("p (q s) -> p q s", q=Q)
        eo_ps = bank[0].rearrange("p (q s) -> p q s", q=Q)
        LOOPS = E1 // Q

        with nc.Block() as block:
            @block.sync
            def _(sp):
                for u in range(2):
                    sp.dma_start(wgu[u][:, :, :], gate_up[:, u * Q:(u + 1) * Q, :]).then_inc(loaded[u].sem, 16)
                    sp.dma_start(wdn[u][:, :, :], down[:, u * Q:(u + 1) * Q, :]).then_inc(loaded[u].sem, 16)
                with sp.Fori(0, LOOPS // 2 - 1) as pair:
                    for u in range(2):
                        sp.wait_ge(eo_ready.sem, eo_ready.at(pair * 2, u + 1))
                        sp.dma_start(wgu[u][:, :, :], gate_up[:, bass.ds(pair * (2 * Q) + (2 + u) * Q, Q), :]).then_inc(loaded[u].sem, 16)
                        sp.dma_start(wdn[u][:, :, :], down[:, bass.ds(pair * (2 * Q) + (2 + u) * Q, Q), :]).then_inc(loaded[u].sem, 16)

            @block.tensor
            def _(pe):
                pe.wait_ge(upto_ready.sem, 1)
                pe.sem_inc(eo_ready.sem, 1)
                with pe.Fori(0, LOOPS // 2) as pair:
                    g = pair * 2
                    for u in range(2):
                        pe.wait_ge(pick_ready.sem, pick_ready.at(g, u + 1))
                        for q in range(Q):
                            last = nc.tensor.matmul(local_ps[0:NT, q, :], pick[:, q, :], upto[:, :], start=True, stop=True)
                        last.then_inc(local_ready.sem, 1)
                        pe.wait_ge(total_ready.sem, total_ready.at(g, u + 1))
                        nc.tensor.matmul(excl_ps, K("before"), total[:, :], start=True, stop=True).then_inc(excl_ready.sem, 1)
                        pe.wait_ge(hot_ready.sem, hot_ready.at(g, u + 1))
                        for q in range(Q):
                            nc.tensor.matmul(sel_ps[:, q, :], onehot[:, q, :], count[:, q, :], start=True, stop=True)
                        for q in range(Q):
                            last = nc.tensor.matmul(tiles_ps[:, q:q + 1], passed[:, q, :], onesb[:, :], start=True, stop=True)
                        last.then_inc(sel_ready.sem, 1)
                        pe.wait_ge(gathered.sem, gathered.at(g, (u + 1) * Q))
                        for q in range(Q):
                            last = nc.tensor.transpose(rt_ps[:, q, :], row[:, q, 0:D], K("ident"))
                        last.then_inc(rt_ready.sem, 1)
                        pe.wait_ge(rt_copied.sem, rt_copied.at(g, u + 1))
                        pe.wait_ge(loaded[u].sem, pair * 32 + 32)
                        for q in range(Q):
                            last = nc.tensor.matmul(gu_ps[:, q, :], rt[:, q, :], wgu[u][:, q, :], start=True, stop=True)
                        last.then_inc(gu_ready.sem, 1)
                        pe.wait_ge(h_ready.sem, h_ready.at(g, u + 1))
                        for q in range(Q):
                            last = nc.tensor.transpose(ht_ps[:, q, :], h[:, q, :], K("ident"))
                        last.then_inc(ht_ready.sem, 1)
                        pe.wait_ge(ht_copied.sem, ht_copied.at(g, u + 1))
                        for q in range(Q):
                            last = nc.tensor.matmul(eo_ps[:, q, :], ht[:, q, :], wdn[u][:, q, :], start=True, stop=True)
                        last.then_inc(eo_ready.sem, 1)

            @block.scalar
            def _(act):
                with act.Fori(0, LOOPS) as g:
                    act.wait_ge(rt_ready.sem, rt_ready.at(g, 1))
                    nc.scalar.activation(rt[:, :, :], rt_ps, ACT.Copy).then_inc(rt_copied.sem, 1)
                    act.wait_ge(gu_ready.sem, gu_ready.at(g, 1))
                    nc.scalar.activation(th[:, :, :], gu_ps[:, :, 0:F1], ACT.Tanh, scale=0.5).then_inc(tanh_ready.sem, 1)
                    act.wait_ge(ht_ready.sem, ht_ready.at(g, 1))
                    nc.scalar.activation(ht[:, :, :], ht_ps, ACT.Copy).then_inc(ht_copied.sem, 1)

            @block.gpsimd
            def _(pool):
                nc.gpsimd.tensor_copy(upto[:, :], K("upto"))
                nc.gpsimd.memset(still[:, :], 0.0)
                nc.gpsimd.memset(onesb[:, :], 1.0).then_inc(upto_ready.sem, 1)
                pool.wait_ge(upto_ready.sem, 1)
                pool.sem_inc(round_done.sem, 1)

                pool.sem_inc(held.sem, 1)

                def hold(g, k):
                    pool.wait_ge(held.sem, held.at(g, k))
                    nc.gpsimd.tensor_tensor(still[:, 0:1], still[:, 1:2], still[:, 1:2], ALU.add).then_inc(held.sem, 1)

                with pool.Fori(0, LOOPS) as g:
                    pool.wait_ge(index_ready.sem, index_ready.at(g, 1))
                    hold(g, 0)
                    for q in range(Q):
                        nc.gpsimd.indirect_dma_start(out=row[:, q, :], out_offset=None, in_=table_d,
                                                     in_offset=bass.IndirectOffsetOnAxis(ap=index[:, q:q + 1], axis=0)
                                                     ).then_inc(gathered.sem, 16)
                    pool.wait_ge(out_ready.sem, out_ready.at(g, 1))
                    hold(g, 1)
                    for q in range(Q):
                        if q:
                            pool.wait_ge(added.sem, added.at(g, q))
                            hold(g, q + 1)
                        nc.gpsimd.indirect_dma_start(out=sum_d, out_offset=bass.IndirectOffsetOnAxis(ap=index[:, q:q + 1], axis=0),
                                                     in_=out[:, q, :], in_offset=None, compute_op=ALU.add
                                                     ).then_inc(added.sem, 16)
                    pool.wait_ge(added.sem, added.at(g, Q))
                    pool.sem_inc(round_done.sem, 1)

            @block.vector
            def _(dve):
                own = Own(ctx0, nc, "r_own", dve, 14)
                nc.vector.memset(total[:, :], 0.0).then_inc(zeroed.sem, 1)
                dve.wait_ge(zeroed.sem, 1)
                with dve.Fori(0, LOOPS) as g:
                    own.start(g)
                    own.hold(nc)
                    nc.vector.tensor_copy(pick[:, :, :], chosen[:, :].rearrange("p (t e) -> p e t", e=E1)[:, bass.ds(g * Q, Q), :]
                                          ).then_inc(pick_ready.sem, 1)
                    dve.wait_ge(local_ready.sem, local_ready.at(g, 1))
                    nc.vector.tensor_copy(total[0:NT, :], local_ps[0:NT, :, P - 1]).then_inc(total_ready.sem, 1)
                    dve.wait_ge(excl_ready.sem, excl_ready.at(g, 1))
                    own.done(nc.vector.tensor_copy(excl[:, :], excl_ps))
                    own.done(nc.vector.tensor_tensor(incl[:, :], excl[:, :], total[0:NT, :], ALU.add))
                    for q in range(Q):
                        nc.vector.tensor_scalar(count[:, q, :], local_ps[0:NT, q, :], excl[:, q:q + 1], float(CAP + 1), ALU.add, ALU.min)
                        last = nc.vector.tensor_scalar(passed[:, q, :], K("slots")[0:NT, :], incl[:, q:q + 1], None, ALU.is_ge)
                    own.done(last)
                    for q in range(Q):
                        last = nc.vector.tensor_scalar(onehot[:, q, :], K("slots")[0:NT, :], excl[:, q:q + 1], None, ALU.is_ge)
                    own.done(last)
                    nc.vector.tensor_tensor(onehot[:, :, :], onehot[:, :, :], passed[:, :, :], ALU.subtract).then_inc(hot_ready.sem, 1)
                    dve.wait_ge(sel_ready.sem, sel_ready.at(g, 1))
                    own.done(nc.vector.tensor_scalar(tiles_before[:, :], tiles_ps, float(P), None, ALU.mult))
                    own.done(nc.vector.tensor_scalar(below[:, :, :], sel_ps, K("slot"), None, ALU.is_le))
                    own.done(nc.vector.tensor_reduce(slot[:, :], below[:, :, :], X, ALU.add))
                    own.done(nc.vector.tensor_tensor(token[:, :], tiles_before[:, :], slot[:, :], ALU.add))
                    own.done(nc.vector.tensor_scalar(token[:, :], token[:, :], K("spare"), None, ALU.min))
                    dve.wait_ge(round_done.sem, round_done.at(g, 0))
                    nc.vector.tensor_copy(index[:, :], token[:, :]).then_inc(index_ready.sem, 1)
                    dve.wait_ge(tanh_ready.sem, tanh_ready.at(g, 1))
                    own.done(nc.vector.scalar_tensor_tensor(th[:, :, :], th[:, :, :], 1.0, gu_ps[:, :, 0:F1], ALU.add, ALU.mult))
                    own.done(nc.vector.tensor_tensor(h[:, :, :], th[:, :, :], gu_ps[:, :, F1:2 * F1], ALU.mult))
                    nc.vector.sem_inc(h_ready.sem, 1)
                    own.hold(nc)
                    for q in range(Q):
                        last = nc.vector.tensor_copy(share[:, q, :], row[:, q, bass.ds(g * Q + (D + q), 1)])
                    own.done(last)
                    own.done(nc.vector.tensor_scalar(share[:, :, :], share[:, :, :], 0.5, None, ALU.mult))
                    dve.wait_ge(eo_ready.sem, eo_ready.at(g, 1))
                    for q in range(Q):
                        last = nc.vector.tensor_scalar(out[:, q, :], eo_ps[:, q, :], share[:, q, :], None, ALU.mult)
                    own.done(last)
                    nc.vector.sem_inc(out_ready.sem, 1)
                    assert own.k == own.per, own.k


def layer1(nc, ctx0, K, ps, bank, xnt2_d, sum_d, result):
    with ExitStack() as ctx:
        def sb(name, shape, dt=F32):
            return ctx.enter_context(nc.sbuf_tensor("b_" + name, shape, dt))

        def sig(name, **kw):
            return Signal(ctx0, nc, "b_" + name, **kw)

        xt = [sb(f"xt{n}", [P, S]) for n in range(2)]
        cpad = sb("cpad", [P, S + 2])
        ctxt = sb("ctxt", [P, S])
        before = sb("before", [P, T, D])
        res = sb("res", [P, T, D])
        both, queries = 1 + 2 * PARTS, 1 + PARTS
        starts = (7, 8, 8, 7)
        att = TurnAttention(ctx, ctx0, nc, K, ps, bank, "b", True, 4,
                             [spread(n) for n in starts], [both, queries, queries, both])
        misc = 4 * (2 * G + 1)
        att.misc_free = sig("misc_free", per=misc, first=G + 1)
        LOOPS = NB // 2

        copied = sig("copied", unit=16)
        x_loaded = [sig(f"x_loaded{n}", first=1, unit=16) for n in range(2)]
        before_loaded = sig("before_loaded", per=2, unit=16)
        edges_ready = sig("edges_ready")
        proj_ready = sig("proj_ready", per=2, first=1)
        vp_ready = sig("vp_ready", per=2 * T, first=T)
        v_ready = sig("v_ready", per=2 * T, first=T)
        cpad_ready = sig("cpad_ready", per=2)
        conv_ready = sig("conv_ready", per=2)
        ctxt_copied = sig("ctxt_copied", per=2)
        out_ready = sig("out_ready", per=2, first=1)
        res_ready = sig("res_ready", per=2, first=1)
        res_stored = sig("res_stored", per=2, first=1, unit=16)

        def tiled(ap):
            return ap.rearrange("p (t d) -> p t d", t=T)

        def load_x(sp, item, n):
            sp.dma_start(xt[n][:, :], xnt2_d[bass.ds(item * P, P), :]).then_inc(x_loaded[n].sem, 16)

        with nc.Block() as block:
            @block.sync
            def _(sp):
                sp.dma_start(xnt2_d[NB * P:(NB + 2) * P, :], xnt2_d[0:2 * P, :]).then_inc(copied.sem, 16)
                for n in range(2):
                    load_x(sp, n, n)
                att.setup_sync(sp)
                sp.sem_inc(res_stored.sem, 16)
                sp.wait_ge(copied.sem, 16)
                att.load_rows(sp, -1, 3, 2)
                att.load_shifts(sp, -1, 3)
                with sp.Fori(0, LOOPS) as i:
                    att.load_rows(sp, i, 0, 2)
                    att.load_shifts(sp, i, 0)
                    att.load_rows(sp, i, 1, 1)
                    sp.wait_ge(vp_ready.sem, vp_ready.at(i, 0))
                    load_x(sp, i * 2 + 2, 0)
                    att.load_shifts(sp, i, 1)
                    att.load_rows(sp, i, 2, 1)
                    sp.wait_ge(vp_ready.sem, vp_ready.at(i, T))
                    load_x(sp, i * 2 + 3, 1)
                    sp.wait_ge(res_ready.sem, res_ready.at(i, 0))
                    sp.dma_start(before[:, :, :], sum_d[bass.ds(i * (2 * S), S), :].rearrange("(t p) d -> p t d", p=P)
                                 ).then_inc(before_loaded.sem, 16)
                    att.load_shifts(sp, i, 2)
                    att.load_rows(sp, i, 3, 2)
                    att.load_shifts(sp, i, 3)
                    sp.wait_ge(res_ready.sem, res_ready.at(i, 1))
                    sp.dma_start(result[bass.ds(i * 2, 1), :, :].rearrange("o (t p) d -> p (o t) d", p=P), res[:, :, :]
                                 ).then_inc(res_stored.sem, 16)
                    sp.dma_start(before[:, :, :], sum_d[bass.ds(i * (2 * S) + S, S), :].rearrange("(t p) d -> p t d", p=P)
                                 ).then_inc(before_loaded.sem, 16)
                    sp.wait_ge(res_ready.sem, res_ready.at(i, 2))
                    sp.dma_start(result[bass.ds(i * 2 + 1, 1), :, :].rearrange("o (t p) d -> p (o t) d", p=P), res[:, :, :]
                                 ).then_inc(res_stored.sem, 16)
                sp.wait_ge(res_stored.sem, res_stored.at(LOOPS, 0))

            @block.gpsimd
            def _(pool):
                nc.gpsimd.memset(cpad[:, 0:1], 0.0)
                nc.gpsimd.memset(cpad[:, S + 1:S + 2], 0.0).then_inc(edges_ready.sem, 1)
                att.setup_pool(pool)

            @block.tensor
            def _(pe):
                def project(i, n, k):
                    pe.wait_ge(x_loaded[n].sem, x_loaded[n].at(i + k, 0))
                    nc.tensor.matmul(bank[2], K("q1"), xt[n][:, :], start=True, stop=True)
                    nc.tensor.matmul(bank[5], K("k1"), xt[n][:, :], start=True, stop=True).then_inc(proj_ready.sem, 1)

                def values(i, n, k, t):
                    if t < 2:
                        pe.wait_ge(att.qk_ready.sem, k)
                    else:
                        pe.wait_ge(v_ready.sem, v_ready.at(i, (0 if n else T) + t - 1))
                    nc.tensor.matmul(bank[2 if t % 2 == 0 else 5], xt[n][:, t * P:(t + 1) * P], K("v1"), start=True, stop=True
                                     ).then_inc(vp_ready.sem, 1)

                def convolve(i, k):
                    pe.wait_ge(cpad_ready.sem, cpad_ready.at(i, k + 1))
                    att.maxima_done(pe, i, k + 1)
                    for tap in range(3):
                        last = nc.tensor.matmul(bank[2], K("conv1", tap * D, D), cpad[:, tap:tap + S], start=tap == 0, stop=tap == 2)
                    last.then_inc(conv_ready.sem, 1)

                def output(i, k):
                    pe.wait_ge(ctxt_copied.sem, ctxt_copied.at(i, k + 1))
                    for t in range(T):
                        nc.tensor.matmul(tiled(bank[3])[:, t, :], ctxt[:, t * P:(t + 1) * P], K("out1"), start=True, stop=False)
                        last = nc.tensor.matmul(tiled(bank[3])[:, t, :], K("ones")[0:1, :], K("outb1")[0:1, :], start=False, stop=True)
                    last.then_inc(out_ready.sem, 1)

                att.setup_tensor(pe)
                pe.sem_inc(out_ready.sem, 1)
                pe.wait_ge(edges_ready.sem, 1)
                att.misc_used = misc - G
                pe.wait_ge(x_loaded[0].sem, 16)
                nc.tensor.matmul(bank[2], K("q1"), xt[0][:, :], start=True, stop=True)
                nc.tensor.matmul(bank[5], K("k1"), xt[0][:, :], start=True, stop=True).then_inc(proj_ready.sem, 1)
                for t in range(T):
                    if t == 0:
                        pe.wait_ge(att.qk_ready.sem, 1)
                    if t >= 2:
                        pe.wait_ge(v_ready.sem, t - 1)
                    nc.tensor.matmul(bank[2 if t % 2 == 0 else 5], xt[0][:, t * P:(t + 1) * P], K("v1"), start=True, stop=True
                                     ).then_inc(vp_ready.sem, 1)
                pe.wait_ge(v_ready.sem, T)
                att.tensor_early(pe)
                with pe.Fori(0, LOOPS) as i:
                    att.misc_used = 0

                    def odd_start(s):
                        if s == 0:
                            pe.wait_ge(res_ready.sem, res_ready.at(i, 0))
                            att.maxima_done(pe, i, 0)
                            project(i, 1, 0)
                        if s in (3, 4, 5, 6):
                            values(i, 1, att.qk_ready.at(i, 1), s - 3)
                        if s == 6:
                            pe.wait_ge(v_ready.sem, v_ready.at(i, T))

                    def even_queries(s):
                        if s == 2:
                            att.tensor_whole_context(pe, i, 0)
                        if s == 3:
                            convolve(i, 0)

                    def odd_queries(s):
                        if s == 2:
                            att.tensor_whole_context(pe, i, 1)
                        if s == 3:
                            convolve(i, 1)

                    def next_start(s):
                        if s == 0:
                            att.maxima_done(pe, i, 3)
                            project(i, 0, 1)
                        if s == 2:
                            att.tensor_whole_context(pe, i, 2)
                        if s in (3, 4, 5, 6):
                            values(i, 0, att.qk_ready.at(i, 4), s - 3)
                        if s == 3:
                            output(i, 0)
                        if s == 6:
                            pe.wait_ge(v_ready.sem, v_ready.at(i, 2 * T))
                            pe.wait_ge(res_ready.sem, res_ready.at(i, 1))

                    att.tensor_turn(pe, i, 0, odd_start)
                    att.tensor_turn(pe, i, 1, even_queries)
                    att.tensor_turn(pe, i, 2, odd_queries)
                    att.tensor_turn(pe, i, 3, next_start)
                    att.tensor_tail(pe, i, 3)
                    att.tensor_whole_context(pe, i, 3)
                    att.maxima_done(pe, i, 4)
                    output(i, 1)
                    assert att.misc_used == misc

            @block.scalar
            def _(act):
                cols = K("cols1")

                def queries_keys(i, a, k):
                    act.wait_ge(proj_ready.sem, proj_ready.at(i, k))
                    att.before_qk(act, i, a)
                    nc.scalar.activation(att.qk[:, 0, :], bank[2], ACT.Identity, bias=cols[:, 0:1])
                    nc.scalar.activation(att.qk[:, 1, :], bank[5], ACT.Identity, bias=cols[:, 1:2]).then_inc(att.qk_ready.sem, 1)
                    att.split_hi(act, i, a, 2)

                def second_queries(i, a, k):
                    act.wait_ge(conv_ready.sem, conv_ready.at(i, k))
                    att.before_qk(act, i, a)
                    nc.scalar.activation(att.qk[:, 0, :], bank[2], ACT.Identity, bias=cols[:, 2:3]).then_inc(att.qk_ready.sem, 1)
                    att.split_hi(act, i, a, 1)

                def whole_context(i, a, out, signal, k):
                    act.wait_ge(att.ctxt_ready.sem, att.ctxt_ready.at(i, a + 1))
                    nc.scalar.activation(out, bank[7], ACT.Copy).then_inc(signal.sem, 1)
                    act.wait_ge(signal.sem, signal.at(i, k))
                    act.sem_inc(att.misc_free.sem, 1)

                att.setup_scalar(act)
                queries_keys(-1, 3, 2)
                att.split_mid(act, -1, 3, 2)
                with act.Fori(0, LOOPS) as i:
                    def first_start(s, a, k):
                        if s == 0:
                            queries_keys(i, a, k)
                        if s == 1:
                            att.split_mid(act, i, a, 2)

                    def second(s, a, k):
                        if s == 2:
                            whole_context(i, a - 1, cpad[:, 1:S + 1], cpad_ready, k)
                        if s == 3:
                            second_queries(i, a, k)
                        if s == 4:
                            att.split_mid(act, i, a, 1)

                    def last(s):
                        first_start(s, 3, 2)
                        if s == 2:
                            act.wait_ge(out_ready.sem, out_ready.at(i, 0))
                            whole_context(i, 2, ctxt[:, :], ctxt_copied, 1)

                    att.scalar_turn(act, i, 0, lambda s: first_start(s, 0, 1))
                    att.scalar_turn(act, i, 1, lambda s: second(s, 1, 1))
                    att.scalar_turn(act, i, 2, lambda s: second(s, 2, 2))
                    att.scalar_turn(act, i, 3, last)
                    att.scalar_context(act, i, 3, G - 1)
                    act.wait_ge(out_ready.sem, out_ready.at(i, 1))
                    whole_context(i, 3, ctxt[:, :], ctxt_copied, 2)

            @block.vector
            def _(dve):
                def values(i, n, k, t):
                    dve.wait_ge(vp_ready.sem, vp_ready.at(i, k + t + 1))
                    nc.vector.tensor_tensor(att.v[n][:, t, :], bank[2 if t % 2 == 0 else 5], K("vbias1"), ALU.add
                                            ).then_inc(v_ready.sem, 1)

                def finish(i, k):
                    dve.wait_ge(before_loaded.sem, before_loaded.at(i, k + 1))
                    dve.wait_ge(res_stored.sem, res_stored.at(i, k))
                    dve.wait_ge(out_ready.sem, out_ready.at(i, k + 1))
                    nc.vector.tensor_tensor(res[:, :, :], tiled(bank[3]), before[:, :, :], ALU.add).then_inc(res_ready.sem, 1)

                att.setup_vector(dve)
                dve.sem_inc(res_ready.sem, 1)
                per = 4 * G * (SHIFT_STEPS + CONTEXT_STEPS)
                own = Own(ctx0, nc, "b_own", dve, per, first=G * SHIFT_STEPS)
                own.start(-1, per - G * SHIFT_STEPS)
                att.split_rest(dve, -1, 3, 2)
                att.split_lo(dve, -1, 3, 2)
                for t in range(T):
                    values(-1, 0, T, t)
                att.vector_early(dve, own)
                with dve.Fori(0, LOOPS) as i:
                    own.start(i)

                    def first_start(s, a, n, k):
                        if s == 0:
                            att.split_rest(dve, i, a, 2)
                        if s == 1:
                            att.split_lo(dve, i, a, 2)
                        if s in (3, 4, 5, 6):
                            values(i, n, k, s - 3)

                    def second(s, a):
                        if s == 3:
                            att.split_rest(dve, i, a, 1)
                        if s == 4:
                            att.split_lo(dve, i, a, 1)

                    def last(s):
                        first_start(s, 3, 0, T)
                        if s == 3:
                            finish(i, 0)

                    att.vector_turn(dve, i, 0, own, lambda s: first_start(s, 0, 1, 0))
                    att.vector_turn(dve, i, 1, own, lambda s: second(s, 1))
                    att.vector_turn(dve, i, 2, own, lambda s: second(s, 2))
                    att.vector_turn(dve, i, 3, own, last)
                    att.vector_context(dve, i, 3, G - 1, own)
                    finish(i, 1)
                    own.end()


def fused(nc, x, shared, memory, layer0_in, layer1_in, gate_up, down, result):
    given = {"shared": shared, "memory": memory, "layer0": layer0_in, "layer1": layer1_in}
    with ExitStack() as ctx:
        consts = {}
        loaded = ctx.enter_context(nc.semaphore("consts_loaded"))
        loaded0 = ctx.enter_context(nc.semaphore("consts0_loaded"))

        def hold(stack, part):
            consts[part] = stack.enter_context(nc.sbuf_tensor("consts_" + part, [P, WIDTH[part]], F32))

        def K(name, offset=0, width=None):
            part, start, w = PLACE[name]
            return consts[part][:, start + offset:start + offset + (w if width is None else width)]

        hold(ctx, "shared")
        mem = ctx.enter_context(nc.sbuf_tensor("mem", [P, 2 * INTER + D], F32))
        chosen = ctx.enter_context(nc.sbuf_tensor("chosen", [P, NT * E1], BF16))
        spare = ctx.enter_context(nc.sbuf_tensor("spare_column", [P, 1], F32))
        Own.column = spare[:, :]
        psum = ctx.enter_context(nc.psum_tensor("psum", [P, 8, 512], F32))
        ps = psum[:, :, :]
        bank = [psum[:, i, :] for i in range(8)]

        xnt_d = nc.dram_tensor("xnt", [(NB + 2) * P, S], F32, kind="Internal").ap()
        xc_d = nc.dram_tensor("xc", [(NB + 2) * P, S], F32, kind="Internal").ap()
        ctxt_d = nc.dram_tensor("ctxt", [NB * P, S], F32, kind="Internal").ap()
        kn_d = nc.dram_tensor("kn", [NC, NB * CHUNK, D], F32, kind="Internal").ap()
        vn_d = nc.dram_tensor("vn", [NC, NB * CHUNK, D], F32, kind="Internal").ap()
        xnt2_d = nc.dram_tensor("xnt2", [(NB + 2) * P, S], F32, kind="Internal").ap()
        table_d = nc.dram_tensor("table", [ROWS, D + E1], F32, kind="Internal").ap()
        sum_d = nc.dram_tensor("sum", [ROWS, D], F32, kind="Internal").ap()

        with ExitStack() as first:
            hold(first, "layer0")
            with ExitStack() as start:
                hold(start, "memory")
                memw1 = start.enter_context(nc.sbuf_tensor("memw1", [P, INTER], F32))
                R = start.enter_context(nc.sbuf_tensor("gate_parts", [P, 3 * NT], F32))
                with nc.Block() as block:
                    @block.sync
                    def _(sp):
                        for part in ("shared", "memory"):
                            sp.dma_start(consts[part][:, :], given[part]).then_inc(loaded, 16)
                        sp.dma_start(consts["layer0"][:, :], given["layer0"]).then_inc(loaded0, 16)
                        sp.wait_ge(loaded, 32)
                with Semaphores() as sems:
                    project(nc, sems, K, bank, x, xnt_d, kn_d, vn_d, R)
                    sems.clear(nc)
                with Semaphores() as sems:
                    learn(nc, sems, K, ps, bank, kn_d, vn_d, R, mem, memw1)
                    sems.clear(nc)
            with nc.Block() as block:
                @block.sync
                def _(sp):
                    sp.wait_ge(loaded0, 16)
            with Semaphores() as sems:
                attend0(nc, sems, K, ps, bank, xnt_d, xc_d, ctxt_d)
                sems.clear(nc)
            with Semaphores() as sems:
                mixture(nc, sems, K, ps, bank, x, xnt_d, xc_d, ctxt_d, mem, chosen, xnt2_d, table_d, sum_d)
                sems.clear(nc)
        with ExitStack() as second:
            hold(second, "layer1")
            with nc.Block() as block:
                @block.sync
                def _(sp):
                    sp.dma_start(consts["layer1"][:, :], given["layer1"]).then_inc(loaded, 16)
                    sp.wait_ge(loaded, 48)
            with Semaphores() as sems:
                routed(nc, sems, K, ps, bank, chosen, gate_up, down, table_d, sum_d)
                sems.clear(nc)
            with Semaphores() as sems:
                layer1(nc, sems, K, ps, bank, xnt2_d, sum_d, result)


def pack(inputs):
    import numpy as np

    a = {k: np.asarray(v) for k, v in inputs.items()}
    out = {part: np.zeros((P, width), np.float32) for part, width in WIDTH.items()}

    def put(name, m, offset=0):
        part, start, _ = PLACE[name]
        out[part][:m.shape[0], start + offset:start + offset + m.shape[1]] = m

    def rows(v):
        return np.broadcast_to(v.reshape(1, -1), (P, v.size))

    p = np.arange(P)
    put("ident", np.eye(P, dtype=np.float32))
    put("ones", np.ones((P, P), np.float32))
    for w, name in enumerate(("alpha", "theta", "eta")):
        put("gates", np.concatenate([a[f"L0_attn_{name}_w"].reshape(CHUNK, D)] * 2), w * D)
    for h in range(2):
        put("half", np.broadcast_to(((p // CHUNK) == h).astype(np.float32)[:, None], (P, P)), h * D)
    put("wk", a["L0_attn_wk_w"].T)
    put("wv", a["L0_attn_wv_w"].T)
    put("wq", a["L0_attn_wq_w"].T)
    put("knorm", rows(a["L0_attn_k_norm_w"]))
    put("qnorm", rows(a["L0_attn_q_norm_w"]))
    w1 = a["L0_attn_mem_w1"]
    put("mem", a["L0_attn_mem_w0"].T)
    put("mem", w1.T[0:P], INTER)
    put("mem", w1.T[P:2 * P], INTER + D)
    put("mem", rows(a["L0_attn_mem_ln_w"]), 2 * INTER)
    put("memw1", w1)

    order = np.arange(D).reshape(H, DH).T.reshape(-1)
    for layer, wqkv, bqkv in ((0, a["L0_ffn_wqkv"], a["L0_ffn_bqkv"]), (1, a["L1_attn_Wqkv_w"], a["L1_attn_Wqkv_b"])):
        put(f"q{layer}", wqkv[0:D][order].T)
        put(f"k{layer}", wqkv[D:2 * D][order].T)
        wv = np.zeros((D, H, 32), np.float32)
        bv = np.zeros((H, 32), np.float32)
        wv[:, :, 0:DH] = wqkv[2 * D:].T.reshape(D, H, DH)
        bv[:, 0:DH] = bqkv[2 * D:].reshape(H, DH)
        bv[:, DH] = 1.0
        put(f"v{layer}", wv.reshape(D, -1))
        put(f"vbias{layer}", rows(bv))
    b0, b1 = a["L0_ffn_bqkv"], a["L1_attn_Wqkv_b"]
    conv = a["L0_ffn_conv_w"]
    for tap in range(3):
        put("conv0", conv[:, :, tap].T, tap * D)
        put("conv1", a["L1_attn_conv_w"][order, :, tap].T, tap * D)
    put("cols0", np.stack([a["L0_ffn_conv_b"], b0[0:D][order], b0[D:2 * D][order], a["L0_ffn_ln1_g"], a["L0_ffn_ln1_b"]], 1))
    put("cols1", np.stack([b1[0:D][order], b1[D:2 * D][order], a["L1_attn_conv_b"][order]], 1))
    put("out0", a["L0_ffn_wo"].T)
    put("outb0", a["L0_ffn_bo"].reshape(1, -1))
    put("gate0", a["L0_ffn_gate_w"])
    put("gateb0", a["L0_ffn_gate_b"].reshape(1, -1))
    put("up0", a["L0_ffn_w1"].transpose(1, 0, 2).reshape(D, -1))
    put("upb0", a["L0_ffn_b1"].reshape(E0 * FC, P).T)
    put("down0", a["L0_ffn_w2"].reshape(E0 * FC, P, D).transpose(1, 0, 2).reshape(P, -1))
    put("downb0", a["L0_ffn_b2"])
    put("ln2g", rows(a["L0_ffn_ln2_g"]))
    put("ln2b", rows(a["L0_ffn_ln2_b"]))
    put("out1", a["L1_attn_out_w"].T)
    put("outb1", a["L1_attn_out_b"].reshape(1, -1))
    put("router", a["L1_ffn_gate_weight"].T)
    put("maskq", np.where(p[None, :] > p[:, None], np.float32(NEG), np.float32(0)))
    put("maskk", np.where(p[:, None] > p[None, :], np.float32(NEG), np.float32(0)))
    put("upto", (p[:, None] <= p[None, :]).astype(np.float32))
    q = np.arange(NT)
    put("before", (q[:, None] < q[None, :]).astype(np.float32))
    put("slots", rows(np.arange(CAP, dtype=np.float32)))
    put("slot", p.astype(np.float32)[:, None])
    put("spare", (N + p).astype(np.float32)[:, None])
    return out


def kernel(**inputs):
    import numpy as np
    import concourse.bacc as bacc
    from concourse.bass_utils import run_bass_kernel_spmd

    nc = bacc.Bacc("TRN2", target_bir_lowering=False, num_devices=1)
    arrays = {
        "x": np.ascontiguousarray(inputs["L0_attn_x"]),
        **{f"{part}_in": a for part, a in pack(inputs).items()},
        "gate_up": np.ascontiguousarray(np.asarray(inputs["L1_ffn_gate_up_proj"]).transpose(2, 0, 1)),
        "down": np.ascontiguousarray(np.asarray(inputs["L1_ffn_down_proj"]).transpose(2, 0, 1)),
    }
    args = [nc.dram_tensor(n, a.shape, mybir.dt.from_np(a.dtype), kind="ExternalInput").ap() for n, a in arrays.items()]
    result = nc.dram_tensor("result", (NB, S, D), F32, kind="ExternalOutput").ap()
    fused(nc, *args, result)
    r = run_bass_kernel_spmd(nc, [arrays], core_ids=[0])
    return r.results[0]["result"]
```
